# Optimizing a Trainium2 kernel written in Bass

```python
import numpy as np
import jax
import jax.numpy as jnp

def _softmax(x, axis=-1):
    return jax.nn.softmax(x, axis=axis)

def _gelu(x):
    return jax.nn.gelu(x, approximate=True)

def _silu(x):
    return jax.nn.silu(x)

def _sigmoid(x):
    return jax.nn.sigmoid(x)

def _layernorm(x, axis=-1, eps=1e-05):
    m = jnp.mean(x, axis=axis, keepdims=True)
    v = jnp.var(x, axis=axis, keepdims=True)
    return (x - m) / jnp.sqrt(v + eps)

def _scatter_add(tgt, idx, src, axis=0):
    return tgt.at[idx].add(src)

def _segment_sum(src, seg, n):
    return jax.ops.segment_sum(src, seg, n)
kernel_name = 'mk_seq_preln_d1_jaxref_r4_a006e2'

def setup_inputs(seed: int=0):
    np.random.seed(seed)
    _w = jnp.asarray

    def _L0_attn_setup():
        import jax, jax.numpy as jnp
        import numpy as np
        H = 16

        def _pairwise_l2(pos):
            sq = jnp.sum((pos[:, :, None, :] - pos[:, None, :, :]) ** 2, axis=-1)
            safe = jnp.where(sq > 0, sq, 1.0)
            return jnp.where(sq > 0, jnp.sqrt(safe), 0.0)
        key = jax.random.key(seed)
        ks = jax.random.split(key, 12)
        B, S, D = (2, 512, 256)
        init = lambda k, shape: jax.random.normal(k, shape, dtype=jnp.float32) * 0.02
        return {'x': jax.random.normal(ks[0], (B, S, D), dtype=jnp.float32), 'wq': init(ks[1], (D, D)), 'bq': init(ks[2], (D,)), 'wk': init(ks[3], (D, D)), 'bk': init(ks[4], (D,)), 'wv': init(ks[5], (D, D)), 'bv': init(ks[6], (D,)), 'wo': init(ks[7], (D, D)), 'bo': init(ks[8], (D,)), 'w3d': init(ks[9], (3, D)), 'b3d': init(ks[10], (3,))}
    _L0_attn_in = _L0_attn_setup()

    def _L0_ffn_setup():
        import jax, jax.numpy as jnp
        import numpy as np
        DIM = 256
        INTER = 256
        N_EXPERTS = 8
        TOPK = 2
        N_SHARED = 2
        key = jax.random.key(seed)
        ks = jax.random.split(key, 10)
        s = 0.02
        return {'x': jax.random.normal(ks[0], (4, 512, DIM), dtype=jnp.float32), 'gate_w': jax.random.normal(ks[1], (N_EXPERTS, DIM), dtype=jnp.float32) * s, 'gate_bias': jax.random.normal(ks[2], (N_EXPERTS,), dtype=jnp.float32) * s, 'w1': jax.random.normal(ks[3], (N_EXPERTS, INTER, DIM), dtype=jnp.float32) * s, 'w3': jax.random.normal(ks[4], (N_EXPERTS, INTER, DIM), dtype=jnp.float32) * s, 'w2': jax.random.normal(ks[5], (N_EXPERTS, DIM, INTER), dtype=jnp.float32) * s, 'sw1': jax.random.normal(ks[6], (N_SHARED * INTER, DIM), dtype=jnp.float32) * s, 'sw3': jax.random.normal(ks[7], (N_SHARED * INTER, DIM), dtype=jnp.float32) * s, 'sw2': jax.random.normal(ks[8], (DIM, N_SHARED * INTER), dtype=jnp.float32) * s}
    _L0_ffn_in = _L0_ffn_setup()
    _d = {'L0_attn_x': _L0_attn_in['x'], 'L0_attn_wq': _L0_attn_in['wq'], 'L0_attn_bq': _L0_attn_in['bq'], 'L0_attn_wk': _L0_attn_in['wk'], 'L0_attn_bk': _L0_attn_in['bk'], 'L0_attn_wv': _L0_attn_in['wv'], 'L0_attn_bv': _L0_attn_in['bv'], 'L0_attn_wo': _L0_attn_in['wo'], 'L0_attn_bo': _L0_attn_in['bo'], 'L0_attn_w3d': _L0_attn_in['w3d'], 'L0_attn_b3d': _L0_attn_in['b3d'], 'L0_ffn_gate_w': _L0_ffn_in['gate_w'], 'L0_ffn_gate_bias': _L0_ffn_in['gate_bias'], 'L0_ffn_w1': _L0_ffn_in['w1'], 'L0_ffn_w3': _L0_ffn_in['w3'], 'L0_ffn_w2': _L0_ffn_in['w2'], 'L0_ffn_sw1': _L0_ffn_in['sw1'], 'L0_ffn_sw3': _L0_ffn_in['sw3'], 'L0_ffn_sw2': _L0_ffn_in['sw2']}
    _x0 = _d['L0_attn_x']
    _d['L0_attn_x'] = jax.random.normal(jax.random.fold_in(jax.random.key(seed), 1), (2, 2048, 256), dtype=_x0.dtype)
    del _x0
    return _d

def reference(L0_attn_x, L0_attn_wq, L0_attn_bq, L0_attn_wk, L0_attn_bk, L0_attn_wv, L0_attn_bv, L0_attn_wo, L0_attn_bo, L0_attn_w3d, L0_attn_b3d, L0_ffn_gate_w, L0_ffn_gate_bias, L0_ffn_w1, L0_ffn_w3, L0_ffn_w2, L0_ffn_sw1, L0_ffn_sw3, L0_ffn_sw2):

    def _L0_attn_ref(x, wq, bq, wk, bk, wv, bv, wo, bo, w3d, b3d):
        import jax, jax.numpy as jnp
        import numpy as np
        H = 16

        def _pairwise_l2(pos):
            sq = jnp.sum((pos[:, :, None, :] - pos[:, None, :, :]) ** 2, axis=-1)
            safe = jnp.where(sq > 0, sq, 1.0)
            return jnp.where(sq > 0, jnp.sqrt(safe), 0.0)
        B, S, D = x.shape
        hd = D // H
        scale = 1.0 / hd ** 0.5
        V = (x @ wv.T + bv).reshape(B, S, H, hd).transpose(0, 2, 1, 3)
        pos = x @ w3d.T + b3d
        dist = _pairwise_l2(pos)
        scores = -dist[:, None, :, :] * scale
        causal = jnp.triu(jnp.ones((S, S), dtype=bool), k=1)
        scores = jnp.where(causal[None, None], -jnp.inf, scores)
        attn = jax.nn.softmax(scores, axis=-1)
        attn = jnp.nan_to_num(attn, nan=0.0)
        out = jnp.einsum('bhqk,bhkd->bhqd', attn, V)
        out = out.transpose(0, 2, 1, 3).reshape(B, S, D)
        return out @ wo.T + bo

    def _L0_ffn_ref(x, gate_w, gate_bias, w1, w3, w2, sw1, sw3, sw2):
        import jax, jax.numpy as jnp
        import numpy as np
        DIM = 256
        INTER = 256
        N_EXPERTS = 8
        TOPK = 2
        N_SHARED = 2
        shape = x.shape
        xt = x.reshape(-1, shape[-1])
        scores = jax.nn.softmax((xt @ gate_w.T).astype(jnp.float32), axis=-1)
        _, idx = jax.lax.top_k(scores + gate_bias, TOPK)
        weights = jnp.take_along_axis(scores, idx, axis=1).astype(x.dtype)
        y = jnp.zeros_like(xt)
        for e in range(N_EXPERTS):
            gate_e = jnp.sum(jnp.where(idx == e, weights, 0.0), axis=1)
            h = jax.nn.silu(xt @ w1[e].T) * (xt @ w3[e].T)
            y = y + gate_e[:, None] * (h @ w2[e].T)
        z = jax.nn.silu(xt @ sw1.T) * (xt @ sw3.T) @ sw2.T
        return (y + z).reshape(shape)
    x = L0_attn_x
    x = x + _L0_attn_ref(_layernorm(x, axis=-1), L0_attn_wq, L0_attn_bq, L0_attn_wk, L0_attn_bk, L0_attn_wv, L0_attn_bv, L0_attn_wo, L0_attn_bo, L0_attn_w3d, L0_attn_b3d)
    x = x + _L0_ffn_ref(_layernorm(x, axis=-1), L0_ffn_gate_w, L0_ffn_gate_bias, L0_ffn_w1, L0_ffn_w3, L0_ffn_w2, L0_ffn_sw1, L0_ffn_sw3, L0_ffn_sw2)
    return x

_drawn_inputs = setup_inputs


def setup_inputs(seed=0):
    import zlib

    import numpy as np

    out = dict(_drawn_inputs(seed))
    spreads = {}
    factors = {'L0_attn_wv': 8.0,
     'L0_attn_bv': 8.0,
     'L0_attn_wo': 6.23,
     'L0_attn_bo': 2.947,
     'L0_attn_w3d': 8.0,
     'L0_attn_b3d': 64.0,
     'L0_ffn_gate_w': 8.0,
     'L0_ffn_gate_bias': 8.0,
     'L0_ffn_w1': 8.0,
     'L0_ffn_w3': 8.0,
     'L0_ffn_w2': 8.0,
     'L0_ffn_sw1': 8.0,
     'L0_ffn_sw3': 8.0,
     'L0_ffn_sw2': 8.0}
    for name, (base, spread) in spreads.items():
        noise = np.random.default_rng([zlib.crc32(name.encode()), seed]).standard_normal(out[name].shape)
        drawn = base * np.exp(spread * noise) if base else spread * noise
        out[name] = jnp.asarray(drawn.astype(out[name].dtype))
    for name, factor in factors.items():
        out[name] = (out[name] * factor).astype(out[name].dtype)
    return out
```

```python
import concourse.bass as bass
from concourse import mybir
from contextlib import ExitStack

P = 128
NB, S, D = 2, 2048, 256
NT = NB * S // P
TB = S // P
GT = 4
GB = TB // GT
KC = D // P
MW = D + 4
VW = 2 * D + 2
TRI = sum(S - P * k for k in range(TB))
NE = 4
NG = NT // GT
NX, TOPK = 8, 2
NS = 512
MC = NS // P
NSLOT = NT * TOPK + NX
N_CHOSEN = 18
H = 16
SCALE = 1.0 / (D // H) ** 0.5
EPS = 1e-5
f32 = mybir.dt.float32
f32r = mybir.dt.float32r
bf16 = mybir.dt.bfloat16
i32 = mybir.dt.int32
u32 = mybir.dt.uint32
ALU = mybir.AluOpType
ACT = mybir.ActivationFunctionType
AX = mybir.AxisListType


def flat(ap):
    return ap.rearrange("p a n -> p (a n)")


def tile_of(T, i):
    return flat(T[:, bass.ds(i, 1), :])


def unit(G, k):
    per_group, at = ((4, [1, 1, 2, 2, 3, 3, 4]), (3, [1, 1, 2, 2, 3, 3, 4]))[(k if k < GT else k - GT) % 2]
    return per_group * G + at[k]



def attention_and_experts(nc, x, wv, bv, woT, bo, w3dT, b3d, gateT, gate_bias, wT, sw13T, sw2T, out):
    x_v = x.rearrange("b (t p) d -> p (b t) d", p=P)
    out_v = out.rearrange("b (t p) d -> p (b t) d", p=P)
    vo_v = nc.dram_tensor("vo_scratch", (P, NG, GT * VW), f32, kind="Internal").ap()
    xn_v = nc.dram_tensor("xn_scratch", (P, NT, D), f32, kind="Internal").ap()
    xs = nc.dram_tensor("slots_in", (NSLOT * P, D), f32, kind="Internal").ap()
    ys = nc.dram_tensor("slots_out", (NSLOT * P, D), f32, kind="Internal").ap()
    xs_p = xs.rearrange("(p i) d -> p i d", p=P)
    xs_t = xs.rearrange("(i p) d -> i p d", p=P)
    ys_t = ys.rearrange("(i p) d -> i p d", p=P)
    outer = ExitStack()
    X = outer.enter_context(nc.sbuf_tensor("X", [P, NT, D], f32))

    with ExitStack() as ctx:
        def sb(name, shape, dt=f32):
            return ctx.enter_context(nc.sbuf_tensor(name, shape, dt))

        def pb(name):
            return ctx.enter_context(nc.psum_tensor(name, [P, 512], f32))

        def sem(name):
            return ctx.enter_context(nc.semaphore(name))

        wv_raw = sb("wv_raw", [P, KC, D])
        woT_raw = sb("woT_raw", [P, KC, D])
        M_raw = sb("M_raw", [P, KC, MW])
        M_hi = sb("M_hi", [P, KC, MW], f32r)
        M_lo = sb("M_lo", [P, KC, MW], f32r)
        bv_col = sb("bv_col", [P, KC])
        c_raw = sb("c_raw", [1, MW])
        c_hi = sb("c_hi", [1, MW], f32r)
        c_lo = sb("c_lo", [1, MW], f32r)
        bo_row = sb("bo_row", [1, D])
        one_f = sb("one_f", [1, P])
        one_row = sb("one_row", [1, P], f32r)
        ident = sb("ident", [P, P])
        eps_col = sb("eps_col", [P, 1])
        one_zero = sb("one_zero", [P, GT, 2])
        st = sb("st", [P, TB, 6])
        mv = sb("mv", [P, TB, 2])
        std = sb("std", [P, TB])
        rstd = sb("rstd", [P, TB])
        XT_hi = sb("XT_hi", [P, 2, KC, GT * P], f32r)
        XT_lo = sb("XT_lo", [P, 2, KC, GT * P], f32r)
        VS = sb("VS", [P, 2, GT, VW], f32r)
        pos = sb("pos", [P, 2, GT, 4])
        negpos = sb("negpos", [P, TB, 4])
        E = sb("E", [P, TRI])
        rden = sb("rden", [P, GT])
        with ExitStack() as first:
            def early(name, shape):
                return first.enter_context(nc.sbuf_tensor(name, shape, f32))
            XN = early("XN", [P, 2, GT, D])
            sqB = early("sqB", [P, S])
            sqC = early("sqC", [P, S])
            PR = early("PR", [P, 3, S])
        VO = sb("VO", [P, TB, VW], f32r)
        E_hi = sb("E_hi", [P, NE, 512], f32r)
        E_lo = sb("E_lo", [P, NE, 512], f32r)

        T_ps = [pb("T0_ps"), pb("T1_ps")]
        V_ps = [pb("V0_ps"), pb("V1_ps")]
        O_ps = [pb(f"O{j}_ps") for j in range(GT)]

        s_x = sem("s_x")
        s_w = sem("s_w")
        s_const = sem("s_const")
        s_cps = sem("s_cps")
        s_craw = sem("s_craw")
        s_chi = sem("s_chi")
        s_M = sem("s_M")
        s_st = sem("s_st")
        s_mv = sem("s_mv")
        s_std = sem("s_std")
        s_rstd = sem("s_rstd")
        s_xn = sem("s_xn")
        s_T = sem("s_T")
        s_xth = sem("s_xth")
        s_xtl = sem("s_xtl")
        s_vps = [sem(f"s_vps{i}") for i in range(2)]
        s_voh = sem("s_voh")
        s_vol = sem("s_vol")
        s_pos = sem("s_pos")
        s_neg = sem("s_neg")
        s_pr = sem("s_pr")
        s_vow = [sem(f"s_vow{i}") for i in range(2)]
        s_vld = sem("s_vld")
        s_sq = sem("s_sq")
        s_add = sem("s_add")
        s_dist = sem("s_dist")
        s_exp = sem("s_exp")
        s_mask = sem("s_mask")
        s_eh = sem("s_eh")
        s_el = sem("s_el")
        s_eb = sem("s_eb")
        s_acc = sem("s_acc")
        s_rd = sem("s_rd")
        s_x1 = sem("s_x1")
        s_x1out = sem("s_x1out")

        block = ctx.enter_context(nc.Block())

        def off(kt):
            return sum(S - P * k for k in range(kt))

        blocks = [(Q, kt) for Q in reversed(range(GB)) for kt in range(GT * Q + GT)]
        NBLK = len(blocks)
        last_use = {kt: n for n, (Q, kt) in enumerate(blocks)}
        order = list(reversed(range(TB)))

        def block_of(Q, kt):
            q0 = max(P * kt, GT * P * Q)
            w = GT * P * (Q + 1) - q0
            at = off(kt) + q0 - P * kt
            return E[:, at:at + w], w

        @block.sync
        def _(sp):
            for v in range(2):
                sp.sem_inc(s_vow[v], 16)
            for b in range(NB):
                for g in range(GB):
                    n = b * GB + g
                    sp.dma_start(X[:, n * GT:(n + 1) * GT, :], x_v[:, n * GT:(n + 1) * GT, :]).then_inc(s_x, 16)
                sp.wait_ge(s_x, 64 * (b + 1))
            for b in range(NB):
                for g in range(GB):
                    G, v = b * GB + g, g % 2
                    sp.wait_ge(s_vol, G * GT + GT)
                    sp.dma_start(vo_v[:, G, :], VS[:, v, :, :].bitcast(f32).rearrange("p a n -> p (a n)"))\
                      .then_inc(s_vow[v], 16)
                for v in range(2):
                    sp.wait_ge(s_vow[v], 32 * b + 48)
                sp.wait_ge(s_add, 2 * TB * b + 2 * TB + 2)
                sp.dma_start(VO[:, :, :].bitcast(f32).rearrange("p (a t) n -> p a (t n)", a=GB),
                             vo_v[:, b * GB:(b + 1) * GB, :]).then_inc(s_vld, 16)
            sp.wait_ge(s_vld, 16 * NB)

        @block.gpsimd
        def _(pool):
            pool.memset(ident[:, :], 0.0).then_inc(s_const, 1)
            pool.memset(one_f[:, :], 1.0).then_inc(s_const, 1)
            pool.memset(eps_col[:, :], EPS).then_inc(s_const, 1)
            pool.memset(M_raw[:, :, D + 3:MW], 0.0).then_inc(s_const, 1)
            pool.memset(c_raw[:, D + 3:MW], 0.0).then_inc(s_const, 1)
            pool.memset(one_zero[:, :, 0], 1.0).then_inc(s_const, 1)
            pool.memset(one_zero[:, :, 1], 0.0).then_inc(s_const, 1)
            pool.wait_ge(s_const, 7)
            pool.affine_select(out=ident[:, :], in_=ident[:, :], compare_op=ALU.not_equal, fill=1.0, base=0,
                               pattern=[[-1, P]], channel_multiplier=1).then_inc(s_const, 1)
            for b in range(NB):
                for i, kt in enumerate(order):
                    pool.wait_ge(s_exp, b * TB + i + 1)
                    blk = E[:, off(kt):off(kt) + P]
                    pool.affine_select(out=blk, in_=blk, compare_op=ALU.is_ge, fill=0.0, base=0,
                                       pattern=[[1, P]], channel_multiplier=-1).then_inc(s_mask, 1)

        @block.scalar
        def _(act):
            act.sem_inc(s_pr, 3)
            act.dma_start(wv_raw[:, :, :], wv.rearrange("(c p) n -> p c n", c=KC)).then_inc(s_w, 16)
            act.dma_start(woT_raw[:, :, :], woT.rearrange("(c p) n -> p c n", c=KC)).then_inc(s_w, 16)
            act.dma_start(bv_col[:, :], bv.rearrange("(c p) -> p c", c=KC), allow_slow_non_contiguous=True).then_inc(s_w, 16)
            act.dma_start(bo_row[:, :], bo.rearrange("(a n) -> a n", a=1)).then_inc(s_w, 16)
            act.dma_start(M_raw[:, :, D:D + 3], w3dT.rearrange("(c p) n -> p c n", c=KC)).then_inc(s_w, 16)
            act.dma_start(c_raw[:, D:D + 3], b3d.rearrange("(a n) -> a n", a=1)).then_inc(s_w, 16)
            act.wait_ge(s_const, 8)
            with act.Fori(0, NB) as b:
                act.wait_ge(s_mv, TB * b + TB)
                act.activation(std[:, :], mv[:, :, 1], ACT.Sqrt, bias=eps_col[:, 0:1]).then_inc(s_std, 1)
                with act.Fori(0, GB // 2) as g2:
                    for v in range(2):
                        gb = g2 * 2 + v
                        G = b * GB + gb
                        for c in range(KC):
                            act.wait_ge(s_T, 2 * G + c + 1)
                            act.activation(XT_hi[:, v, c, :], T_ps[c][:, :], ACT.Copy).then_inc(s_xth, 1)
                        act.wait_ge(s_vow[v], 32 * b + 16 * g2 + 16)
                        for j in range(GT):
                            act.wait_ge(s_vps[j % 2], unit(G, j))
                            act.activation(VS[:, v, j, 0:D], V_ps[j % 2][:, 0:D], ACT.Copy).then_inc(s_voh, 1)
                        for c in range(3):
                            act.wait_ge(s_vps[c % 2], unit(G, GT + c))
                            act.activation(PR[:, c, bass.ds(gb * (GT * P), GT * P)], V_ps[c % 2][:, :],
                                           ACT.Copy).then_inc(s_pr, 1)
                act.wait_ge(s_pr, 3 * GB * b + 3 * GB + 3)
                act.wait_ge(s_neg, GB * b + GB)
                act.wait_ge(s_el, NBLK * b + 1)

                def squares(i):
                    kt = order[i]
                    span = S - P * kt
                    n = b * TB + i
                    act.activation(E[:, off(kt):off(kt) + span], PR[:, 0, P * kt:S], ACT.Square,
                                   bias=negpos[:, kt, 0:1]).then_inc(s_sq, 1)
                    act.wait_ge(s_add, 2 * n + 1)
                    act.activation(sqB[:, 0:span], PR[:, 1, P * kt:S], ACT.Square,
                                   bias=negpos[:, kt, 1:2]).then_inc(s_sq, 1)
                    act.wait_ge(s_add, 2 * n + 2)
                    act.activation(sqC[:, 0:span], PR[:, 2, P * kt:S], ACT.Square,
                                   bias=negpos[:, kt, 2:3]).then_inc(s_sq, 1)

                def root(i):
                    row = E[:, off(order[i]):off(order[i]) + S - P * order[i]]
                    act.wait_ge(s_add, 2 * (b * TB + i) + 4)
                    act.activation(row, row, ACT.Sqrt).then_inc(s_dist, 1)

                for i in range(TB):
                    squares(i)
                    if i >= 1:
                        root(i - 1)
                root(TB - 1)
                for i, kt in enumerate(order):
                    row = E[:, off(kt):off(kt) + S - P * kt]
                    act.wait_ge(s_dist, b * TB + i + 1)
                    act.activation(row, row, ACT.Exp, scale=-SCALE).then_inc(s_exp, 1)
                for n, (Q, kt) in enumerate(blocks):
                    src, w = block_of(Q, kt)
                    act.wait_ge(s_mask, b * TB + TB - kt)
                    act.wait_ge(s_eb, b * NBLK + n + 1)
                    act.activation(E_hi[:, n % NE, 0:w], src, ACT.Copy).then_inc(s_eh, 1)

        @block.vector
        def _(dve):
            dve.sem_inc(s_xtl, 2)
            dve.sem_inc(s_add, 2)
            dve.sem_inc(s_el, 1)
            dve.sem_inc(s_x1, GT)
            dve.wait_ge(s_w, 96)
            dve.wait_ge(s_const, 8)
            dve.wait_ge(s_cps, 1)
            for c in range(KC):
                dve.tensor_copy(M_raw[:, c, 0:D], V_ps[c][:, 0:D]).then_inc(s_craw, 1)
            dve.tensor_tensor(c_raw[:, 0:D], T_ps[0][0:1, 0:D], bo_row[:, :], ALU.add).then_inc(s_craw, 1)
            dve.wait_ge(s_craw, 3)
            dve.tensor_copy(M_hi[:, :, :], M_raw[:, :, :]).then_inc(s_chi, 1)
            dve.tensor_copy(c_hi[:, :], c_raw[:, :]).then_inc(s_chi, 1)
            dve.tensor_copy(one_row[:, :], one_f[:, :]).then_inc(s_M, 1)
            for v in range(2):
                dve.tensor_copy(VS[:, v, :, D:D + 2], one_zero[:, :, :]).then_inc(s_M, 1)
            dve.wait_ge(s_chi, 2)
            dve.tensor_tensor(M_lo[:, :, :], M_raw[:, :, :], M_hi[:, :, :].bitcast(f32), ALU.subtract).then_inc(s_M, 1)
            dve.tensor_tensor(c_lo[:, :], c_raw[:, :], c_hi[:, :].bitcast(f32), ALU.subtract).then_inc(s_M, 1)
            with dve.Fori(0, NB) as b:
                dve.wait_ge(s_x, 64 * b + 64)
                for t in range(TB + 1):
                    if t >= 1:
                        dve.wait_ge(s_st, b * TB + t)
                    if t < TB:
                        dve.bn_stats(st[:, t, :], tile_of(X, b * TB + t)).then_inc(s_st, 1)
                    else:
                        dve.tensor_copy(rden[:, 0:1], eps_col[:, :])
                    if t >= 1:
                        dve.bn_aggr(mv[:, t - 1, :], st[:, t - 1, :]).then_inc(s_mv, 1)
                dve.wait_ge(s_std, b + 1)
                dve.reciprocal(rstd[:, :], std[:, :]).then_inc(s_rstd, 1)

                with dve.Fori(0, GB // 2) as g2:
                    for v in range(2):
                        gb = g2 * 2 + v
                        G = b * GB + gb
                        dve.wait_ge(s_rstd, b + 1)
                        dve.wait_ge(s_mv, TB * b + TB)
                        for j in range(GT):
                            t = gb * GT + j
                            dve.tensor_scalar(XN[:, v, j, :], tile_of(X, b * TB + t), flat(mv[:, bass.ds(t, 1), 0:1]),
                                              rstd[:, bass.ds(t, 1)], ALU.subtract, ALU.mult).then_inc(s_xn, 1)
                        for c in range(KC):
                            dve.wait_ge(s_xth, 2 * G + c + 1)
                            dve.tensor_tensor(XT_lo[:, v, c, :], T_ps[c][:, :], XT_hi[:, v, c, :].bitcast(f32),
                                              ALU.subtract).then_inc(s_xtl, 1)
                        for j in range(GT):
                            dve.wait_ge(s_voh, GT * G + j + 1)
                            dve.tensor_copy(pos[:, v, j, 0:3], V_ps[j % 2][:, D:D + 3]).then_inc(s_pos, 1)
                            dve.tensor_tensor(VS[:, v, j, D + 2:VW], V_ps[j % 2][:, 0:D], VS[:, v, j, 0:D].bitcast(f32),
                                              ALU.subtract).then_inc(s_vol, 1)
                        dve.wait_ge(s_pos, GT * G + GT)
                        dve.tensor_scalar(negpos[:, bass.ds(gb * GT, GT), 0:3], pos[:, v, :, 0:3], -1.0, None,
                                          ALU.mult).then_inc(s_neg, 1)

                for i, kt in enumerate(order):
                    n = b * TB + i
                    span = S - P * kt
                    row = E[:, off(kt):off(kt) + span]
                    dve.wait_ge(s_sq, 3 * n + 2)
                    dve.tensor_tensor(row, row, sqB[:, 0:span], ALU.add).then_inc(s_add, 1)
                    dve.wait_ge(s_sq, 3 * n + 3)
                    dve.wait_ge(s_add, 2 * n + 3)
                    dve.tensor_tensor(row, row, sqC[:, 0:span], ALU.add).then_inc(s_add, 1)

                def finish(Q, j):
                    t = b * TB + GT * Q + j
                    n = GT * (GB - 1 - Q) + j
                    if j < GT - 1:
                        dve.wait_ge(s_acc, b * (GT - 1) * GB + (GT - 1) * (GB - 1 - Q) + j + 1)
                    else:
                        dve.wait_ge(s_eb, b * NBLK + last_use[GT * Q + j] + 1 + NE)
                    dve.reciprocal(rden[:, j:j + 1], O_ps[j][:, D:D + 1]).then_inc(s_rd, 1)
                    dve.wait_ge(s_rd, b * TB + n + 1)
                    dve.scalar_tensor_tensor(out=tile_of(X, t), in0=O_ps[j][:, 0:D], scalar=rden[:, j:j + 1],
                                             in1=tile_of(X, t), op0=ALU.mult, op1=ALU.add).then_inc(s_x1, 1)

                for n, (Q, kt) in enumerate(blocks):
                    src, w = block_of(Q, kt)
                    dve.wait_ge(s_eh, b * NBLK + n + 1)
                    dve.tensor_tensor(E_lo[:, n % NE, 0:w], src, E_hi[:, n % NE, 0:w].bitcast(f32),
                                      ALU.subtract).then_inc(s_el, 1)
                    if Q < GB - 1 and kt < GT:
                        finish(Q + 1, kt)
                for j in range(GT):
                    finish(0, j)

        @block.tensor
        def _(pe):
            pe.sem_inc(s_eb, NE)
            pe.wait_ge(s_w, 96)
            for ci in range(KC):
                for cd in range(KC):
                    pe.matmul(V_ps[ci][:, 0:D], wv_raw[:, cd, ci * P:(ci + 1) * P], woT_raw[:, cd, :],
                              start=(cd == 0), stop=(cd == KC - 1))
            for cd in range(KC):
                mm = pe.matmul(T_ps[0][0:1, 0:D], bv_col[:, cd:cd + 1], woT_raw[:, cd, :],
                               start=(cd == 0), stop=(cd == KC - 1))
            mm.then_inc(s_cps, 1)
            pe.wait_ge(s_const, 8)
            pe.wait_ge(s_M, 5)
            with pe.Fori(0, NB) as b:
                with pe.Fori(0, GB // 2) as g2:
                    for v in range(2):
                        G = b * GB + g2 * 2 + v
                        pe.wait_ge(s_xn, GT * G + GT)
                        for c in range(KC):
                            pe.wait_ge(s_xtl, 2 * G + c + 1)
                            for j in range(GT):
                                mm = pe.transpose(T_ps[c][:, j * P:(j + 1) * P], XN[:, v, j, c * P:(c + 1) * P],
                                                  ident[:, :])
                            mm.then_inc(s_T, 1)
                        pe.wait_ge(s_xtl, 2 * G + 4)
                        for j in range(GT):
                            if j < 2:
                                pe.wait_ge(s_pr, 3 * G + 3 - j)
                            else:
                                pe.wait_ge(s_vol, GT * G + j - 1)
                            tok = slice(j * P, (j + 1) * P)
                            out = V_ps[j % 2][:, 0:MW]
                            for c in range(KC):
                                pe.matmul(out, XT_hi[:, v, c, tok], M_hi[:, c, :], start=(c == 0), stop=False)
                                pe.matmul(out, XT_hi[:, v, c, tok], M_lo[:, c, :], start=False, stop=False)
                                pe.matmul(out, XT_lo[:, v, c, tok], M_hi[:, c, :], start=False, stop=False)
                            pe.matmul(out, one_row[:, :], c_hi[:, :], start=False, stop=False)
                            pe.matmul(out, one_row[:, :], c_lo[:, :], start=False, stop=True).then_inc(s_vps[j % 2], 1)
                        pe.wait_ge(s_pos, GT * G + GT)
                        for c in range(3):
                            if c < 2:
                                pe.wait_ge(s_vol, GT * G + 3 + c)
                            else:
                                pe.wait_ge(s_pr, 3 * G + 4)
                            for j in range(GT):
                                mm = pe.transpose(V_ps[c % 2][:, j * P:(j + 1) * P],
                                                  pos[:, v, j, c:c + 1].to_broadcast([P, P]), ident[:, :])
                            mm.then_inc(s_vps[c % 2], 1)
                pe.wait_ge(s_vld, 16 * b + 16)
                for n, (Q, kt) in enumerate(blocks):
                    pe.wait_ge(s_el, b * NBLK + n + 2)
                    q0 = max(kt, GT * Q)
                    for qt in range(q0, GT * Q + GT):
                        j = qt - GT * Q
                        if kt == 0:
                            pe.wait_ge(s_x1, b * TB + GT * (GB - 1 - Q) + j + 1)
                        cols = slice((qt - q0) * P, (qt - q0 + 1) * P)
                        pe.matmul(O_ps[j][:, 0:D + 2], E_hi[:, n % NE, cols], VO[:, kt, 0:D + 2],
                                  start=(kt == 0), stop=False)
                        pe.matmul(O_ps[j][:, 0:D], E_hi[:, n % NE, cols], VO[:, kt, D + 2:VW], start=False, stop=False)
                        mm = pe.matmul(O_ps[j][:, 0:D + 2], E_lo[:, n % NE, cols], VO[:, kt, 0:D + 2],
                                       start=False, stop=(kt == qt))
                        if kt == qt and j < GT - 1:
                            mm.then_inc(s_acc, 1)
                    mm.then_inc(s_eb, 1)

    with ExitStack() as ctx:
        def sb(name, shape, dt=f32):
            return ctx.enter_context(nc.sbuf_tensor(name, shape, dt))

        def sem(name):
            return ctx.enter_context(nc.semaphore(name))

        ident = sb("ident2", [P, P])
        eps_col = sb("eps_col2", [P, 1])
        st = sb("st2", [P, TB, 6])
        mv = sb("mv2", [P, TB, 2])
        std = sb("std2", [P, TB])
        rstd = sb("rstd2", [P, TB])
        carry = sb("carry2", [P, 1])
        gate_raw = sb("gate_raw", [P, KC, NX])
        gate_hi = sb("gate_hi", [P, KC, NX], f32r)
        gate_lo = sb("gate_lo", [P, KC, NX], f32r)
        gbias = sb("gbias", [P, NX])
        logit = sb("logit", [P, NT, NX])
        score = sb("score", [P, NT, NX])
        biased = sb("biased", [P, NT, NX])
        pick = [sb(f"pick{k}", [P, NT, NX]) for k in range(TOPK)]
        tmp = sb("tmp", [P, NT, NX])
        slot_e = sb("slot_e", [P, NT, NX])
        chosen = sb("chosen", [P, NT, NX], bf16)
        total = sb("total", [P, NX, NT])
        upto = sb("upto", [P, NX, NT])
        keep = sb("keep", [P, NX, NT])
        red = sb("red", [P, NT])
        red2 = sb("red2", [P, NT])
        weight = [sb(f"weight{k}", [P, NT]) for k in range(TOPK)]
        slot = [sb(f"slot{k}", [P, NT], u32) for k in range(TOPK)]
        rank = sb("rank", [P, NX])
        before = sb("before", [P, P], bf16)
        ones_b = sb("ones_b", [P, P], bf16)
        one8 = sb("one8", [P, NX])
        n_i = sb("n_i", [P, NX], i32)
        n_j = sb("n_j", [P, NX], i32)
        n_f = sb("n_f", [P, NX])
        ends = sb("ends", [P, NX])
        base = sb("base", [P, NX])
        tile_id = sb("tile_id", [P, NSLOT])
        passed = sb("passed", [P, NSLOT, NX])
        which = sb("which", [P, NSLOT])
        expert = sb("expert", [P, NSLOT], i32)
        XR = sb("XR", [P, 4, D])
        zero = sb("zero", [P, D])
        with ExitStack() as first:
            def early(name, shape, dt=f32):
                return first.enter_context(nc.sbuf_tensor(name, shape, dt))
            XN = early("XN2", [P, 2, GT, D])
            XT_hi = early("XT2_hi", [P, 2, KC, GT * P], f32r)
            XT_lo = early("XT2_lo", [P, 2, KC, GT * P], f32r)
            sw13_raw = early("sw13_raw", [P, KC, 2 * NS])
            sw2_raw = early("sw2_raw", [P, MC, D])
            sw13_hi = early("sw13_hi", [P, KC, 2 * NS], f32r)
            sw13_lo = early("sw13_lo", [P, KC, 2 * NS], f32r)
            sw2_hi = early("sw2_hi", [P, MC, D], f32r)
            sw2_lo = early("sw2_lo", [P, MC, D], f32r)
            sg = early("sg", [P, 2, GT * P])
            hf = early("hf", [P, 2, GT * P])
            h_hi = early("h_hi", [P, 2, GT * P], f32r)
            h_lo = early("h_lo", [P, 2, GT * P], f32r)
        W_raw = sb("W_raw", [P, 2, KC, 3 * D])
        W_hi = sb("W_hi", [P, KC, NX, 3 * D], f32r)
        W_lo = sb("W_lo", [P, KC, NX, 3 * D], f32r)
        XS = sb("XS", [P, 4, D])
        XST_hi = sb("XST_hi", [P, 2, KC, P], f32r)
        XST_lo = sb("XST_lo", [P, 2, KC, P], f32r)
        sr = sb("sr", [P, 2, D])
        hr = sb("hr", [P, 2, D])
        hT_hi = sb("hT_hi", [P, 2, KC, P], f32r)
        hT_lo = sb("hT_lo", [P, 2, KC, P], f32r)
        YS = sb("YS", [P, 2, D])
        YG = sb("YG", [P, 4, TOPK, D])

        bank = [ctx.enter_context(nc.psum_tensor(f"bank{i}", [P, 512], f32)) for i in range(8)]
        T_ps, G_ps, U_ps, Z_ps = bank[0:2], bank[2:4], bank[4:6], bank[6:8]
        XT_ps, S_ps, HT_ps, Y_ps = bank[0:2], bank[2:4], bank[4:6], bank[6:8]

        s_const = sem("f_const")
        s_w = sem("f_w")
        s_whi = sem("f_whi")
        s_wlo = sem("f_wlo")
        s_st = sem("f_st")
        s_mv = sem("f_mv")
        s_std = sem("f_std")
        s_rstd = sem("f_rstd")
        s_xn = sem("f_xn")
        s_xst = [sem(f"f_xst{i}") for i in range(2)]
        s_T = sem("f_T")
        s_xth = sem("f_xth")
        s_xtl = sem("f_xtl")
        s_lps = sem("f_lps")
        s_lg = sem("f_lg")
        s_g = sem("f_g")
        s_u = sem("f_u")
        s_sg = sem("f_sg")
        s_hf = sem("f_hf")
        s_hh = sem("f_hh")
        s_hl = sem("f_hl")
        s_hu = sem("f_hu")
        s_z = sem("f_z")
        s_zf = sem("f_zf")
        s_r = sem("f_r")
        s_ex = sem("f_ex")
        s_cnt = sem("f_cnt")
        s_zero = sem("f_zero")
        s_slot = sem("f_slot")
        s_xr = [sem(f"f_xr{i}") for i in range(4)]
        s_sc = [sem(f"f_sc{i}") for i in range(4)]
        s_wr = [sem(f"f_wr{i}") for i in range(2)]
        s_wrh = sem("f_wrh")
        s_wrl = sem("f_wrl")
        s_xs = [sem(f"f_xs{i}") for i in range(4)]
        s_xsT = sem("f_xsT")
        s_xsh = sem("f_xsh")
        s_xsl = sem("f_xsl")
        s_s1 = sem("f_s1")
        s_sr = sem("f_sr")
        s_hr = sem("f_hr")
        s_hT = sem("f_hT")
        s_hTh = sem("f_hTh")
        s_hTl = sem("f_hTl")
        s_s2 = sem("f_s2")
        s_ys = sem("f_ys")
        s_yst = [sem(f"f_yst{i}") for i in range(2)]
        s_yg = [sem(f"f_yg{i}") for i in range(4)]
        s_y = sem("f_y")
        s_out = sem("f_out")

        block = ctx.enter_context(nc.Block())

        @block.sync
        def _(sp):
            for v in range(2):
                sp.sem_inc(s_xst[v], 16)
            sp.dma_start(sw13_raw[:, :, :], sw13T.rearrange("(c p) n -> p c n", p=P)).then_inc(s_w, 16)
            sp.dma_start(sw2_raw[:, :, :], sw2T.rearrange("(c p) n -> p c n", p=P)).then_inc(s_w, 16)
            sp.dma_start(gate_raw[:, :, :], gateT.rearrange("(c p) n -> p c n", p=P)).then_inc(s_w, 16)
            sp.dma_start(gbias[:, :], gate_bias.rearrange("(a n) -> a n", a=1).to_broadcast([P, NX])).then_inc(s_w, 16)
            for G in range(NG):
                sp.wait_ge(s_xn, GT * G + GT)
                sp.dma_start(xn_v[:, GT * G:GT * G + GT, :], XN[:, G % 2, :, :]).then_inc(s_xst[G % 2], 16)
            sp.wait_ge(s_zf, 2 * NG + 2)
            for v in range(2):
                sp.wait_ge(s_xst[v], 8 * NG + 16)
            for e in range(NX):
                for t in range(e * NT // NX, (e + 1) * NT // NX):
                    if t >= 4:
                        sp.wait_ge(s_sc[t % 4], 16 * TOPK * (t // 4))
                    sp.dma_start(XR[:, t % 4, :], xn_v[:, t, :]).then_inc(s_xr[t % 4], 16)
                if e >= 2:
                    sp.wait_ge(s_wrh, e - 1)
                    sp.wait_ge(s_wrl, e - 1)
                sp.dma_start(W_raw[:, e % 2, :, :], wT[e, :, :].rearrange("(c p) n -> p c n", p=P))\
                  .then_inc(s_wr[e % 2], 16)
            for k in range(4):
                sp.wait_ge(s_sc[k], 16 * TOPK * NT // 4)
            for k in range(4):
                sp.dma_start(XS[:, k, :], xs_t[k, :, :]).then_inc(s_xs[k], 16)
            for i in range(NSLOT):
                if i + 4 < NSLOT:
                    sp.wait_ge(s_xsT, i + 1)
                    sp.dma_start(XS[:, i % 4, :], xs_t[i + 4, :, :]).then_inc(s_xs[i % 4], 16)
                sp.wait_ge(s_ys, i + 3)
                sp.dma_start(ys_t[i, :, :], YS[:, i % 2, :]).then_inc(s_yst[i % 2], 16)
            for t in range(NT):
                sp.wait_ge(s_y, TOPK * t + TOPK)
                sp.dma_start(out_v[:, t, :], X[:, t, :]).then_inc(s_out, 16)
            sp.wait_ge(s_out, 16 * NT)

        @block.gpsimd
        def _(pool):
            def const(ins):
                ins.then_inc(s_const, 1)
            const(pool.memset(ident[:, :], 0.0))
            const(pool.memset(before[:, :], 1.0))
            const(pool.memset(ones_b[:, :], 1.0))
            const(pool.memset(eps_col[:, :], EPS))
            const(pool.memset(one8[:, :], 1.0))
            const(pool.memset(keep[:, :, 1:NT], 1.0))
            const(pool.memset(keep[:, :, 0:1], 0.0))
            const(pool.iota(rank[:, :], pattern=[[-1, NX]], base=NX, channel_multiplier=0,
                            allow_small_or_imprecise_dtypes=True))
            const(pool.iota(tile_id[:, :], pattern=[[1, NSLOT]], base=0, channel_multiplier=0,
                            allow_small_or_imprecise_dtypes=True))
            const(pool.memset(zero[:, :], 0.0))
            pool.wait_ge(s_const, 10)
            const(pool.affine_select(out=ident[:, :], in_=ident[:, :], compare_op=ALU.not_equal, fill=1.0, base=0,
                                     pattern=[[-1, P]], channel_multiplier=1))
            const(pool.affine_select(out=before[:, :], in_=before[:, :], compare_op=ALU.is_gt, fill=0.0, base=0,
                                     pattern=[[1, P]], channel_multiplier=-1))
            pool.wait_ge(s_slot, 2)
            pool.wait_ge(s_zero, 128)
            for t in range(NT):
                pool.wait_ge(s_xr[t % 4], 16 * (t // 4 + 1))
                for k in range(TOPK):
                    pool.indirect_dma_start(out=xs, out_offset=bass.IndirectOffsetOnAxis(ap=slot[k][:, t:t + 1], axis=0),
                                            in_=XR[:, t % 4, :], in_offset=None).then_inc(s_sc[t % 4], 16)
            for v in range(2):
                pool.wait_ge(s_yst[v], 16 * (NSLOT // 2) + 16)
            for t in range(NT):
                if t >= 4:
                    pool.wait_ge(s_y, TOPK * (t - 3))
                for k in range(TOPK):
                    pool.indirect_dma_start(out=YG[:, t % 4, k, :], out_offset=None, in_=ys,
                                            in_offset=bass.IndirectOffsetOnAxis(ap=slot[k][:, t:t + 1], axis=0))\
                        .then_inc(s_yg[t % 4], 16)

        @block.scalar
        def _(act):
            act.sem_inc(s_yst[0], 16)
            act.sem_inc(s_yst[1], 16)
            act.sem_inc(s_ys, 2)
            act.wait_ge(s_const, 12)
            for i in range(8):
                w = NSLOT // 8
                act.dma_start(xs_p[:, i * w:(i + 1) * w, :], zero[:, :].unsqueeze(1).to_broadcast([P, w, D]))\
                   .then_inc(s_zero, 16)
            act.wait_ge(s_w, 64)
            act.activation(sw13_hi[:, :, :], sw13_raw[:, :, :], ACT.Copy).then_inc(s_whi, 1)
            act.activation(sw2_hi[:, :, :], sw2_raw[:, :, :], ACT.Copy).then_inc(s_whi, 1)
            act.activation(gate_hi[:, :, :], gate_raw[:, :, :], ACT.Copy).then_inc(s_whi, 1)
            with act.Fori(0, NB) as b:
                act.wait_ge(s_mv, TB * b + TB)
                act.activation(std[:, :], mv[:, :, 1], ACT.Sqrt, bias=eps_col[:, 0:1]).then_inc(s_std, 1)
                with act.Fori(0, GB // 2) as g2:
                    for v in range(2):
                        G = b * GB + g2 * 2 + v
                        for c in range(KC):
                            act.wait_ge(s_T, 2 * G + c + 1)
                            act.activation(XT_hi[:, v, c, :], T_ps[c][:, :], ACT.Copy).then_inc(s_xth, 1)
                        for m in range(MC):
                            n = MC * G + m
                            act.wait_ge(s_g, n + 1)
                            act.activation(sg[:, m % 2, :], G_ps[m % 2][:, :], ACT.Silu).then_inc(s_sg, 1)
                            act.wait_ge(s_hf, n + 3)
                            if m == 1:
                                act.wait_ge(s_z, 2 * G + 1)
                            else:
                                act.wait_ge(s_hu, 3 * G + max(m, 1))
                            act.activation(h_hi[:, m % 2, :], hf[:, m % 2, :], ACT.Copy).then_inc(s_hh, 1)
            act.wait_ge(s_r, 2)
            act.activation(tmp[:, :, :], logit[:, :, :], ACT.Exp).then_inc(s_ex, 1)
            for e in range(NX):
                act.wait_ge(s_wr[e % 2], 16 * (e // 2 + 1))
                act.activation(W_hi[:, :, e, :], W_raw[:, e % 2, :, :], ACT.Copy).then_inc(s_wrh, 1)

            def hidden_hi(i, v):
                act.wait_ge(s_hT, i + 1)
                act.activation(hT_hi[:, v, :, :], HT_ps[v][:, 0:D].rearrange("p (c n) -> p c n", c=KC), ACT.Copy)\
                   .then_inc(s_hTh, 1)

            def silu(i, v):
                act.wait_ge(s_s1, i + 1)
                act.activation(sr[:, v, :], S_ps[v][:, 0:D], ACT.Silu).then_inc(s_sr, 1)

            def tokens_hi(i, v):
                act.wait_ge(s_xsT, i + 1)
                act.activation(XST_hi[:, v, :, :], XT_ps[v][:, 0:D].rearrange("p (c n) -> p c n", c=KC), ACT.Copy)\
                   .then_inc(s_xsh, 1)

            def output(i, v, k):
                act.wait_ge(s_s2, i + 1)
                act.wait_ge(s_yst[v], 16 * k + 16)
                act.activation(YS[:, v, :], Y_ps[v][:, 0:D], ACT.Copy).then_inc(s_ys, 1)

            tokens_hi(0, 0)
            silu(0, 0)
            tokens_hi(1, 1)
            with act.Fori(0, NSLOT // 2 - 1) as k:
                for v in range(2):
                    hidden_hi(k * 2 + v, v)
                    silu(k * 2 + v + 1, 1 - v)
                    tokens_hi(k * 2 + v + 2, v)
                    output(k * 2 + v, v, k)
            hidden_hi(NSLOT - 2, 0)
            silu(NSLOT - 1, 1)
            output(NSLOT - 2, 0, NSLOT // 2 - 1)
            hidden_hi(NSLOT - 1, 1)
            output(NSLOT - 1, 1, NSLOT // 2 - 1)

        @block.vector
        def _(dve):
            dve.sem_inc(s_xtl, 2)
            dve.sem_inc(s_lg, 1)
            dve.sem_inc(s_hf, 2)
            dve.sem_inc(s_zf, 2)
            dve.sem_inc(s_xsl, 2)
            dve.sem_inc(s_hTl, 2)
            dve.sem_inc(s_hr, 2)
            dve.wait_ge(s_w, 64)
            dve.wait_ge(s_const, 12)
            dve.wait_ge(s_whi, 3)
            for raw, hi, lo in ((sw13_raw, sw13_hi, sw13_lo), (sw2_raw, sw2_hi, sw2_lo), (gate_raw, gate_hi, gate_lo)):
                dve.tensor_tensor(lo[:, :, :], raw[:, :, :], hi[:, :, :].bitcast(f32), ALU.subtract).then_inc(s_wlo, 1)
            with dve.Fori(0, NB) as b:
                for t in range(TB + 1):
                    if t >= 1:
                        dve.wait_ge(s_st, b * TB + t)
                    if t < TB:
                        dve.bn_stats(st[:, t, :], tile_of(X, b * TB + t)).then_inc(s_st, 1)
                    else:
                        dve.tensor_copy(carry[:, :], eps_col[:, :])
                    if t >= 1:
                        dve.bn_aggr(mv[:, t - 1, :], st[:, t - 1, :]).then_inc(s_mv, 1)
                dve.wait_ge(s_std, b + 1)
                dve.reciprocal(rstd[:, :], std[:, :]).then_inc(s_rstd, 1)
                with dve.Fori(0, GB // 2) as g2:
                    for v in range(2):
                        gb = g2 * 2 + v
                        G = b * GB + gb
                        dve.wait_ge(s_rstd, b + 1)
                        dve.wait_ge(s_mv, TB * b + TB)
                        dve.wait_ge(s_xst[v], 32 * b + 16 * g2 + 16)
                        for j in range(GT):
                            t = gb * GT + j
                            dve.tensor_scalar(XN[:, v, j, :], tile_of(X, b * TB + t), flat(mv[:, bass.ds(t, 1), 0:1]),
                                              rstd[:, bass.ds(t, 1)], ALU.subtract, ALU.mult).then_inc(s_xn, 1)
                        for c in range(KC):
                            dve.wait_ge(s_xth, 2 * G + c + 1)
                            dve.tensor_tensor(XT_lo[:, v, c, :], T_ps[c][:, :], XT_hi[:, v, c, :].bitcast(f32),
                                              ALU.subtract).then_inc(s_xtl, 1)
                        dve.wait_ge(s_lps, G + 1)
                        dve.tensor_copy(logit[:, bass.ds(G * GT, GT), :],
                                        T_ps[0][:, 0:GT * NX].rearrange("p (t e) -> p t e", t=GT)).then_inc(s_lg, 1)
                        for m in range(MC):
                            n = MC * G + m
                            dve.wait_ge(s_sg, n + 1)
                            dve.wait_ge(s_u, n + 1)
                            dve.tensor_tensor(hf[:, m % 2, :], U_ps[m % 2][:, :], sg[:, m % 2, :], ALU.mult)\
                               .then_inc(s_hf, 1)
                            dve.wait_ge(s_hh, n + 1)
                            dve.tensor_tensor(h_lo[:, m % 2, :], hf[:, m % 2, :], h_hi[:, m % 2, :].bitcast(f32),
                                              ALU.subtract).then_inc(s_hl, 1)
                        for z in range(2):
                            dve.wait_ge(s_z, 2 * G + z + 2)
                            xz = X[:, bass.ds(G * GT + 2 * z, 2), :].rearrange("p t n -> p (t n)")
                            dve.tensor_tensor(xz, xz, Z_ps[z][:, :], ALU.add).then_inc(s_zf, 1)

            step = [0]

            def done(ins):
                step[0] += 1
                ins.then_inc(s_r, 1)
                dve.wait_ge(s_r, step[0])

            def over_e(ap):
                return ap[:, :].unsqueeze(2).to_broadcast([P, NT, NX])

            def over_t(ap):
                return ap[:, :].unsqueeze(1).to_broadcast([P, NT, NX])

            dve.wait_ge(s_lg, NG + 1)
            done(dve.tensor_reduce(red[:, :], logit[:, :, :], AX.X, ALU.max))
            done(dve.tensor_tensor(logit[:, :, :], logit[:, :, :], over_e(red), ALU.subtract))
            dve.wait_ge(s_ex, 1)
            done(dve.tensor_reduce(red[:, :], tmp[:, :, :], AX.X, ALU.add))
            done(dve.reciprocal(red2[:, :], red[:, :]))
            done(dve.tensor_tensor(score[:, :, :], tmp[:, :, :], over_e(red2), ALU.mult))
            done(dve.tensor_tensor(biased[:, :, :], score[:, :, :], over_t(gbias), ALU.add))
            for k in range(TOPK):
                done(dve.tensor_reduce(red[:, :], biased[:, :, :], AX.X, ALU.max))
                done(dve.tensor_tensor(tmp[:, :, :], biased[:, :, :], over_e(red), ALU.is_equal))
                done(dve.tensor_tensor(tmp[:, :, :], tmp[:, :, :], over_t(rank), ALU.mult))
                done(dve.tensor_reduce(red2[:, :], tmp[:, :, :], AX.X, ALU.max))
                done(dve.tensor_tensor(pick[k][:, :, :], over_t(rank), over_e(red2), ALU.is_equal))
                if k + 1 < TOPK:
                    done(dve.scalar_tensor_tensor(out=biased[:, :, :], in0=pick[k][:, :, :], scalar=-3.0e38,
                                                  in1=biased[:, :, :], op0=ALU.mult, op1=ALU.add))
            done(dve.tensor_tensor(chosen[:, :, :], pick[0][:, :, :], pick[1][:, :, :], ALU.add))
            assert step[0] == N_CHOSEN
            for k in range(TOPK):
                done(dve.tensor_tensor(tmp[:, :, :], pick[k][:, :, :], score[:, :, :], ALU.mult))
                done(dve.tensor_reduce(weight[k][:, :], tmp[:, :, :], AX.X, ALU.add))
            dve.wait_ge(s_cnt, 1)
            done(dve.tensor_copy(total[:, :, :], bank[1][:, 0:NT * NX].rearrange("p (t e) -> p e t", t=NT)))
            flat3 = [ap[:, :, :].rearrange("p e t -> p (e t)") for ap in (keep, total, upto)]
            done(dve.tensor_tensor_scan(out=flat3[2], data0=flat3[0], data1=flat3[1], initial=0.0,
                                        op0=ALU.mult, op1=ALU.add))
            done(dve.tensor_scalar(n_i[:, :], upto[:, :, NT - 1], float(P - 1), None, ALU.add))
            done(dve.tensor_scalar(n_j[:, :], n_i[:, :], P.bit_length() - 1, None, ALU.logical_shift_right))
            done(dve.tensor_copy(n_f[:, :], n_j[:, :]))
            done(dve.tensor_tensor_scan(out=ends[:, :], data0=one8[:, :], data1=n_f[:, :], initial=0.0,
                                        op0=ALU.mult, op1=ALU.add))
            done(dve.tensor_tensor(base[:, :], ends[:, :], n_f[:, :], ALU.subtract))
            done(dve.tensor_scalar(base[:, :], base[:, :], float(P), None, ALU.mult))
            done(dve.tensor_tensor(upto[:, :, :], upto[:, :, :], total[:, :, :], ALU.subtract))
            done(dve.tensor_tensor(upto[:, :, :], upto[:, :, :],
                                   base[:, :].unsqueeze(2).to_broadcast([P, NX, NT]), ALU.add))
            done(dve.tensor_tensor(slot_e[:, :, :], bank[0][:, 0:NT * NX].rearrange("p (t e) -> p t e", t=NT),
                                   upto[:, :, :].rearrange("p e t -> p t e"), ALU.add))
            for k in range(TOPK):
                done(dve.tensor_tensor(tmp[:, :, :], pick[k][:, :, :], slot_e[:, :, :], ALU.mult))
                done(dve.tensor_reduce(red[:, :], tmp[:, :, :], AX.X, ALU.add))
                done(dve.tensor_copy(slot[k][:, :], red[:, :]))
            dve.sem_inc(s_slot, 1)
            done(dve.tensor_tensor(passed[:, :, :], tile_id[:, :].unsqueeze(2).to_broadcast([P, NSLOT, NX]),
                                   ends[:, :].unsqueeze(1).to_broadcast([P, NSLOT, NX]), ALU.is_ge))
            done(dve.tensor_reduce(which[:, :], passed[:, :, :], AX.X, ALU.add))
            done(dve.tensor_scalar(expert[:, :], which[:, :], float(NX - 1), None, ALU.min))
            dve.sem_inc(s_slot, 1)
            for e in range(NX):
                dve.wait_ge(s_wrh, e + 1)
                dve.tensor_tensor(W_lo[:, :, e, :], W_raw[:, e % 2, :, :], W_hi[:, :, e, :].bitcast(f32),
                                  ALU.subtract).then_inc(s_wrl, 1)

            def hidden_lo(i, v):
                dve.wait_ge(s_hTh, i + 1)
                dve.tensor_tensor(hT_lo[:, v, :, :], HT_ps[v][:, 0:D].rearrange("p (c n) -> p c n", c=KC),
                                  hT_hi[:, v, :, :].bitcast(f32), ALU.subtract).then_inc(s_hTl, 1)

            def hidden(i, v):
                dve.wait_ge(s_sr, i + 1)
                dve.tensor_tensor(hr[:, v, :], S_ps[v][:, D:2 * D], sr[:, v, :], ALU.mult).then_inc(s_hr, 1)

            def tokens_lo(i, v):
                dve.wait_ge(s_xsh, i + 1)
                dve.tensor_tensor(XST_lo[:, v, :, :], XT_ps[v][:, 0:D].rearrange("p (c n) -> p c n", c=KC),
                                  XST_hi[:, v, :, :].bitcast(f32), ALU.subtract).then_inc(s_xsl, 1)

            tokens_lo(0, 0)
            hidden(0, 0)
            tokens_lo(1, 1)
            with dve.Fori(0, NSLOT // 2 - 1) as k:
                for v in range(2):
                    hidden_lo(k * 2 + v, v)
                    hidden(k * 2 + v + 1, 1 - v)
                    tokens_lo(k * 2 + v + 2, v)
            hidden_lo(NSLOT - 2, 0)
            hidden(NSLOT - 1, 1)
            hidden_lo(NSLOT - 1, 1)
            for t in range(NT):
                dve.wait_ge(s_yg[t % 4], 16 * TOPK * (t // 4 + 1))
                for k in range(TOPK):
                    if k:
                        dve.wait_ge(s_y, TOPK * t + k)
                    dve.scalar_tensor_tensor(out=X[:, t, :], in0=YG[:, t % 4, k, :], scalar=weight[k][:, t:t + 1],
                                             in1=X[:, t, :], op0=ALU.mult, op1=ALU.add).then_inc(s_y, 1)

        @block.tensor
        def _(pe):
            pe.sem_inc(s_hu, 1)
            pe.sem_inc(s_z, 1)
            pe.wait_ge(s_const, 12)
            pe.wait_ge(s_whi, 3)
            pe.wait_ge(s_wlo, 3)

            def three(out, a_hi, a_lo, b_hi, b_lo, start, stop, **kw):
                pe.matmul(out, a_hi, b_hi, start=start, stop=False, **kw)
                pe.matmul(out, a_hi, b_lo, start=False, stop=False, **kw)
                return pe.matmul(out, a_lo, b_hi, start=False, stop=stop, **kw)

            with pe.Fori(0, NB) as b:
                with pe.Fori(0, GB // 2) as g2:
                    for v in range(2):
                        G = b * GB + g2 * 2 + v
                        pe.wait_ge(s_xn, GT * G + GT)
                        pe.wait_ge(s_lg, G + 1)
                        for c in range(KC):
                            pe.wait_ge(s_xtl, 2 * G + c + 1)
                            for j in range(GT):
                                mm = pe.transpose(T_ps[c][:, j * P:(j + 1) * P], XN[:, v, j, c * P:(c + 1) * P],
                                                  ident[:, :])
                            mm.then_inc(s_T, 1)
                        pe.wait_ge(s_xtl, 2 * G + 4)

                        def products(m):
                            n = MC * G + m
                            pe.wait_ge(s_hf, n + 1)
                            for w, bk, s_ready in ((0, G_ps, s_g), (NS, U_ps, s_u)):
                                rows = slice(w + m * P, w + (m + 1) * P)
                                for c in range(KC):
                                    mm = three(bk[m % 2][:, :], sw13_hi[:, c, rows], sw13_lo[:, c, rows],
                                               XT_hi[:, v, c, :], XT_lo[:, v, c, :], c == 0, c == KC - 1)
                                mm.then_inc(s_ready, 1)

                        def outputs(m):
                            n = MC * G + m
                            pe.wait_ge(s_hl, n + 1)
                            for j in range(GT):
                                if m == 0 and j % 2 == 0:
                                    pe.wait_ge(s_zf, 2 * G + j // 2 + 1)
                                tok = slice(j * P, (j + 1) * P)
                                mm = three(Z_ps[j // 2][:, (j % 2) * D:(j % 2 + 1) * D], h_hi[:, m % 2, tok],
                                           h_lo[:, m % 2, tok], sw2_hi[:, m, :], sw2_lo[:, m, :],
                                           m == 0 and j % 2 == 0, m == MC - 1, skip_group_check=True)
                                if m == MC - 1 and j == 1:
                                    mm.then_inc(s_z, 1)
                            mm.then_inc(s_z if m == MC - 1 else s_hu, 1)

                        products(0)
                        for j in range(GT):
                            tok = slice(j * P, (j + 1) * P)
                            for c in range(KC):
                                mm = three(T_ps[0][:, j * NX:(j + 1) * NX], XT_hi[:, v, c, tok], XT_lo[:, v, c, tok],
                                           gate_hi[:, c, :], gate_lo[:, c, :], c == 0, c == KC - 1)
                        mm.then_inc(s_lps, 1)
                        products(1)
                        outputs(0)
                        products(2)
                        outputs(1)
                        products(3)
                        outputs(2)
                        outputs(3)
            pe.wait_ge(s_r, N_CHOSEN)
            rhs = chosen[:, :, :].rearrange("p t e -> p (t e)")
            pe.matmul(bank[0][:, 0:NT * NX], before[:, :], rhs, start=True, stop=True)
            pe.matmul(bank[1][:, 0:NT * NX], ones_b[:, :], rhs, start=True, stop=True).then_inc(s_cnt, 1)
            pe.wait_ge(s_slot, 2)
            pe.wait_ge(s_wrl, NX)
            pe.wait_ge(s_wrh, NX)

            def weights(i, lo, hi):
                e = pe.value_load(expert[0:1, bass.ds(i, 1)], min_val=0, max_val=NX - 1)
                return [[w[:, c, bass.ds(e, 1), lo:hi].rearrange("p a n -> p (a n)") for w in (W_hi, W_lo)]
                        for c in range(KC)]

            def transpose_tokens(i, v, slot4, k4):
                pe.wait_ge(s_xs[slot4], 16 * k4 + 16)
                pe.wait_ge(s_xsl, i + 1)
                for c in range(KC):
                    mm = pe.transpose(XT_ps[v][:, c * P:(c + 1) * P], XS[:, slot4, c * P:(c + 1) * P], ident[:, :])
                mm.then_inc(s_xsT, 1)

            def gate_up(i, v):
                w = weights(i, 0, 2 * D)
                pe.wait_ge(s_xsl, i + 3)
                pe.wait_ge(s_hr, i + 1)
                for c in range(KC):
                    mm = three(S_ps[v][:, :], XST_hi[:, v, c, :], XST_lo[:, v, c, :], w[c][0], w[c][1],
                               c == 0, c == KC - 1)
                mm.then_inc(s_s1, 1)

            def transpose_hidden(i, v):
                pe.wait_ge(s_hr, i + 3)
                pe.wait_ge(s_hTl, i + 1)
                for c in range(KC):
                    mm = pe.transpose(HT_ps[v][:, c * P:(c + 1) * P], hr[:, v, c * P:(c + 1) * P], ident[:, :])
                mm.then_inc(s_hT, 1)

            def down(i, v):
                w = weights(i, 2 * D, 3 * D)
                pe.wait_ge(s_hTl, i + 3)
                pe.wait_ge(s_ys, i + 1)
                for c in range(KC):
                    mm = three(Y_ps[v][:, 0:D], hT_hi[:, v, c, :], hT_lo[:, v, c, :], w[c][0], w[c][1],
                               c == 0, c == KC - 1)
                mm.then_inc(s_s2, 1)

            LOOP = NSLOT // 4 - 1
            transpose_tokens(0, 0, 0, 0)
            gate_up(0, 0)
            transpose_tokens(1, 1, 1, 0)
            with pe.Fori(0, LOOP) as k:
                for q in range(4):
                    i, v = k * 4 + q, q % 2
                    transpose_hidden(i, v)
                    gate_up(i + 1, 1 - v)
                    transpose_tokens(i + 2, v, (q + 2) % 4, k + (q + 2) // 4)
                    down(i, v)
            for i in range(4 * LOOP, NSLOT):
                v = i % 2
                transpose_hidden(i, v)
                if i + 1 < NSLOT:
                    gate_up(i + 1, 1 - v)
                if i + 2 < NSLOT:
                    transpose_tokens(i + 2, v, (i + 2) % 4, (i + 2) // 4)
                down(i, v)

    outer.close()


def kernel(**inputs):
    import numpy as _np
    import concourse.bacc as _bacc
    from concourse import mybir as _mybir
    from concourse.bass_utils import run_bass_kernel_spmd as _run

    a = {name: _np.asarray(v) for name, v in inputs.items()}
    laid = {
        "x": a["L0_attn_x"], "wv": a["L0_attn_wv"], "bv": a["L0_attn_bv"], "woT": a["L0_attn_wo"].T,
        "bo": a["L0_attn_bo"], "w3dT": a["L0_attn_w3d"].T, "b3d": a["L0_attn_b3d"],
        "gateT": a["L0_ffn_gate_w"].T, "gate_bias": a["L0_ffn_gate_bias"],
        "wT": _np.concatenate([a[f"L0_ffn_{w}"].transpose(0, 2, 1) for w in ("w1", "w3", "w2")], axis=2),
        "sw13T": _np.concatenate([a["L0_ffn_sw1"].T, a["L0_ffn_sw3"].T], axis=1),
        "sw2T": a["L0_ffn_sw2"].T,
    }
    nc = _bacc.Bacc("TRN2", target_bir_lowering=False, num_devices=1)
    arrays, args = {}, []
    for name, v in laid.items():
        arrays[f"in_{name}_dram"] = v = _np.ascontiguousarray(v)
        args.append(nc.dram_tensor(f"in_{name}_dram", v.shape, _mybir.dt.from_np(v.dtype), kind="ExternalInput").ap())
    args.append(nc.dram_tensor("out_0_dram", (NB, S, D), f32, kind="ExternalOutput").ap())
    attention_and_experts(nc, *args)
    r = _run(nc, [arrays], core_ids=[0])
    return r.results[0]["out_0_dram"]
```

```python
import concourse.bass as bass
from concourse import mybir
from contextlib import ExitStack

P = 128
NB, S, D = 2, 2048, 256
NT = NB * S // P
TB = S // P
GT = 4
GB = TB // GT
KC = D // P
MW = D + 4
VW = 2 * D + 2
TRI = sum(S - P * k for k in range(TB))
KR = 32
NQ = 4
N_POS = 48
NE = 4
NG = NT // GT
NX, TOPK = 8, 2
NS = 512
MC = NS // P
NSLOT = NT * TOPK + NX
N_CHOSEN = 18
N_FULL = (NSLOT - 3) // 4 * 4
H = 16
SCALE = 1.0 / (D // H) ** 0.5
EPS = 1e-5
f32 = mybir.dt.float32
f32r = mybir.dt.float32r
bf16 = mybir.dt.bfloat16
i32 = mybir.dt.int32
u32 = mybir.dt.uint32
ALU = mybir.AluOpType
ACT = mybir.ActivationFunctionType
AX = mybir.AxisListType


def flat(ap):
    return ap.rearrange("p a n -> p (a n)")


def tile_of(T, i):
    return flat(T[:, bass.ds(i, 1), :])



def attention_and_experts(nc, x, wv, bv, woT, bo, w3dT, b3d, gateT, gate_bias, wT, sw13T, sw2T, out):
    x_v = x.rearrange("b (t p) d -> p (b t) d", p=P)
    out_v = out.rearrange("b (t p) d -> p (b t) d", p=P)
    xs = nc.dram_tensor("slots_in", (NSLOT * P, D), f32, kind="Internal").ap()
    ys = nc.dram_tensor("slots_out", (NSLOT * P, D), f32, kind="Internal").ap()
    xs_p = xs.rearrange("(p i) d -> p i d", p=P)
    xs_t = xs.rearrange("(i p) d -> i p d", p=P)
    ys_t = ys.rearrange("(i p) d -> i p d", p=P)
    outer = ExitStack()
    X = outer.enter_context(nc.sbuf_tensor("X", [P, NT, D], f32))
    st1 = outer.enter_context(nc.sbuf_tensor("st1", [P, NT, 6], f32))

    with ExitStack() as ctx:
        def sb(name, shape, dt=f32):
            return ctx.enter_context(nc.sbuf_tensor(name, shape, dt))

        def sem(name):
            return ctx.enter_context(nc.semaphore(name))

        wv_raw = sb("wv_raw", [P, KC, D])
        woT_raw = sb("woT_raw", [P, KC, D])
        M_raw = sb("M_raw", [P, KC, MW])
        M_hi = sb("M_hi", [P, KC, MW], f32r)
        M_lo = sb("M_lo", [P, KC, MW], f32r)
        bv_col = sb("bv_col", [P, KC])
        c_raw = sb("c_raw", [1, MW])
        c_hi = sb("c_hi", [1, MW], f32r)
        c_lo = sb("c_lo", [1, MW], f32r)
        bo_row = sb("bo_row", [1, D])
        one_f = sb("one_f", [1, P])
        one_row = sb("one_row", [1, P], f32r)
        ident = sb("ident", [P, P])
        eps_col = sb("eps_col", [P, 1])
        zero = sb("zero", [P, D])
        one_zero = sb("one_zero", [P, TB, 2])
        st = sb("st", [P, TB, 6])
        mv = sb("mv", [P, TB, 2])
        std = sb("std", [P, TB])
        rstd = sb("rstd", [P, TB])
        XT_hi = sb("XT_hi", [P, KC, GT * P], f32r)
        XT_lo = sb("XT_lo", [P, KC, GT * P], f32r)
        VO = sb("VO", [P, TB, VW], f32r)
        pos = sb("pos", [P, TB, 3])
        pmax = sb("pmax", [P, 1])
        pmax_row = sb("pmax_row", [1, 1])
        pbits = sb("pbits", [P, 1], i32)
        magic = sb("magic", [P, 1])
        hsum = sb("hsum", [P, TB, 3])
        h = sb("h", [P, TB, 3])
        l = sb("l", [P, TB, 3])
        lh = sb("lh", [P, TB, 3], f32r)
        t3 = sb("t3", [P, TB, 3])
        t3b = sb("t3b", [P, TB, 3])
        nrm = sb("nrm", [P, 2, TB])
        nrm_hi = sb("nrm_hi", [P, 2, TB], f32r)
        QT = sb("QT", [2 * KR, S], f32r)
        KTh = sb("KTh", [2 * KR, S], f32r)
        KTl = sb("KTl", [2 * KR, S], f32r)
        E = sb("E", [P, TRI])
        rden = sb("rden", [P, GT])
        st_x = sb("st_x", [P, GT, 6])
        with ExitStack() as first:
            def early(name, shape):
                return first.enter_context(nc.sbuf_tensor(name, shape, f32))
            XN = early("XN", [P, 2, GT, D])
            FQ = early("FQ", [P, TB, 2 * KR])
            FKh = early("FKh", [P, TB, 2 * KR])
            FKl = early("FKl", [P, TB, 2 * KR])
        E_hi = sb("E_hi", [P, NE, 512], f32r)
        E_lo = sb("E_lo", [P, NE, 512], f32r)

        bank = [ctx.enter_context(nc.psum_tensor(f"a_bank{i}", [P, 512], f32)) for i in range(8)]
        T_ps, V_ps, O_ps = bank[0:2], bank[2:4], bank[4:8]
        Q_ps = bank[0:4]

        s_x = sem("s_x")
        s_zero = sem("s_zero")
        s_w = sem("s_w")
        s_const = sem("s_const")
        s_cps = sem("s_cps")
        s_craw = sem("s_craw")
        s_chi = sem("s_chi")
        s_M = sem("s_M")
        s_st = sem("s_st")
        s_mv = sem("s_mv")
        s_std = sem("s_std")
        s_rstd = sem("s_rstd")
        s_xn = sem("s_xn")
        s_T = sem("s_T")
        s_xth = sem("s_xth")
        s_xtl = sem("s_xtl")
        s_vps = [sem(f"s_vps{i}") for i in range(2)]
        s_voh = sem("s_voh")
        s_pos = sem("s_pos")
        s_vol = sem("s_vol")
        s_f = sem("s_f")
        s_pt = sem("s_pt")
        s_ft = sem("s_ft")
        s_fr = sem("s_fr")
        s_q = sem("s_q")
        s_e2 = sem("s_e2")
        s_diag = sem("s_diag")
        s_dist = sem("s_dist")
        s_exp = sem("s_exp")
        s_eh = sem("s_eh")
        s_el = sem("s_el")
        s_eb = sem("s_eb")
        s_acc = sem("s_acc")
        s_rd = sem("s_rd")
        s_x1 = sem("s_x1")
        s_st1 = sem("s_st1")

        block = ctx.enter_context(nc.Block())

        def off(kt):
            return sum(S - P * k for k in range(kt))

        def block_of(Q, kt):
            q0 = max(P * kt, GT * P * Q)
            w = GT * P * (Q + 1) - q0
            at = off(kt) + q0 - P * kt
            return E[:, at:at + w], q0, w

        blocks = [(Q, kt) for Q in range(GB) for kt in range(GT * Q + GT)]
        NBLK = len(blocks)
        sq_blocks = [(Q, kt) for kt in range(TB) for Q in range(kt // GT, GB)]
        row_done = {kt: n + 1 for n, (Q, kt) in enumerate(sq_blocks)}
        first_block = {kt: n + 1 for n, (Q, kt) in reversed(list(enumerate(sq_blocks)))}

        @block.sync
        def _(sp):
            for b in range(NB):
                for g in range(GB):
                    n = b * GB + g
                    sp.dma_start(X[:, n * GT:(n + 1) * GT, :], x_v[:, n * GT:(n + 1) * GT, :]).then_inc(s_x, 16)
                sp.wait_ge(s_x, 64 * (b + 1))
            sp.wait_ge(s_const, 9)
            for i in range(8):
                w = NSLOT // 8
                sp.dma_start(xs_p[:, i * w:(i + 1) * w, :], zero[:, :].unsqueeze(1).to_broadcast([P, w, D]))\
                  .then_inc(s_zero, 16)
            sp.wait_ge(s_zero, 128)

        @block.gpsimd
        def _(pool):
            pool.memset(ident[:, :], 0.0).then_inc(s_const, 1)
            pool.memset(one_f[:, :], 1.0).then_inc(s_const, 1)
            pool.memset(eps_col[:, :], EPS).then_inc(s_const, 1)
            pool.memset(M_raw[:, :, D + 3:MW], 0.0).then_inc(s_const, 1)
            pool.memset(c_raw[:, D + 3:MW], 0.0).then_inc(s_const, 1)
            pool.memset(one_zero[:, :, 0], 1.0).then_inc(s_const, 1)
            pool.memset(one_zero[:, :, 1], 0.0).then_inc(s_const, 1)
            pool.memset(zero[:, :], 0.0).then_inc(s_const, 1)
            pool.wait_ge(s_const, 8)
            pool.affine_select(out=ident[:, :], in_=ident[:, :], compare_op=ALU.not_equal, fill=1.0, base=0,
                               pattern=[[-1, P]], channel_multiplier=1).then_inc(s_const, 1)
            for b in range(NB):
                for kt in range(TB):
                    blk = E[:, off(kt):off(kt) + P]
                    pool.wait_ge(s_e2, b * NBLK + first_block[kt] + NQ)
                    pool.affine_select(out=blk, in_=blk, compare_op=ALU.is_ge, fill=1.0e30, base=0,
                                       pattern=[[1, P]], channel_multiplier=-1).then_inc(s_diag, 1)
                    pool.wait_ge(s_diag, 2 * (b * TB + kt) + 1)
                    pool.affine_select(out=blk, in_=blk, compare_op=ALU.not_equal, fill=0.0, base=0,
                                       pattern=[[1, P]], channel_multiplier=-1).then_inc(s_diag, 1)

        @block.scalar
        def _(act):
            act.dma_start(wv_raw[:, :, :], wv.rearrange("(c p) n -> p c n", c=KC)).then_inc(s_w, 16)
            act.dma_start(woT_raw[:, :, :], woT.rearrange("(c p) n -> p c n", c=KC)).then_inc(s_w, 16)
            act.dma_start(bv_col[:, :], bv.rearrange("(c p) -> p c", c=KC), allow_slow_non_contiguous=True)\
               .then_inc(s_w, 16)
            act.dma_start(bo_row[:, :], bo.rearrange("(a n) -> a n", a=1)).then_inc(s_w, 16)
            act.dma_start(M_raw[:, :, D:D + 3], w3dT.rearrange("(c p) n -> p c n", c=KC)).then_inc(s_w, 16)
            act.dma_start(c_raw[:, D:D + 3], b3d.rearrange("(a n) -> a n", a=1)).then_inc(s_w, 16)
            act.wait_ge(s_const, 9)
            with act.Fori(0, NB) as b:
                act.wait_ge(s_mv, TB * b + TB)
                act.activation(std[:, :], mv[:, :, 1], ACT.Sqrt, bias=eps_col[:, 0:1]).then_inc(s_std, 1)
                with act.Fori(0, GB) as g:
                    G = b * GB + g
                    for c in range(KC):
                        act.wait_ge(s_T, 2 * G + c + 1)
                        act.activation(XT_hi[:, c, :], T_ps[c][:, :], ACT.Copy).then_inc(s_xth, 1)
                    for j in range(GT):
                        act.wait_ge(s_vps[j % 2], 2 * G + j // 2 + 1)
                        act.activation(flat(VO[:, bass.ds(g * GT + j, 1), 0:D]), V_ps[j % 2][:, 0:D], ACT.Copy)\
                           .then_inc(s_voh, 1)
                for g in range(GB):
                    for k, dst in enumerate((QT, KTh, KTl)):
                        n = 3 * g + k
                        act.wait_ge(s_ft, 3 * GB * b + n + 1)
                        act.activation(dst[:, g * 512:(g + 1) * 512], Q_ps[n % 4][0:2 * KR, :], ACT.Copy)\
                           .then_inc(s_fr, 1)
                for kt in range(TB):
                    row = E[:, off(kt):off(kt) + S - P * kt]
                    act.wait_ge(s_e2, b * NBLK + row_done[kt] + NQ)
                    act.wait_ge(s_diag, 2 * (b * TB + kt) + 2)
                    act.activation(row, row, ACT.Sqrt).then_inc(s_dist, 1)
                for n, (Q, kt) in enumerate(blocks):
                    blk, _, w = block_of(Q, kt)
                    if n < TB:
                        act.wait_ge(s_dist, b * TB + TB)
                    act.activation(blk, blk, ACT.Exp, scale=-SCALE).then_inc(s_exp, 1)

        @block.vector
        def _(dve):
            nc.disable_value_cache = True
            dve.sem_inc(s_xtl, 2)
            dve.sem_inc(s_vol, 2)
            dve.sem_inc(s_e2, NQ)
            dve.sem_inc(s_x1, GT)
            dve.wait_ge(s_w, 96)
            dve.wait_ge(s_const, 9)
            dve.wait_ge(s_cps, 1)
            for c in range(KC):
                dve.tensor_copy(M_raw[:, c, 0:D], V_ps[c][:, 0:D]).then_inc(s_craw, 1)
            dve.tensor_tensor(c_raw[:, 0:D], T_ps[0][0:1, 0:D], bo_row[:, :], ALU.add).then_inc(s_craw, 1)
            dve.wait_ge(s_craw, 3)
            dve.tensor_copy(M_hi[:, :, :], M_raw[:, :, :]).then_inc(s_chi, 1)
            dve.tensor_copy(c_hi[:, :], c_raw[:, :]).then_inc(s_chi, 1)
            dve.tensor_copy(one_row[:, :], one_f[:, :]).then_inc(s_M, 1)
            dve.tensor_copy(VO[:, :, D:D + 2], one_zero[:, :, :]).then_inc(s_M, 1)
            dve.wait_ge(s_chi, 2)
            dve.tensor_tensor(M_lo[:, :, :], M_raw[:, :, :], M_hi[:, :, :].bitcast(f32), ALU.subtract).then_inc(s_M, 1)
            dve.tensor_tensor(c_lo[:, :], c_raw[:, :], c_hi[:, :].bitcast(f32), ALU.subtract).then_inc(s_M, 1)
            with dve.Fori(0, NB) as b:
                dve.wait_ge(s_x, 64 * b + 64)
                for t in range(TB + 1):
                    if t >= 1:
                        dve.wait_ge(s_st, b * TB + t)
                    if t < TB:
                        dve.bn_stats(st[:, t, :], tile_of(X, b * TB + t)).then_inc(s_st, 1)
                    else:
                        dve.tensor_copy(rden[:, 0:1], eps_col[:, :])
                    if t >= 1:
                        dve.bn_aggr(mv[:, t - 1, :], st[:, t - 1, :]).then_inc(s_mv, 1)
                dve.wait_ge(s_std, b + 1)
                dve.reciprocal(rstd[:, :], std[:, :]).then_inc(s_rstd, 1)

                def normalise(g, v):
                    dve.wait_ge(s_rstd, b + 1)
                    dve.wait_ge(s_mv, TB * b + TB)
                    for j in range(GT):
                        t = g * GT + j
                        dve.tensor_scalar(XN[:, v, j, :], tile_of(X, b * TB + t), mv[:, t, 0:1], rstd[:, t:t + 1],
                                          ALU.subtract, ALU.mult).then_inc(s_xn, 1)

                normalise(0, 0)
                for g in range(GB):
                    G = b * GB + g
                    for c in range(KC):
                        dve.wait_ge(s_xth, 2 * G + c + 1)
                        dve.tensor_tensor(XT_lo[:, c, :], T_ps[c][:, :], XT_hi[:, c, :].bitcast(f32),
                                          ALU.subtract).then_inc(s_xtl, 1)
                    if g + 1 < GB:
                        normalise(g + 1, (g + 1) % 2)
                    for j in range(GT):
                        t = g * GT + j
                        dve.wait_ge(s_voh, GT * G + j + 1)
                        dve.tensor_copy(pos[:, t, :], V_ps[j % 2][:, D:D + 3]).then_inc(s_pos, 1)
                        dve.tensor_tensor(VO[:, t, D + 2:VW], V_ps[j % 2][:, 0:D], VO[:, t, 0:D].bitcast(f32),
                                          ALU.subtract).then_inc(s_vol, 1)

                step = [0]

                def done(ins):
                    step[0] += 1
                    ins.then_inc(s_f, 1)
                    dve.wait_ge(s_f, N_POS * b + step[0])

                def thrice(ap):
                    return ap.unsqueeze(2).to_broadcast([P, TB, 3])

                dve.wait_ge(s_pos, TB * b + TB)
                done(dve.tensor_reduce(pmax[:, :], pos[:, :, :].rearrange("p t c -> p (t c)"), AX.X, ALU.max,
                                       apply_absolute_value=True))
                dve.wait_ge(s_pt, 2 * b + 1)
                done(dve.tensor_reduce(pmax_row[:, :], T_ps[0][0:1, 0:P], AX.X, ALU.max))
                dve.wait_ge(s_pt, 2 * b + 2)
                done(dve.tensor_copy(pmax[:, :], T_ps[1][:, 0:1]))
                done(dve.tensor_scalar(pbits[:, :], pmax[:, :].bitcast(i32), 0x7F800000, None, ALU.bitwise_and))
                done(dve.tensor_scalar(magic[:, :], pbits[:, :].bitcast(f32), 1.5 * 2.0 ** 14, None, ALU.mult))
                done(dve.tensor_scalar(hsum[:, :, :], pos[:, :, :], magic[:, 0:1], None, ALU.add))
                done(dve.tensor_scalar(h[:, :, :], hsum[:, :, :], magic[:, 0:1], None, ALU.subtract))
                done(dve.tensor_tensor(l[:, :, :], pos[:, :, :], h[:, :, :], ALU.subtract))
                done(dve.tensor_copy(lh[:, :, :], l[:, :, :]))
                done(dve.tensor_tensor(t3[:, :, :], h[:, :, :], h[:, :, :], ALU.mult))
                done(dve.tensor_reduce(nrm[:, 0, :], t3[:, :, :], AX.X, ALU.add))
                done(dve.scalar_tensor_tensor(out=t3b[:, :, :], in0=h[:, :, :], scalar=2.0, in1=l[:, :, :],
                                              op0=ALU.mult, op1=ALU.add))
                done(dve.tensor_tensor(t3b[:, :, :], t3b[:, :, :], l[:, :, :], ALU.mult))
                done(dve.tensor_reduce(nrm[:, 1, :], t3b[:, :, :], AX.X, ALU.add))
                done(dve.tensor_copy(nrm_hi[:, :, :], nrm[:, :, :]))
                lhf = lh[:, :, :].bitcast(f32)
                for F in (FQ, FKh, FKl):
                    done(dve.memset(F[:, :, :], 0.0))
                done(dve.tensor_copy(FQ[:, :, 0:3], h[:, :, :]))
                done(dve.memset(FQ[:, :, 3:5], 1.0))
                done(dve.memset(FQ[:, :, KR + 24:KR + 26], 1.0))
                done(dve.memset(FKh[:, :, 5:7], 1.0))
                done(dve.memset(FKl[:, :, KR + 26:KR + 28], 1.0))
                for k, (F, at) in enumerate(((FQ, 5), (FQ, KR + 26), (FKh, 3), (FKl, KR + 24))):
                    done(dve.tensor_copy(F[:, :, at], nrm_hi[:, k % 2, :].bitcast(f32)))
                    done(dve.tensor_tensor(F[:, :, at + 1], nrm[:, k % 2, :], nrm_hi[:, k % 2, :].bitcast(f32),
                                           ALU.subtract))
                done(dve.tensor_copy(FQ[:, :, KR:KR + 3], lhf))
                done(dve.tensor_tensor(FQ[:, :, KR + 3:KR + 6], l[:, :, :], lhf, ALU.subtract))
                ll = FQ[:, :, KR + 3:KR + 6]
                for k, src in ((6, h[:, :, :]), (9, h[:, :, :]), (12, lhf), (15, lhf), (18, ll), (21, ll)):
                    done(dve.tensor_copy(FQ[:, :, KR + k:KR + k + 3], src))
                done(dve.tensor_scalar(FKh[:, :, 0:3], h[:, :, :], -2.0, None, ALU.mult))
                for k, src in ((0, h[:, :, :]), (3, h[:, :, :]), (6, lhf), (9, ll), (12, lhf), (15, ll), (18, lhf),
                               (21, ll)):
                    done(dve.tensor_scalar(FKl[:, :, KR + k:KR + k + 3], src, -2.0, None, ALU.mult))
                assert step[0] == N_POS

                for n, (Q, kt) in enumerate(sq_blocks):
                    blk, _, w = block_of(Q, kt)
                    dve.wait_ge(s_q, b * NBLK + n + 1)
                    dve.tensor_scalar(blk, Q_ps[n % NQ][:, 0:w], 0.0, None, ALU.max).then_inc(s_e2, 1)

                def finish(Q, j):
                    t = b * TB + GT * Q + j
                    n = GT * Q + j
                    if j < GT - 1:
                        dve.wait_ge(s_acc, b * (GT - 1) * GB + (GT - 1) * Q + j + 1)
                    else:
                        dve.wait_ge(s_eb, b * NBLK + blocks.index((Q, GT * Q + j)) + 1 + NE)
                    dve.reciprocal(rden[:, j:j + 1], O_ps[j][:, D:D + 1]).then_inc(s_rd, 1)
                    dve.wait_ge(s_rd, b * TB + n + 1)
                    dve.scalar_tensor_tensor(out=tile_of(X, t), in0=O_ps[j][:, 0:D], scalar=rden[:, j:j + 1],
                                             in1=tile_of(X, t), op0=ALU.mult, op1=ALU.add).then_inc(s_x1, 1)
                    dve.wait_ge(s_x1, t + 1 + GT)
                    dve.bn_stats(tile_of(st1, t), tile_of(X, t)).then_inc(s_st1, 1)

                def split_hi(n):
                    blk, _, w = block_of(*blocks[n])
                    dve.wait_ge(s_exp, b * NBLK + n + 1)
                    dve.wait_ge(s_eb, b * NBLK + n + 1)
                    dve.tensor_copy(E_hi[:, n % NE, 0:w], blk).then_inc(s_eh, 1)

                def split_lo(n):
                    blk, _, w = block_of(*blocks[n])
                    dve.wait_ge(s_eh, b * NBLK + n + 1)
                    dve.tensor_tensor(E_lo[:, n % NE, 0:w], blk, E_hi[:, n % NE, 0:w].bitcast(f32),
                                      ALU.subtract).then_inc(s_el, 1)

                split_hi(0)
                for n, (Q, kt) in enumerate(blocks):
                    if n + 1 < NBLK:
                        split_hi(n + 1)
                    split_lo(n)
                    if Q > 0 and kt < GT - 1:
                        finish(Q - 1, kt)
                        if kt == GT - 2:
                            finish(Q - 1, kt + 1)
                for j in range(GT):
                    finish(GB - 1, j)
            nc.disable_value_cache = False

        @block.tensor
        def _(pe):
            pe.sem_inc(s_eb, NE)
            pe.wait_ge(s_w, 96)
            for ci in range(KC):
                for cd in range(KC):
                    pe.matmul(V_ps[ci][:, 0:D], wv_raw[:, cd, ci * P:(ci + 1) * P], woT_raw[:, cd, :],
                              start=(cd == 0), stop=(cd == KC - 1))
            for cd in range(KC):
                mm = pe.matmul(T_ps[0][0:1, 0:D], bv_col[:, cd:cd + 1], woT_raw[:, cd, :],
                               start=(cd == 0), stop=(cd == KC - 1))
            mm.then_inc(s_cps, 1)
            pe.wait_ge(s_const, 9)
            pe.wait_ge(s_M, 4)
            with pe.Fori(0, NB) as b:
                for g in range(GB):
                    G = b * GB + g
                    v = g % 2
                    pe.wait_ge(s_xn, GT * G + GT)
                    for c in range(KC):
                        pe.wait_ge(s_xtl, 2 * G + c + 1)
                        for j in range(GT):
                            mm = pe.transpose(T_ps[c][:, j * P:(j + 1) * P], XN[:, v, j, c * P:(c + 1) * P],
                                              ident[:, :])
                        mm.then_inc(s_T, 1)
                    pe.wait_ge(s_xtl, 2 * G + 4)
                    for j in range(GT):
                        pe.wait_ge(s_vol, GT * G + j + 1)
                        tok = slice(j * P, (j + 1) * P)
                        out = V_ps[j % 2][:, 0:MW]
                        for c in range(KC):
                            pe.matmul(out, XT_hi[:, c, tok], M_hi[:, c, :], start=(c == 0), stop=False)
                            pe.matmul(out, XT_hi[:, c, tok], M_lo[:, c, :], start=False, stop=False)
                            pe.matmul(out, XT_lo[:, c, tok], M_hi[:, c, :], start=False, stop=False)
                        pe.matmul(out, one_row[:, :], c_hi[:, :], start=False, stop=False)
                        pe.matmul(out, one_row[:, :], c_lo[:, :], start=False, stop=True).then_inc(s_vps[j % 2], 1)
                pe.wait_ge(s_f, N_POS * b + 1)
                pe.wait_ge(s_vol, GT * GB * b + GT * GB + 2)
                pe.transpose(T_ps[0][0:1, 0:P], pmax[:, :], ident[:, :]).then_inc(s_pt, 1)
                pe.wait_ge(s_f, N_POS * b + 2)
                pe.matmul(T_ps[1][:, 0:1], one_f[:, :], pmax_row[:, :], start=True, stop=True).then_inc(s_pt, 1)
                pe.wait_ge(s_f, N_POS * b + N_POS)
                for g in range(GB):
                    for k, F in enumerate((FQ, FKh, FKl)):
                        n = 3 * g + k
                        if n >= 4:
                            pe.wait_ge(s_fr, 3 * GB * b + n - 3)
                        pe.transpose(Q_ps[n % 4][:, 0:P], ident[:, :], ident[:, :])
                        for j in range(GT):
                            mm = pe.transpose(Q_ps[n % 4][0:2 * KR, j * P:(j + 1) * P], F[:, g * GT + j, :],
                                              ident[:, :])
                        mm.then_inc(s_ft, 1)
                pe.wait_ge(s_fr, 3 * GB * b + 3 * GB)
                for n, (Q, kt) in enumerate(sq_blocks):
                    _, q0, w = block_of(Q, kt)
                    pe.wait_ge(s_e2, b * NBLK + n + 1)
                    key = slice(kt * P, (kt + 1) * P)
                    pe.matmul(Q_ps[n % NQ][:, 0:w], KTh[:, key], QT[:, q0:q0 + w], start=True, stop=False)
                    pe.matmul(Q_ps[n % NQ][:, 0:w], KTl[:, key], QT[:, q0:q0 + w], start=False, stop=True)\
                      .then_inc(s_q, 1)
                for n, (Q, kt) in enumerate(blocks):
                    pe.wait_ge(s_el, b * NBLK + n + 1)
                    q0 = max(kt, GT * Q)
                    for qt in range(q0, GT * Q + GT):
                        j = qt - GT * Q
                        if kt == 0:
                            pe.wait_ge(s_x1, b * TB + GT * Q + j + 1)
                        cols = slice((qt - q0) * P, (qt - q0 + 1) * P)
                        pe.matmul(O_ps[j][:, 0:D + 2], E_hi[:, n % NE, cols], VO[:, kt, 0:D + 2],
                                  start=(kt == 0), stop=False)
                        pe.matmul(O_ps[j][:, 0:D], E_hi[:, n % NE, cols], VO[:, kt, D + 2:VW], start=False, stop=False)
                        mm = pe.matmul(O_ps[j][:, 0:D + 2], E_lo[:, n % NE, cols], VO[:, kt, 0:D + 2],
                                       start=False, stop=(kt == qt))
                        if kt == qt and j < GT - 1:
                            mm.then_inc(s_acc, 1)
                    mm.then_inc(s_eb, 1)

    with ExitStack() as ctx:
        def sb(name, shape, dt=f32):
            return ctx.enter_context(nc.sbuf_tensor(name, shape, dt))

        def sem(name):
            return ctx.enter_context(nc.semaphore(name))

        ident = sb("ident2", [P, P])
        eps_col = sb("eps_col2", [P, 1])
        mv = sb("mv2", [P, NT, 2])
        std = sb("std2", [P, NT])
        rstd = sb("rstd2", [P, NT])
        gate_raw = sb("gate_raw", [P, KC, NX])
        gate_hi = sb("gate_hi", [P, KC, NX], f32r)
        gate_lo = sb("gate_lo", [P, KC, NX], f32r)
        gbias = sb("gbias", [P, NX])
        logit = sb("logit", [P, NT, NX])
        score = sb("score", [P, NT, NX])
        pick = [sb(f"pick{k}", [P, NT, NX]) for k in range(TOPK)]
        tmp = sb("tmp", [P, NT, NX])
        chosen = sb("chosen", [P, NT, NX], bf16)
        red = sb("red", [P, NT])
        red2 = sb("red2", [P, NT])
        weight = [sb(f"weight{k}", [P, NT]) for k in range(TOPK)]
        slot = [sb(f"slot{k}", [P, NT], u32) for k in range(TOPK)]
        rank = sb("rank", [P, NX])
        before = sb("before", [P, P], bf16)
        ones_b = sb("ones_b", [P, P], bf16)
        one8 = sb("one8", [P, NX])
        n_i = sb("n_i", [P, NX], i32)
        n_j = sb("n_j", [P, NX], i32)
        n_f = sb("n_f", [P, NX])
        ends = sb("ends", [P, NX])
        base = sb("base", [P, NX])
        tile_id = sb("tile_id", [P, NSLOT])
        which = sb("which", [P, NSLOT])
        expert = sb("expert", [P, NSLOT], i32)

        def whole_and_low(name, shape):
            with nc.sbuf_tensor(name + "_raw", shape, f32) as raw:
                pass
            return raw, sb(name + "_lo", shape, f32r)

        sw13_hi = sb("sw13_hi", [P, KC, 2 * NS], f32r)
        sw13_raw, sw13_lo = whole_and_low("sw13", [P, KC, 2 * NS])
        sw2_hi = sb("sw2_hi", [P, MC, D], f32r)
        sw2_raw, sw2_lo = whole_and_low("sw2", [P, MC, D])
        W_hi = sb("W_hi", [P, KC, NX, 3 * D], f32r)
        W_raw, W_lo = whole_and_low("W", [P, KC, NX, 3 * D])
        with ExitStack() as first:
            def early(name, shape, dt=f32):
                return first.enter_context(nc.sbuf_tensor(name, shape, dt))
            biased = early("biased", [P, NT, NX])
            slot_e = early("slot_e", [P, NT, NX])
            total = early("total", [P, NX, NT])
            upto = early("upto", [P, NX, NT])
            keep = early("keep", [P, NX, NT])
            passed = early("passed", [P, NSLOT, NX])
        YG = sb("YG", [P, 4, TOPK, D])
        XR = YG[:, :, 0, :]
        with ExitStack() as first:
            XN = early("XN2", [P, 2, GT, D])
            sg = early("sg", [P, 2, GT * P])
            lgT = sg
            h_hi = early("h_hi", [P, 2, GT * P], f32r)
            with nc.sbuf_tensor("hf", [P, 2, GT * P], f32) as hf:
                pass
            h_lo = early("h_lo", [P, 2, GT * P], f32r)
            XT_hi = early("XT2_hi", [P, 2, KC, GT * P], f32r)
            XT_lo = early("XT2_lo", [P, 2, KC, GT * P], f32r)
        XS = sb("XS", [P, 4, D])
        YS = sb("YS", [P, 2, D])
        sr = sb("sr", [P, 2, D])
        hr = sb("hr", [P, 2, D])
        hT_hi = sb("hT_hi", [P, 2, KC, P], f32r)
        hT_lo = sb("hT_lo", [P, 2, KC, P], f32r)
        XST_hi = sb("XST_hi", [P, 2, KC, P], f32r)
        XST_lo = sb("XST_lo", [P, 2, KC, P], f32r)
        sb("rest", [P, 9, 512])

        bank = [ctx.enter_context(nc.psum_tensor(f"bank{i}", [P, 512], f32)) for i in range(8)]
        TL_ps, L_ps, LT_ps, C_ps = (bank[0:2], bank[2:4]), bank[4:6], bank[6:8], bank[6:8]
        T_ps, G_ps, U_ps, Z_ps = bank[0:2], bank[2:4], bank[4:6], bank[6:8]
        XT_ps, S_ps, HT_ps, Y_ps = bank[0:2], bank[2:4], bank[4:6], bank[6:8]

        s_const = sem("f_const")
        s_gate = sem("f_gate")
        s_w = sem("f_w")
        s_whi = sem("f_whi")
        s_wlo = sem("f_wlo")
        s_mv = sem("f_mv")
        s_std = sem("f_std")
        s_rstd = sem("f_rstd")
        s_xn = sem("f_xn")
        s_T = sem("f_T")
        s_xth = sem("f_xth")
        s_xtl = sem("f_xtl")
        s_lps = sem("f_lps")
        s_lc = sem("f_lc")
        s_lt = sem("f_lt")
        s_lg = sem("f_lg")
        s_g = sem("f_g")
        s_u = sem("f_u")
        s_sg = sem("f_sg")
        s_hf = sem("f_hf")
        s_hh = sem("f_hh")
        s_hl = sem("f_hl")
        s_hu = sem("f_hu")
        s_z = sem("f_z")
        s_zf = sem("f_zf")
        s_r = sem("f_r")
        s_ex = sem("f_ex")
        s_cnt = sem("f_cnt")
        s_slot = sem("f_slot")
        s_xr = sem("f_xr")
        s_sc = [sem(f"f_sc{i}") for i in range(4)]
        s_wr = sem("f_wr")
        s_wrh = sem("f_wrh")
        s_wrl = sem("f_wrl")
        s_xs = [sem(f"f_xs{i}") for i in range(4)]
        s_xsT = sem("f_xsT")
        s_xsh = sem("f_xsh")
        s_xsl = sem("f_xsl")
        s_s1 = sem("f_s1")
        s_sr = sem("f_sr")
        s_hr = sem("f_hr")
        s_hT = sem("f_hT")
        s_hTh = sem("f_hTh")
        s_hTl = sem("f_hTl")
        s_s2 = sem("f_s2")
        s_ys = sem("f_ys")
        s_yst = [sem(f"f_yst{i}") for i in range(2)]
        s_yg = [sem(f"f_yg{i}") for i in range(4)]
        s_y = sem("f_y")
        s_out = sem("f_out")

        N_XN, N_T, N_XTL = NT, KC * NG, KC * NG + 2 * KC
        HALF = NG // 2

        def tiles_to_scatter(n):
            return range(2 * n + 2, min(2 * n + 4, NT))

        def tiles_to_add(n):
            c = n - MC * HALF
            return range(max(2 * c - 4, 0), max(2 * c - 2, 0))

        block = ctx.enter_context(nc.Block())

        @block.sync
        def _(sp):
            sp.dma_start(gate_raw[:, :, :], gateT.rearrange("(c p) n -> p c n", p=P)).then_inc(s_gate, 16)
            sp.dma_start(gbias[:, :], gate_bias.rearrange("(a n) -> a n", a=1).to_broadcast([P, NX]))\
              .then_inc(s_gate, 16)
            sp.dma_start(sw13_raw[:, :, :], sw13T.rearrange("(c p) n -> p c n", p=P)).then_inc(s_w, 16)
            sp.dma_start(sw2_raw[:, :, :], sw2T.rearrange("(c p) n -> p c n", p=P)).then_inc(s_w, 16)
            for e in range(NX):
                sp.dma_start(W_raw[:, :, e, :], wT[e, :, :].rearrange("(c p) n -> p c n", p=P))\
                  .then_inc(s_wr, 16)
            sp.wait_ge(s_T, N_T + KC * HALF)
            for k in range(4):
                sp.wait_ge(s_sc[k], 16 * TOPK * NT // 4)
            for k in range(4):
                sp.dma_start(XS[:, k, :], xs_t[k, :, :]).then_inc(s_xs[k], 16)
            for i in range(-3, NSLOT):
                if i + 7 < NSLOT:
                    sp.wait_ge(s_xsT, i + 4)
                    sp.dma_start(XS[:, (i + 3) % 4, :], xs_t[i + 7, :, :]).then_inc(s_xs[(i + 3) % 4], 16)
                if i < 0:
                    continue
                sp.wait_ge(s_ys, i + 3)
                sp.dma_start(ys_t[i, :, :], YS[:, i % 2, :]).then_inc(s_yst[i % 2], 16)
            for t in range(NT):
                sp.wait_ge(s_y, TOPK * t + TOPK)
                sp.dma_start(out_v[:, t, :], X[:, t, :]).then_inc(s_out, 16)
            sp.wait_ge(s_out, 16 * NT)

        @block.gpsimd
        def _(pool):
            def const(ins):
                ins.then_inc(s_const, 1)
            const(pool.memset(ident[:, :], 0.0))
            const(pool.memset(before[:, :], 1.0))
            const(pool.memset(ones_b[:, :], 1.0))
            const(pool.memset(eps_col[:, :], EPS))
            const(pool.memset(one8[:, :], 1.0))
            const(pool.memset(keep[:, :, 1:NT], 1.0))
            const(pool.memset(keep[:, :, 0:1], 0.0))
            const(pool.iota(rank[:, :], pattern=[[-1, NX]], base=NX, channel_multiplier=0,
                            allow_small_or_imprecise_dtypes=True))
            const(pool.iota(tile_id[:, :], pattern=[[1, NSLOT]], base=0, channel_multiplier=0,
                            allow_small_or_imprecise_dtypes=True))
            pool.wait_ge(s_const, 9)
            const(pool.affine_select(out=ident[:, :], in_=ident[:, :], compare_op=ALU.not_equal, fill=1.0, base=0,
                                     pattern=[[-1, P]], channel_multiplier=1))
            const(pool.affine_select(out=before[:, :], in_=before[:, :], compare_op=ALU.is_gt, fill=0.0, base=0,
                                     pattern=[[1, P]], channel_multiplier=-1))
            pool.wait_ge(s_slot, 1)
            for t in range(NT):
                pool.wait_ge(s_xr, t + 1)
                for k in range(TOPK):
                    pool.indirect_dma_start(out=xs, out_offset=bass.IndirectOffsetOnAxis(ap=slot[k][:, t:t + 1], axis=0),
                                            in_=XR[:, t % 4, :], in_offset=None).then_inc(s_sc[t % 4], 16)
            for v in range(2):
                pool.wait_ge(s_yst[v], 16 * (NSLOT // 2) + 16)
            for t in range(NT):
                if t >= 4:
                    pool.wait_ge(s_y, TOPK * (t - 3))
                for k in range(TOPK):
                    pool.indirect_dma_start(out=YG[:, t % 4, k, :], out_offset=None, in_=ys,
                                            in_offset=bass.IndirectOffsetOnAxis(ap=slot[k][:, t:t + 1], axis=0))\
                        .then_inc(s_yg[t % 4], 16)

        @block.scalar
        def _(act):
            act.sem_inc(s_yst[0], 16)
            act.sem_inc(s_yst[1], 16)
            act.sem_inc(s_ys, 2)
            act.wait_ge(s_const, 11)
            act.wait_ge(s_mv, NT)
            act.activation(std[:, :], mv[:, :, 1], ACT.Sqrt, bias=eps_col[:, 0:1]).then_inc(s_std, 1)
            act.wait_ge(s_gate, 32)
            act.activation(gate_hi[:, :, :], gate_raw[:, :, :], ACT.Copy).then_inc(s_whi, 1)
            def logits_hi(G, v):
                for c in range(KC):
                    act.wait_ge(s_T, G * KC + c + 1)
                    act.activation(XT_hi[:, v, c, :], TL_ps[v][c][:, :], ACT.Copy).then_inc(s_xth, 1)

            def logits_copy(G, v):
                act.wait_ge(s_lps, G + 1)
                act.activation(lgT[0:NX, v, :], L_ps[v][0:NX, :], ACT.Copy).then_inc(s_lc, 1)

            logits_hi(0, 0)
            logits_hi(1, 1)
            logits_copy(0, 0)
            with act.Fori(0, NG // 2 - 1) as k:
                for v in range(2):
                    logits_hi(k * 2 + v + 2, v)
                    logits_copy(k * 2 + v + 1, 1 - v)
            logits_copy(NG - 1, 1)
            act.wait_ge(s_w, 32)
            act.activation(sw13_hi[:, :, :], sw13_raw[:, :, :], ACT.Copy).then_inc(s_whi, 1)
            act.activation(sw2_hi[:, :, :], sw2_raw[:, :, :], ACT.Copy).then_inc(s_whi, 1)

            def group_hi(G):
                for c in range(KC):
                    act.wait_ge(s_T, N_T + KC * G + c + 1)
                    act.activation(XT_hi[:, G % 2, c, :], T_ps[c][:, :], ACT.Copy).then_inc(s_xth, 1)

            def gate_silu(n):
                act.wait_ge(s_g, n + 1)
                if n >= 2:
                    act.wait_ge(s_hf, n - 1)
                act.activation(sg[:, n % 2, :], G_ps[n % 2][:, :], ACT.Silu).then_inc(s_sg, 1)

            def chunk_hi(n):
                act.wait_ge(s_hf, n + 1)
                if n >= 2:
                    act.wait_ge(s_hu, n - 1)
                act.activation(h_hi[:, n % 2, :], hf[:, n % 2, :], ACT.Copy).then_inc(s_hh, 1)

            def shared(groups):
                for G in groups:
                    for n in range(MC * G, MC * G + MC):
                        gate_silu(n)
                        chunk_hi(n)
                        if n % MC == 2 and G + 1 in groups:
                            group_hi(G + 1)
                        if n < KC * NX:
                            act.activation(W_hi[:, n % KC, n // KC, :], W_raw[:, n % KC, n // KC, :],
                                           ACT.Copy).then_inc(s_wrh, 1)

            group_hi(0)
            act.wait_ge(s_r, 2)
            act.activation(tmp[:, :, :], logit[:, :, :], ACT.Exp).then_inc(s_ex, 1)
            act.wait_ge(s_wr, 16 * NX)
            shared(range(HALF))

            def hidden_hi(i, v):
                act.wait_ge(s_hT, i + 1)
                act.activation(hT_hi[:, v, :, :], HT_ps[v][:, 0:D].rearrange("p (c n) -> p c n", c=KC), ACT.Copy)\
                   .then_inc(s_hTh, 1)

            def silu(i, v):
                act.wait_ge(s_s1, i + 1)
                act.activation(sr[:, v, :], S_ps[v][:, 0:D], ACT.Silu).then_inc(s_sr, 1)

            def tokens_hi(i, v):
                act.wait_ge(s_xsT, i + 1)
                act.activation(XST_hi[:, v, :, :], XT_ps[v][:, 0:D].rearrange("p (c n) -> p c n", c=KC), ACT.Copy)\
                   .then_inc(s_xsh, 1)

            def output(i, v, k):
                act.wait_ge(s_s2, i + 1)
                act.wait_ge(s_yst[v], 16 * k + 16)
                act.activation(YS[:, v, :], Y_ps[v][:, 0:D], ACT.Copy).then_inc(s_ys, 1)

            for i in range(-3, 0):
                tokens_hi(i + 3, (i + 3) % 2)
                if i + 2 >= 0:
                    silu(i + 2, i % 2)
                if i + 1 >= 0:
                    hidden_hi(i + 1, (i + 1) % 2)
            with act.Fori(0, N_FULL // 2) as k:
                for v in range(2):
                    tokens_hi(k * 2 + v + 3, 1 - v)
                    silu(k * 2 + v + 2, v)
                    hidden_hi(k * 2 + v + 1, 1 - v)
                    output(k * 2 + v, v, k)
            for i in range(N_FULL, NSLOT):
                if i + 3 < NSLOT:
                    tokens_hi(i + 3, (i + 3) % 2)
                if i + 2 < NSLOT:
                    silu(i + 2, i % 2)
                if i + 1 < NSLOT:
                    hidden_hi(i + 1, (i + 1) % 2)
                output(i, i % 2, i // 2)
            group_hi(HALF)
            for v in range(2):
                act.wait_ge(s_yst[v], 16 * (NSLOT // 2) + 16)
            shared(range(HALF, NG))

        @block.vector
        def _(dve):
            dve.sem_inc(s_xtl, 2 * KC)
            dve.sem_inc(s_lg, 2)
            dve.sem_inc(s_xsl, 2)
            dve.sem_inc(s_hTl, 2)
            dve.sem_inc(s_hr, 2)
            dve.wait_ge(s_const, 11)
            for t in range(NT):
                dve.bn_aggr(mv[:, t, :], st1[:, t, :]).then_inc(s_mv, 1)
            dve.wait_ge(s_std, 1)
            dve.reciprocal(rstd[:, :], std[:, :]).then_inc(s_rstd, 1)
            dve.wait_ge(s_rstd, 1)
            dve.wait_ge(s_mv, NT)

            def normalised(out, t):
                return dve.tensor_scalar(out, tile_of(X, t), flat(mv[:, bass.ds(t, 1), 0:1]), rstd[:, bass.ds(t, 1)],
                                         ALU.subtract, ALU.mult)

            def logits_xn(G, v):
                for j in range(GT):
                    normalised(XN[:, v, j, :], G * GT + j).then_inc(s_xn, 1)

            def logits_lo(G, v):
                for c in range(KC):
                    dve.wait_ge(s_xth, G * KC + c + 1)
                    dve.tensor_tensor(XT_lo[:, v, c, :], TL_ps[v][c][:, :], XT_hi[:, v, c, :].bitcast(f32),
                                      ALU.subtract).then_inc(s_xtl, 1)

            def logits_out(G, v):
                dve.wait_ge(s_lt, G + 1)
                dve.tensor_copy(logit[:, bass.ds(G * GT, GT), :],
                                LT_ps[v][:, 0:GT * NX].rearrange("p (t e) -> p t e", t=GT)).then_inc(s_lg, 1)

            logits_xn(0, 0)
            dve.wait_ge(s_whi, 1)
            dve.tensor_tensor(gate_lo[:, :, :], gate_raw[:, :, :], gate_hi[:, :, :].bitcast(f32), ALU.subtract)\
               .then_inc(s_wlo, 1)
            logits_xn(1, 1)
            logits_lo(0, 0)
            logits_xn(2, 0)
            logits_lo(1, 1)
            with dve.Fori(0, NG // 2 - 2) as k:
                for v in range(2):
                    logits_xn(k * 2 + v + 3, 1 - v)
                    logits_lo(k * 2 + v + 2, v)
                    logits_out(k * 2 + v, v)
            logits_xn(NG - 1, 1)
            logits_lo(NG - 2, 0)
            logits_out(NG - 4, 0)
            logits_lo(NG - 1, 1)
            logits_out(NG - 3, 1)

            def group_xn(G):
                for j in range(GT):
                    normalised(XN[:, G % 2, j, :], G * GT + j).then_inc(s_xn, 1)

            def group_lo(G):
                for c in range(KC):
                    dve.wait_ge(s_xth, KC * (NG + G) + c + 1)
                    dve.tensor_tensor(XT_lo[:, G % 2, c, :], T_ps[c][:, :], XT_hi[:, G % 2, c, :].bitcast(f32),
                                      ALU.subtract).then_inc(s_xtl, 1)

            group_xn(0)
            for G in (NG - 2, NG - 1):
                logits_out(G, G % 2)
            dve.wait_ge(s_whi, 3)
            for raw, hi, lo in ((sw13_raw, sw13_hi, sw13_lo), (sw2_raw, sw2_hi, sw2_lo)):
                dve.tensor_tensor(lo[:, :, :], raw[:, :, :], hi[:, :, :].bitcast(f32), ALU.subtract)\
                   .then_inc(s_wlo, 1)
            group_lo(0)

            step = [0]

            def done(ins):
                step[0] += 1
                ins.then_inc(s_r, 1)
                dve.wait_ge(s_r, step[0])

            def over_e(ap):
                return ap[:, :].unsqueeze(2).to_broadcast([P, NT, NX])

            def over_t(ap):
                return ap[:, :].unsqueeze(1).to_broadcast([P, NT, NX])

            dve.wait_ge(s_lg, NG + 2)
            done(dve.tensor_reduce(red[:, :], logit[:, :, :], AX.X, ALU.max))
            done(dve.tensor_tensor(logit[:, :, :], logit[:, :, :], over_e(red), ALU.subtract))
            dve.wait_ge(s_ex, 1)
            done(dve.tensor_reduce(red[:, :], tmp[:, :, :], AX.X, ALU.add))
            done(dve.reciprocal(red2[:, :], red[:, :]))
            done(dve.tensor_tensor(score[:, :, :], tmp[:, :, :], over_e(red2), ALU.mult))
            done(dve.tensor_tensor(biased[:, :, :], score[:, :, :], over_t(gbias), ALU.add))
            for k in range(TOPK):
                done(dve.tensor_reduce(red[:, :], biased[:, :, :], AX.X, ALU.max))
                done(dve.tensor_tensor(tmp[:, :, :], biased[:, :, :], over_e(red), ALU.is_equal))
                done(dve.tensor_tensor(tmp[:, :, :], tmp[:, :, :], over_t(rank), ALU.mult))
                done(dve.tensor_reduce(red2[:, :], tmp[:, :, :], AX.X, ALU.max))
                done(dve.tensor_tensor(pick[k][:, :, :], over_t(rank), over_e(red2), ALU.is_equal))
                if k + 1 < TOPK:
                    done(dve.scalar_tensor_tensor(out=biased[:, :, :], in0=pick[k][:, :, :], scalar=-3.0e38,
                                                  in1=biased[:, :, :], op0=ALU.mult, op1=ALU.add))
            done(dve.tensor_tensor(chosen[:, :, :], pick[0][:, :, :], pick[1][:, :, :], ALU.add))
            assert step[0] == N_CHOSEN
            dve.wait_ge(s_cnt, 1)
            done(dve.tensor_copy(total[:, :, :], C_ps[1][:, 0:NT * NX].rearrange("p (t e) -> p e t", t=NT)))
            flat3 = [ap[:, :, :].rearrange("p e t -> p (e t)") for ap in (keep, total, upto)]
            done(dve.tensor_tensor_scan(out=flat3[2], data0=flat3[0], data1=flat3[1], initial=0.0,
                                        op0=ALU.mult, op1=ALU.add))
            done(dve.tensor_scalar(n_i[:, :], upto[:, :, NT - 1], float(P - 1), None, ALU.add))
            done(dve.tensor_scalar(n_j[:, :], n_i[:, :], P.bit_length() - 1, None, ALU.logical_shift_right))
            done(dve.tensor_copy(n_f[:, :], n_j[:, :]))
            done(dve.tensor_tensor_scan(out=ends[:, :], data0=one8[:, :], data1=n_f[:, :], initial=0.0,
                                        op0=ALU.mult, op1=ALU.add))
            done(dve.tensor_tensor(base[:, :], ends[:, :], n_f[:, :], ALU.subtract))
            done(dve.tensor_scalar(base[:, :], base[:, :], float(P), None, ALU.mult))
            done(dve.tensor_tensor(upto[:, :, :], upto[:, :, :], total[:, :, :], ALU.subtract))
            done(dve.tensor_tensor(upto[:, :, :], upto[:, :, :],
                                   base[:, :].unsqueeze(2).to_broadcast([P, NX, NT]), ALU.add))
            done(dve.tensor_tensor(slot_e[:, :, :], C_ps[0][:, 0:NT * NX].rearrange("p (t e) -> p t e", t=NT),
                                   upto[:, :, :].rearrange("p e t -> p t e"), ALU.add))
            for k in range(TOPK):
                done(dve.tensor_tensor(tmp[:, :, :], pick[k][:, :, :], slot_e[:, :, :], ALU.mult))
                done(dve.tensor_reduce(red[:, :], tmp[:, :, :], AX.X, ALU.add))
                done(dve.tensor_copy(slot[k][:, :], red[:, :]))
            dve.sem_inc(s_slot, 1)

            def slot_experts():
                done(dve.tensor_tensor(passed[:, :, :], tile_id[:, :].unsqueeze(2).to_broadcast([P, NSLOT, NX]),
                                       ends[:, :].unsqueeze(1).to_broadcast([P, NSLOT, NX]), ALU.is_ge))
                done(dve.tensor_reduce(which[:, :], passed[:, :, :], AX.X, ALU.add))
                done(dve.tensor_scalar(expert[:, :], which[:, :], float(NX - 1), None, ALU.min))
                dve.sem_inc(s_slot, 1)

            def choice_weights():
                for k in range(TOPK):
                    done(dve.tensor_tensor(tmp[:, :, :], pick[k][:, :, :], score[:, :, :], ALU.mult))
                    done(dve.tensor_reduce(weight[k][:, :], tmp[:, :, :], AX.X, ALU.add))

            def scatter_tile(t):
                if t >= 4:
                    dve.wait_ge(s_sc[t % 4], 16 * TOPK * (t // 4))
                normalised(XR[:, t % 4, :], t).then_inc(s_xr, 1)

            def add_routed(t):
                dve.wait_ge(s_yg[t % 4], 16 * TOPK * (t // 4 + 1))
                dve.wait_ge(s_zf, 2 * (t // GT) + 2)
                for k in range(TOPK):
                    if k:
                        dve.wait_ge(s_y, TOPK * t + k)
                    dve.scalar_tensor_tensor(out=X[:, t, :], in0=YG[:, t % 4, k, :], scalar=weight[k][:, t:t + 1],
                                             in1=X[:, t, :], op0=ALU.mult, op1=ALU.add).then_inc(s_y, 1)

            def add_shared(G, z):
                if z == 0:
                    dve.wait_ge(s_z, G + 1)
                else:
                    dve.wait_ge(s_hu, MC * G + MC)
                xz = X[:, G * GT + 2 * z:G * GT + 2 * z + 2, :].rearrange("p t n -> p (t n)")
                dve.tensor_tensor(xz, xz, Z_ps[z][:, :], ALU.add).then_inc(s_zf, 1)

            def shared(groups):
                for G in groups:
                    for n in range(MC * G, MC * G + MC):
                        dve.wait_ge(s_sg, n + 1)
                        dve.wait_ge(s_u, n + 1)
                        if n >= 2:
                            dve.wait_ge(s_hu, n - 1)
                        dve.tensor_tensor(hf[:, n % 2, :], U_ps[n % 2][:, :], sg[:, n % 2, :],
                                          ALU.mult).then_inc(s_hf, 1)
                        if n == 0:
                            slot_experts()
                        if n == 2:
                            choice_weights()
                        if G < HALF:
                            for t in tiles_to_scatter(n):
                                scatter_tile(t)
                        else:
                            for t in tiles_to_add(n):
                                add_routed(t)
                        dve.wait_ge(s_hh, n + 1)
                        dve.tensor_tensor(h_lo[:, n % 2, :], hf[:, n % 2, :],
                                          h_hi[:, n % 2, :].bitcast(f32), ALU.subtract).then_inc(s_hl, 1)
                        if n < KC * NX:
                            dve.wait_ge(s_wrh, n + 1)
                            dve.tensor_tensor(W_lo[:, n % KC, n // KC, :], W_raw[:, n % KC, n // KC, :],
                                              W_hi[:, n % KC, n // KC, :].bitcast(f32), ALU.subtract)\
                               .then_inc(s_wrl, 1)
                        if n % MC == 0 and G - 1 in groups:
                            add_shared(G - 1, 0)
                            add_shared(G - 1, 1)
                        if n % MC == 1 and G + 1 in groups:
                            group_xn(G + 1)
                        if n % MC == 2 and G + 1 in groups:
                            group_lo(G + 1)
                add_shared(groups[-1], 0)
                add_shared(groups[-1], 1)

            scatter_tile(0)
            scatter_tile(1)
            shared(range(HALF))

            def hidden_lo(i, v):
                dve.wait_ge(s_hTh, i + 1)
                dve.tensor_tensor(hT_lo[:, v, :, :], HT_ps[v][:, 0:D].rearrange("p (c n) -> p c n", c=KC),
                                  hT_hi[:, v, :, :].bitcast(f32), ALU.subtract).then_inc(s_hTl, 1)

            def hidden(i, v):
                dve.wait_ge(s_sr, i + 1)
                dve.tensor_tensor(hr[:, v, :], S_ps[v][:, D:2 * D], sr[:, v, :], ALU.mult).then_inc(s_hr, 1)

            def tokens_lo(i, v):
                dve.wait_ge(s_xsh, i + 1)
                dve.tensor_tensor(XST_lo[:, v, :, :], XT_ps[v][:, 0:D].rearrange("p (c n) -> p c n", c=KC),
                                  XST_hi[:, v, :, :].bitcast(f32), ALU.subtract).then_inc(s_xsl, 1)

            for i in range(-3, 0):
                tokens_lo(i + 3, (i + 3) % 2)
                if i + 2 >= 0:
                    hidden(i + 2, i % 2)
                if i + 1 >= 0:
                    hidden_lo(i + 1, (i + 1) % 2)
            with dve.Fori(0, N_FULL // 2) as k:
                for v in range(2):
                    tokens_lo(k * 2 + v + 3, 1 - v)
                    hidden(k * 2 + v + 2, v)
                    hidden_lo(k * 2 + v + 1, 1 - v)
            for i in range(N_FULL, NSLOT):
                if i + 3 < NSLOT:
                    tokens_lo(i + 3, (i + 3) % 2)
                if i + 2 < NSLOT:
                    hidden(i + 2, i % 2)
                if i + 1 < NSLOT:
                    hidden_lo(i + 1, (i + 1) % 2)
            dve.wait_ge(s_xsT, NSLOT)
            group_xn(HALF)
            group_lo(HALF)
            for v in range(2):
                dve.wait_ge(s_yst[v], 16 * (NSLOT // 2) + 16)
            shared(range(HALF, NG))
            for t in range(NT - 4, NT):
                add_routed(t)

        @block.tensor
        def _(pe):
            pe.wait_ge(s_const, 11)

            def three(out, a_hi, a_lo, b_hi, b_lo, start, stop, **kw):
                pe.matmul(out, a_hi, b_hi, start=start, stop=False, **kw)
                pe.matmul(out, a_hi, b_lo, start=False, stop=False, **kw)
                return pe.matmul(out, a_lo, b_hi, start=False, stop=stop, **kw)

            def logits_transpose(G, v):
                pe.wait_ge(s_xn, G * GT + GT)
                for c in range(KC):
                    pe.wait_ge(s_xtl, G * KC + c + 1)
                    for j in range(GT):
                        mm = pe.transpose(TL_ps[v][c][:, j * P:(j + 1) * P], XN[:, v, j, c * P:(c + 1) * P],
                                          ident[:, :])
                    mm.then_inc(s_T, 1)

            def logits(G, v):
                pe.wait_ge(s_xtl, G * KC + 3 * KC)
                if not (isinstance(G, int) and G == 0):
                    pe.wait_ge(s_lc, G)
                    pe.wait_ge(s_lg, G)
                for c in range(KC):
                    mm = three(L_ps[v][0:NX, :], gate_hi[:, c, :], gate_lo[:, c, :], XT_hi[:, v, c, :],
                               XT_lo[:, v, c, :], c == 0, c == KC - 1)
                mm.then_inc(s_lps, 1)

            def turn_logits(v):
                for j in range(GT):
                    mm = pe.transpose(LT_ps[v][:, j * NX:(j + 1) * NX], lgT[0:NX, v, j * P:(j + 1) * P],
                                      ident[0:NX, 0:NX])
                mm.then_inc(s_lt, 1)

            logits_transpose(0, 0)
            pe.wait_ge(s_wlo, 1)
            logits_transpose(1, 1)
            logits(0, 0)
            with pe.Fori(0, NG // 2 - 1) as k:
                for v in range(2):
                    logits_transpose(k * 2 + v + 2, v)
                    logits(k * 2 + v + 1, 1 - v)
                    turn_logits(v)
            logits(NG - 1, 1)
            turn_logits(0)
            pe.wait_ge(s_lc, NG)
            pe.wait_ge(s_lg, NG)
            turn_logits(1)

            def group_transpose(G):
                pe.wait_ge(s_xn, N_XN + GT * G + GT)
                for c in range(KC):
                    pe.wait_ge(s_xtl, N_XTL + KC * (G - 1) + c + 1)
                    for j in range(GT):
                        mm = pe.transpose(T_ps[c][:, j * P:(j + 1) * P], XN[:, G % 2, j, c * P:(c + 1) * P],
                                          ident[:, :])
                    mm.then_inc(s_T, 1)

            def products(n):
                G, m = n // MC, n % MC
                pe.wait_ge(s_xtl, N_XTL + KC * G + KC)
                if n >= 2:
                    pe.wait_ge(s_hf, n - 1)
                for w, bk, s_ready in ((0, G_ps, s_g), (NS, U_ps, s_u)):
                    rows = slice(w + m * P, w + (m + 1) * P)
                    for c in range(KC):
                        mm = three(bk[n % 2][:, :], sw13_hi[:, c, rows], sw13_lo[:, c, rows],
                                   XT_hi[:, G % 2, c, :], XT_lo[:, G % 2, c, :], c == 0, c == KC - 1)
                    mm.then_inc(s_ready, 1)

            def outputs(n):
                G, m = n // MC, n % MC
                pe.wait_ge(s_hl, n + 1)
                for j in range(GT):
                    if m == 0 and j % 2 == 0 and G > 0:
                        pe.wait_ge(s_zf, 2 * (G - 1) + j // 2 + 1)
                    tok = slice(j * P, (j + 1) * P)
                    mm = three(Z_ps[j // 2][:, (j % 2) * D:(j % 2 + 1) * D], h_hi[:, n % 2, tok],
                               h_lo[:, n % 2, tok], sw2_hi[:, m, :], sw2_lo[:, m, :],
                               m == 0 and j % 2 == 0, m == MC - 1, skip_group_check=True)
                    if m == MC - 1 and j == 1:
                        mm.then_inc(s_z, 1)
                mm.then_inc(s_hu, 1)

            def shared(groups, ahead):
                for G in groups:
                    for n in range(MC * G, MC * G + MC):
                        if n not in ahead:
                            products(n)
                        if n > MC * groups[0]:
                            outputs(n - 1)
                        if n % MC == 2 and G + 1 in groups:
                            group_transpose(G + 1)
                outputs(MC * groups[-1] + MC - 1)

            group_transpose(0)
            pe.wait_ge(s_wlo, 3)
            products(0)
            products(1)
            pe.wait_ge(s_r, N_CHOSEN)
            rhs = chosen[:, :, :].rearrange("p t e -> p (t e)")
            pe.matmul(C_ps[0][:, 0:NT * NX], before[:, :], rhs, start=True, stop=True)
            pe.matmul(C_ps[1][:, 0:NT * NX], ones_b[:, :], rhs, start=True, stop=True).then_inc(s_cnt, 1)
            shared(range(HALF), (0, 1))
            pe.wait_ge(s_slot, 2)
            pe.wait_ge(s_wrl, KC * NX)
            pe.wait_ge(s_zf, 2 * HALF)

            expert_reg = [pe.alloc_register(f"expert{q}") for q in range(4)]

            def load_expert(i, q):
                pe.reg_load(expert_reg[q], expert[0:1, bass.ds(i, 1)])

            def weights(e, lo, hi):
                return [[w[:, c, bass.ds(e, 1), lo:hi].rearrange("p a n -> p (a n)") for w in (W_hi, W_lo)]
                        for c in range(KC)]

            def transpose_tokens(i, v, slot4, k4):
                pe.wait_ge(s_xs[slot4], 16 * k4 + 16)
                pe.wait_ge(s_xsl, i + 1)
                for c in range(KC):
                    mm = pe.transpose(XT_ps[v][:, c * P:(c + 1) * P], XS[:, slot4, c * P:(c + 1) * P], ident[:, :])
                mm.then_inc(s_xsT, 1)

            def gate_up(i, v, q):
                w = weights(pe.snap(expert_reg[q], min_val=0, max_val=NX - 1), 0, 2 * D)
                pe.wait_ge(s_xsl, i + 3)
                pe.wait_ge(s_hr, i + 1)
                for c in range(KC):
                    mm = three(S_ps[v][:, :], XST_hi[:, v, c, :], XST_lo[:, v, c, :], w[c][0], w[c][1],
                               c == 0, c == KC - 1)
                mm.then_inc(s_s1, 1)

            def transpose_hidden(i, v):
                pe.wait_ge(s_hr, i + 3)
                pe.wait_ge(s_hTl, i + 1)
                for c in range(KC):
                    mm = pe.transpose(HT_ps[v][:, c * P:(c + 1) * P], hr[:, v, c * P:(c + 1) * P], ident[:, :])
                mm.then_inc(s_hT, 1)

            def down(i, v, q):
                w = weights(pe.snap(expert_reg[q], min_val=0, max_val=NX - 1), 2 * D, 3 * D)
                pe.wait_ge(s_hTl, i + 3)
                pe.wait_ge(s_ys, i + 1)
                for c in range(KC):
                    mm = three(Y_ps[v][:, 0:D], hT_hi[:, v, c, :], hT_lo[:, v, c, :], w[c][0], w[c][1],
                               c == 0, c == KC - 1)
                mm.then_inc(s_s2, 1)

            for i in range(-3, 0):
                load_expert(i + 3, i + 3)
                transpose_tokens(i + 3, (i + 3) % 2, i + 3, 0)
                if i + 2 >= 0:
                    gate_up(i + 2, i % 2, i + 2)
                if i + 1 >= 0:
                    transpose_hidden(i + 1, (i + 1) % 2)
            with pe.Fori(0, N_FULL // 4) as k:
                for q in range(4):
                    i, v = k * 4 + q, q % 2
                    load_expert(i + 3, (q + 3) % 4)
                    transpose_tokens(i + 3, 1 - v, (q + 3) % 4, k + (q + 3) // 4)
                    gate_up(i + 2, v, (q + 2) % 4)
                    transpose_hidden(i + 1, 1 - v)
                    down(i, v, q)
            for i in range(N_FULL, NSLOT):
                v = i % 2
                if i + 3 < NSLOT:
                    load_expert(i + 3, (i + 3) % 4)
                    transpose_tokens(i + 3, 1 - v, (i + 3) % 4, (i + 3) // 4)
                if i + 2 < NSLOT:
                    gate_up(i + 2, v, (i + 2) % 4)
                if i + 1 < NSLOT:
                    transpose_hidden(i + 1, 1 - v)
                down(i, v, i % 4)
            group_transpose(HALF)
            pe.wait_ge(s_ys, NSLOT + 2)
            shared(range(HALF, NG), ())

    outer.close()


def kernel(**inputs):
    import numpy as _np
    import concourse.bacc as _bacc
    from concourse import mybir as _mybir
    from concourse.bass_utils import run_bass_kernel_spmd as _run

    a = {name: _np.asarray(v) for name, v in inputs.items()}
    laid = {
        "x": a["L0_attn_x"], "wv": a["L0_attn_wv"], "bv": a["L0_attn_bv"], "woT": a["L0_attn_wo"].T,
        "bo": a["L0_attn_bo"], "w3dT": a["L0_attn_w3d"].T, "b3d": a["L0_attn_b3d"],
        "gateT": a["L0_ffn_gate_w"].T, "gate_bias": a["L0_ffn_gate_bias"],
        "wT": _np.concatenate([a[f"L0_ffn_{w}"].transpose(0, 2, 1) for w in ("w1", "w3", "w2")], axis=2),
        "sw13T": _np.concatenate([a["L0_ffn_sw1"].T, a["L0_ffn_sw3"].T], axis=1),
        "sw2T": a["L0_ffn_sw2"].T,
    }
    nc = _bacc.Bacc("TRN2", target_bir_lowering=False, num_devices=1)
    arrays, args = {}, []
    for name, v in laid.items():
        arrays[f"in_{name}_dram"] = v = _np.ascontiguousarray(v)
        args.append(nc.dram_tensor(f"in_{name}_dram", v.shape, _mybir.dt.from_np(v.dtype), kind="ExternalInput").ap())
    args.append(nc.dram_tensor("out_0_dram", (NB, S, D), f32, kind="ExternalOutput").ap())
    attention_and_experts(nc, *args)
    r = _run(nc, [arrays], core_ids=[0])
    return r.results[0]["out_0_dram"]
```

```python
import concourse.bass as bass
from concourse import mybir
from contextlib import ExitStack

P = 128
NB, S, D = 2, 2048, 256
NT = NB * S // P
TB = S // P
GT = 4
GB = TB // GT
KC = D // P
MW = D + 4
VW = 2 * D + 2
TRI = sum(S - P * k for k in range(TB))
KR = 32
NQ = 4
N_POS = 45
NE = 8
NG = NT // GT
NX, TOPK = 8, 2
NS = 512
MC = NS // P
NSLOT = NT * TOPK + NX
N_CHOSEN = 18
N_FULL = (NSLOT - 3) // 4 * 4
H = 16
SCALE = 1.0 / (D // H) ** 0.5
EPS = 1e-5
f32 = mybir.dt.float32
f32r = mybir.dt.float32r
bf16 = mybir.dt.bfloat16
i32 = mybir.dt.int32
u32 = mybir.dt.uint32
ALU = mybir.AluOpType
ACT = mybir.ActivationFunctionType
AX = mybir.AxisListType


def flat(ap):
    return ap.rearrange("p a n -> p (a n)")


def tile_of(T, i):
    return flat(T[:, bass.ds(i, 1), :])



def attention_and_experts(nc, x, wv, bv, woT, bo, w3dT, b3d, gateT, gate_bias, wT, sw13T, sw2T, out):
    x_v = x.rearrange("b (t p) d -> p (b t) d", p=P)
    out_v = out.rearrange("b (t p) d -> p (b t) d", p=P)
    xs = nc.dram_tensor("slots_in", (NSLOT * P, D), f32, kind="Internal").ap()
    ys = nc.dram_tensor("slots_out", (NSLOT * P, D), f32, kind="Internal").ap()
    xs_p = xs.rearrange("(p i) d -> p i d", p=P)
    xs_t = xs.rearrange("(i p) d -> i p d", p=P)
    ys_t = ys.rearrange("(i p) d -> i p d", p=P)
    outer = ExitStack()
    X = outer.enter_context(nc.sbuf_tensor("X", [P, NT, D], f32))
    st1 = outer.enter_context(nc.sbuf_tensor("st1", [P, NT, 6], f32))

    with ExitStack() as ctx:
        def sb(name, shape, dt=f32):
            return ctx.enter_context(nc.sbuf_tensor(name, shape, dt))

        def sem(name):
            return ctx.enter_context(nc.semaphore(name))

        M_raw = sb("M_raw", [P, KC, MW])
        M_hi = sb("M_hi", [P, KC, MW], f32r)
        M_lo = sb("M_lo", [P, KC, MW], f32r)
        bv_col = sb("bv_col", [P, KC])
        c_raw = sb("c_raw", [1, MW])
        c_hi = sb("c_hi", [1, MW], f32r)
        c_lo = sb("c_lo", [1, MW], f32r)
        bo_row = sb("bo_row", [1, D])
        one_f = sb("one_f", [1, P])
        one_row = sb("one_row", [1, P], f32r)
        ident = sb("ident", [P, P])
        eps_col = sb("eps_col", [P, 1])
        zero = sb("zero", [P, D])
        one_zero = sb("one_zero", [P, TB, 2])
        st = sb("st", [P, TB, 6])
        mv = sb("mv", [P, TB, 2])
        std = sb("std", [P, TB])
        rstd = sb("rstd", [P, TB])
        with ExitStack() as first:
            wv_raw = first.enter_context(nc.sbuf_tensor("wv_raw", [P, KC, D], f32))
            woT_raw = first.enter_context(nc.sbuf_tensor("woT_raw", [P, KC, D], f32))
        VO = sb("VO", [P, TB, VW], f32r)
        pos = sb("pos", [P, TB, 3])
        pmax = sb("pmax", [P, 1])
        pmax_row = sb("pmax_row", [1, 1])
        pbits = sb("pbits", [P, 1], i32)
        magic = sb("magic", [P, 1])
        hsum = sb("hsum", [P, TB, 3])
        h = sb("h", [P, TB, 3])
        l = sb("l", [P, TB, 3])
        lh = sb("lh", [P, TB, 3], f32r)
        t3 = sb("t3", [P, TB, 3])
        t3b = sb("t3b", [P, TB, 3])
        nrm = sb("nrm", [P, 2, TB])
        nrm_hi = sb("nrm_hi", [P, 2, TB], f32r)
        with ExitStack() as first:
            XT_hi = first.enter_context(nc.sbuf_tensor("XT_hi", [P, 2, KC, GT * P], f32r))
            XT_lo = first.enter_context(nc.sbuf_tensor("XT_lo", [P, 2, KC, GT * P], f32r))
        QT = sb("QT", [2 * KR, S], f32r)
        KTh = sb("KTh", [2 * KR, S], f32r)
        KTl = sb("KTl", [2 * KR, S], f32r)
        E = sb("E", [P, TRI])
        rden = sb("rden", [P, GT])
        with ExitStack() as first:
            def early(name, shape):
                return first.enter_context(nc.sbuf_tensor(name, shape, f32))
            XN = early("XN", [P, 2, GT, D])
            FQ = early("FQ", [P, TB, 2 * KR])
            FKh = early("FKh", [P, TB, 2 * KR])
            FKl = early("FKl", [P, TB, 2 * KR])
        E_hi = sb("E_hi", [P, NE, 512], f32r)
        E_lo = sb("E_lo", [P, NE, 512], f32r)

        bank = [ctx.enter_context(nc.psum_tensor(f"a_bank{i}", [P, 512], f32)) for i in range(8)]
        T_ps, V_ps = (bank[0:2], bank[6:8]), bank[2:6]
        M_ps, c_ps, turn_ps, spread_ps = bank[2:4], bank[0], bank[0], bank[1]
        O_ps = (bank[0:4], bank[4:8])
        Q_ps = bank[0:4]

        s_x = [sem(f"s_x_group{g}") for g in range(GB)]
        s_zero = sem("s_zero")
        s_wm = sem("s_wm")
        s_w = sem("s_w")
        s_const = sem("s_const")
        s_cps = sem("s_cps")
        s_craw = sem("s_craw")
        s_chi = sem("s_chi")
        s_M = sem("s_M")
        s_st = sem("s_st")
        s_mv = sem("s_mv")
        s_std = sem("s_std")
        s_rstd = sem("s_rstd")
        s_xn = sem("s_xn")
        s_T = sem("s_T")
        s_xth = sem("s_xth")
        s_xtl = sem("s_xtl")
        s_vps = [sem(f"s_vps{i}") for i in range(2)]
        s_voh = sem("s_voh")
        s_pos = sem("s_pos")
        s_vol = sem("s_vol")
        s_fz = sem("s_fz")
        s_f = sem("s_f")
        s_pt = sem("s_pt")
        s_ft = sem("s_ft")
        s_fr = sem("s_fr")
        s_q = sem("s_q")
        s_e2 = sem("s_e2")
        s_diag = sem("s_diag")
        s_dist = sem("s_dist")
        s_exp = sem("s_exp")
        s_eh = sem("s_eh")
        s_eh_act = sem("s_eh_act")
        s_el = sem("s_el")
        s_eb = sem("s_eb")
        s_acc = sem("s_acc")
        s_rd = sem("s_rd")
        s_x1 = sem("s_x1")

        block = ctx.enter_context(nc.Block())

        def off(kt):
            return sum(S - P * k for k in range(kt))

        def block_of(Q, kt):
            q0 = max(P * kt, GT * P * Q)
            w = GT * P * (Q + 1) - q0
            at = off(kt) + q0 - P * kt
            return E[:, at:at + w], q0, w

        blocks = [(Q, kt) for Q in range(GB) for kt in range(GT * Q + GT)]
        NBLK = len(blocks)
        halves = [range(0, GB // 2), range(GB // 2, GB)]
        sq_blocks = [(Q, kt) for half in halves for kt in range(GT * half[-1] + GT)
                     for Q in range(max(kt // GT, half[0]), half[-1] + 1)]
        N_HI_DVE = blocks.index((halves[1][0], 0))
        AHEAD = 3
        NROW = sum(GT * half[-1] + GT for half in halves)

        def row_of(half, kt):
            q0, q1 = max(P * kt, GT * P * half[0]), GT * P * (half[-1] + 1)
            return E[:, off(kt) + q0 - P * kt:off(kt) + q1 - P * kt]

        @block.sync
        def _(sp):
            for b in range(NB):
                for g in range(GB):
                    n = b * GB + g
                    if b > 0:
                        sp.wait_ge(s_x[g], 16 * b)
                    sp.dma_start(X[:, n * GT:(n + 1) * GT, :], x_v[:, n * GT:(n + 1) * GT, :]).then_inc(s_x[g], 16)
            sp.wait_ge(s_const, 9)
            for i in range(8):
                w = NSLOT // 8
                sp.dma_start(xs_p[:, i * w:(i + 1) * w, :], zero[:, :].unsqueeze(1).to_broadcast([P, w, D]))\
                  .then_inc(s_zero, 16)
            sp.wait_ge(s_zero, 128)

        @block.gpsimd
        def _(pool):
            pool.memset(ident[:, :], 0.0).then_inc(s_const, 1)
            pool.memset(one_f[:, :], 1.0).then_inc(s_const, 1)
            pool.memset(eps_col[:, :], EPS).then_inc(s_const, 1)
            pool.memset(M_raw[:, :, D + 3:MW], 0.0).then_inc(s_const, 1)
            pool.memset(c_raw[:, D + 3:MW], 0.0).then_inc(s_const, 1)
            pool.memset(one_zero[:, :, 0], 1.0).then_inc(s_const, 1)
            pool.memset(one_zero[:, :, 1], 0.0).then_inc(s_const, 1)
            pool.memset(zero[:, :], 0.0).then_inc(s_const, 1)
            pool.wait_ge(s_const, 8)
            pool.affine_select(out=ident[:, :], in_=ident[:, :], compare_op=ALU.not_equal, fill=1.0, base=0,
                               pattern=[[-1, P]], channel_multiplier=1).then_inc(s_const, 1)
            for b in range(NB):
                if b > 0:
                    pool.wait_ge(s_eb, b * NBLK + NE)
                for F in (FQ, FKh, FKl):
                    pool.memset(F[:, :, :], 0.0).then_inc(s_fz, 1)
                for kt in range(TB):
                    blk = E[:, off(kt):off(kt) + P]
                    pool.wait_ge(s_e2, b * NBLK + sq_blocks.index((kt // GT, kt)) + 1 + NQ)
                    pool.affine_select(out=blk, in_=blk, compare_op=ALU.is_ge, fill=1.0e30, base=0,
                                       pattern=[[1, P]], channel_multiplier=-1).then_inc(s_diag, 1)
                    pool.wait_ge(s_diag, 2 * (b * TB + kt) + 1)
                    pool.affine_select(out=blk, in_=blk, compare_op=ALU.not_equal, fill=0.0, base=0,
                                       pattern=[[1, P]], channel_multiplier=-1).then_inc(s_diag, 1)

        @block.scalar
        def _(act):
            act.dma_start(wv_raw[:, :, :], wv.rearrange("(c p) n -> p c n", c=KC)).then_inc(s_wm, 16)
            act.dma_start(woT_raw[:, :, :], woT.rearrange("(c p) n -> p c n", c=KC)).then_inc(s_wm, 16)
            act.dma_start(bv_col[:, :], bv.rearrange("(c p) -> p c", c=KC), allow_slow_non_contiguous=True)\
               .then_inc(s_w, 16)
            act.dma_start(bo_row[:, :], bo.rearrange("(a n) -> a n", a=1)).then_inc(s_w, 16)
            act.dma_start(M_raw[:, :, D:D + 3], w3dT.rearrange("(c p) n -> p c n", c=KC)).then_inc(s_w, 16)
            act.dma_start(c_raw[:, D:D + 3], b3d.rearrange("(a n) -> a n", a=1)).then_inc(s_w, 16)
            act.wait_ge(s_const, 9)
            for b in range(NB):
                act.wait_ge(s_mv, TB * b + TB)
                act.activation(std[:, :], mv[:, :, 1], ACT.Sqrt, bias=eps_col[:, 0:1]).then_inc(s_std, 1)

                def group_hi(g):
                    for c in range(KC):
                        act.wait_ge(s_T, KC * (b * GB + g) + c + 1)
                        act.activation(XT_hi[:, g % 2, c, :], T_ps[g % 2][c][:, :], ACT.Copy).then_inc(s_xth, 1)

                group_hi(0)
                for g in range(GB):
                    if g + 1 < GB:
                        group_hi(g + 1)
                    for j in range(GT):
                        act.wait_ge(s_vps[j % 2], 2 * (b * GB + g) + j // 2 + 1)
                        act.activation(VO[:, g * GT + j, 0:D], V_ps[j][:, 0:D], ACT.Copy).then_inc(s_voh, 1)
                for g in range(GB):
                    for k, dst in enumerate((QT, KTh, KTl)):
                        n = 3 * g + k
                        act.wait_ge(s_ft, 3 * GB * b + n + 1)
                        act.activation(dst[:, g * 512:(g + 1) * 512], Q_ps[n % 4][0:2 * KR, :], ACT.Copy)\
                           .then_inc(s_fr, 1)
                def high_part(n):
                    blk, _, w = block_of(*blocks[n])
                    act.wait_ge(s_exp, b * NBLK + n + 1)
                    act.wait_ge(s_eb, b * NBLK + n + 1)
                    act.activation(E_hi[:, n % NE, 0:w], blk, ACT.Copy).then_inc(s_eh_act, 1)

                rows = n = 0
                for half in halves:
                    for kt in range(GT * half[-1] + GT):
                        row = row_of(half, kt)
                        act.wait_ge(s_e2, b * NBLK + sq_blocks.index((half[-1], kt)) + 1 + NQ)
                        act.wait_ge(s_diag, 2 * (b * TB + kt) + 2)
                        act.activation(row, row, ACT.Sqrt).then_inc(s_dist, 1)
                    rows += GT * half[-1] + GT
                    act.wait_ge(s_dist, b * NROW + rows)
                    for Q in half:
                        for kt in range(GT * Q + GT):
                            blk = block_of(Q, kt)[0]
                            act.activation(blk, blk, ACT.Exp, scale=-SCALE).then_inc(s_exp, 1)
                            if n - AHEAD >= N_HI_DVE:
                                high_part(n - AHEAD)
                            n += 1
                for n in range(NBLK - AHEAD, NBLK):
                    high_part(n)

        @block.vector
        def _(dve):
            dve.sem_inc(s_xtl, 2 * KC)
            dve.sem_inc(s_vol, GT)
            dve.sem_inc(s_e2, NQ)
            dve.sem_inc(s_x1, 2 * GT)

            def statistics(b, t):
                if t < TB:
                    if t % GT == 0:
                        dve.wait_ge(s_x[t // GT], 16 * b + 16)
                    dve.bn_stats(st[:, t, :], X[:, b * TB + t, :]).then_inc(s_st, 1)
                if t >= 1:
                    dve.wait_ge(s_st, b * TB + t)
                    dve.bn_aggr(mv[:, t - 1, :], st[:, t - 1, :]).then_inc(s_mv, 1)

            for t in range(TB + 1):
                statistics(0, t)
            dve.wait_ge(s_w, 64)
            dve.wait_ge(s_const, 9)
            dve.wait_ge(s_cps, 1)
            for c in range(KC):
                dve.tensor_copy(M_raw[:, c, 0:D], M_ps[c][:, 0:D]).then_inc(s_craw, 1)
            dve.tensor_tensor(c_raw[:, 0:D], c_ps[0:1, 0:D], bo_row[:, :], ALU.add).then_inc(s_craw, 1)
            dve.wait_ge(s_craw, 3)
            dve.tensor_copy(M_hi[:, :, :], M_raw[:, :, :]).then_inc(s_chi, 1)
            dve.tensor_copy(c_hi[:, :], c_raw[:, :]).then_inc(s_chi, 1)
            dve.tensor_copy(one_row[:, :], one_f[:, :]).then_inc(s_M, 1)
            dve.tensor_copy(VO[:, :, D:D + 2], one_zero[:, :, :]).then_inc(s_M, 1)
            dve.wait_ge(s_chi, 2)
            dve.tensor_tensor(M_lo[:, :, :], M_raw[:, :, :], M_hi[:, :, :].bitcast(f32), ALU.subtract).then_inc(s_M, 1)
            dve.tensor_tensor(c_lo[:, :], c_raw[:, :], c_hi[:, :].bitcast(f32), ALU.subtract).then_inc(s_M, 1)
            for b in range(NB):
                dve.wait_ge(s_std, b + 1)
                dve.reciprocal(rstd[:, :], std[:, :]).then_inc(s_rstd, 1)

                def normalise(g, v):
                    dve.wait_ge(s_rstd, b + 1)
                    dve.wait_ge(s_mv, TB * b + TB)
                    for j in range(GT):
                        t = g * GT + j
                        dve.tensor_scalar(XN[:, v, j, :], tile_of(X, b * TB + t), mv[:, t, 0:1], rstd[:, t:t + 1],
                                          ALU.subtract, ALU.mult).then_inc(s_xn, 1)

                def group_lo(g):
                    for c in range(KC):
                        dve.wait_ge(s_xth, KC * (b * GB + g) + c + 1)
                        dve.tensor_tensor(XT_lo[:, g % 2, c, :], T_ps[g % 2][c][:, :],
                                          XT_hi[:, g % 2, c, :].bitcast(f32), ALU.subtract).then_inc(s_xtl, 1)

                normalise(0, 0)
                normalise(1, 1)
                group_lo(0)
                for g in range(GB):
                    if g + 2 < GB:
                        normalise(g + 2, g % 2)
                    if g + 1 < GB:
                        group_lo(g + 1)
                    for j in range(GT):
                        t = g * GT + j
                        dve.wait_ge(s_voh, b * TB + t + 1)
                        dve.tensor_copy(pos[:, t, :], V_ps[j][:, D:D + 3]).then_inc(s_pos, 1)
                        dve.tensor_tensor(VO[:, t, D + 2:VW], V_ps[j][:, 0:D], VO[:, t, 0:D].bitcast(f32),
                                          ALU.subtract).then_inc(s_vol, 1)

                step = [0]

                def put(ins):
                    step[0] += 1
                    ins.then_inc(s_f, 1)

                def done(ins):
                    put(ins)
                    dve.wait_ge(s_f, N_POS * b + step[0])

                dve.wait_ge(s_pos, TB * b + TB)
                put(dve.tensor_reduce(pmax[:, :], pos[:, :, :].rearrange("p t c -> p (t c)"), AX.X, ALU.max,
                                      apply_absolute_value=True))
                dve.wait_ge(s_pt, 2 * b + 1)
                put(dve.tensor_reduce(pmax_row[:, :], turn_ps[0:1, 0:P], AX.X, ALU.max))
                dve.wait_ge(s_pt, 2 * b + 2)
                done(dve.tensor_copy(pmax[:, :], spread_ps[:, 0:1]))
                done(dve.tensor_scalar(pbits[:, :], pmax[:, :].bitcast(i32), 0x7F800000, None, ALU.bitwise_and))
                done(dve.tensor_scalar(magic[:, :], pbits[:, :].bitcast(f32), 1.5 * 2.0 ** 14, None, ALU.mult))
                done(dve.tensor_scalar(hsum[:, :, :], pos[:, :, :], magic[:, 0:1], None, ALU.add))
                done(dve.tensor_scalar(h[:, :, :], hsum[:, :, :], magic[:, 0:1], None, ALU.subtract))
                done(dve.tensor_tensor(l[:, :, :], pos[:, :, :], h[:, :, :], ALU.subtract))
                put(dve.tensor_copy(lh[:, :, :], l[:, :, :]))
                put(dve.tensor_tensor(t3[:, :, :], h[:, :, :], h[:, :, :], ALU.mult))
                done(dve.scalar_tensor_tensor(out=t3b[:, :, :], in0=h[:, :, :], scalar=2.0, in1=l[:, :, :],
                                              op0=ALU.mult, op1=ALU.add))
                put(dve.tensor_reduce(nrm[:, 0, :], t3[:, :, :], AX.X, ALU.add))
                done(dve.tensor_tensor(t3b[:, :, :], t3b[:, :, :], l[:, :, :], ALU.mult))
                done(dve.tensor_reduce(nrm[:, 1, :], t3b[:, :, :], AX.X, ALU.add))
                done(dve.tensor_copy(nrm_hi[:, :, :], nrm[:, :, :]))
                dve.wait_ge(s_fz, 3 * (b + 1))
                lhf = lh[:, :, :].bitcast(f32)
                ll = FQ[:, :, KR + 3:KR + 6]
                put(dve.tensor_tensor(ll, l[:, :, :], lhf, ALU.subtract))
                put(dve.tensor_copy(FQ[:, :, 0:3], h[:, :, :]))
                put(dve.memset(FQ[:, :, 3:5], 1.0))
                put(dve.memset(FQ[:, :, KR + 24:KR + 26], 1.0))
                put(dve.memset(FKh[:, :, 5:7], 1.0))
                put(dve.memset(FKl[:, :, KR + 26:KR + 28], 1.0))
                for k, (F, at) in enumerate(((FQ, 5), (FQ, KR + 26), (FKh, 3), (FKl, KR + 24))):
                    put(dve.tensor_copy(F[:, :, at], nrm_hi[:, k % 2, :].bitcast(f32)))
                    put(dve.tensor_tensor(F[:, :, at + 1], nrm[:, k % 2, :], nrm_hi[:, k % 2, :].bitcast(f32),
                                          ALU.subtract))
                for k, src in ((0, lhf), (6, h[:, :, :]), (9, h[:, :, :]), (12, lhf), (15, lhf)):
                    put(dve.tensor_copy(FQ[:, :, KR + k:KR + k + 3], src))
                put(dve.tensor_scalar(FKh[:, :, 0:3], h[:, :, :], -2.0, None, ALU.mult))
                for k, src in ((0, h[:, :, :]), (3, h[:, :, :]), (6, lhf), (12, lhf)):
                    put(dve.tensor_scalar(FKl[:, :, KR + k:KR + k + 3], src, -2.0, None, ALU.mult))
                done(dve.tensor_scalar(FKl[:, :, KR + 18:KR + 21], lhf, -2.0, None, ALU.mult))
                for k in (18, 21):
                    put(dve.tensor_copy(FQ[:, :, KR + k:KR + k + 3], ll))
                for k in (9, 15, 21):
                    put(dve.tensor_scalar(FKl[:, :, KR + k:KR + k + 3], ll, -2.0, None, ALU.mult))
                assert step[0] == N_POS

                for n, (Q, kt) in enumerate(sq_blocks):
                    blk, _, w = block_of(Q, kt)
                    dve.wait_ge(s_q, b * NBLK + n + 1)
                    dve.tensor_scalar(blk, Q_ps[n % NQ][:, 0:w], 0.0, None, ALU.max).then_inc(s_e2, 1)

                def finish(Q, j):
                    t = b * TB + GT * Q + j
                    n = GT * Q + j
                    if j < GT - 1:
                        dve.wait_ge(s_acc, b * (GT - 1) * GB + (GT - 1) * Q + j + 1)
                    else:
                        dve.wait_ge(s_eb, b * NBLK + blocks.index((Q, GT * Q + j)) + 1 + NE)
                    dve.reciprocal(rden[:, j:j + 1], O_ps[Q % 2][j][:, D:D + 1]).then_inc(s_rd, 1)
                    dve.wait_ge(s_rd, b * TB + n + 1)
                    dve.scalar_tensor_tensor(out=tile_of(X, t), in0=O_ps[Q % 2][j][:, 0:D], scalar=rden[:, j:j + 1],
                                             in1=tile_of(X, t), op0=ALU.mult, op1=ALU.add).then_inc(s_x1, 1)
                    dve.wait_ge(s_x1, t + 1 + 2 * GT)
                    dve.bn_stats(tile_of(st1, t), tile_of(X, t))

                def split_hi(n):
                    blk, _, w = block_of(*blocks[n])
                    dve.wait_ge(s_exp, b * NBLK + n + 1)
                    dve.wait_ge(s_eb, b * NBLK + n + 1)
                    dve.tensor_copy(E_hi[:, n % NE, 0:w], blk).then_inc(s_eh, 1)

                def split_lo(n):
                    blk, _, w = block_of(*blocks[n])
                    if n < N_HI_DVE:
                        dve.wait_ge(s_eh, b * N_HI_DVE + n + 1)
                    else:
                        dve.wait_ge(s_eh_act, (b + 1) * (NBLK - N_HI_DVE) + n + 1 - NBLK)
                    dve.tensor_tensor(E_lo[:, n % NE, 0:w], blk, E_hi[:, n % NE, 0:w].bitcast(f32),
                                      ALU.subtract).then_inc(s_el, 1)

                split_hi(0)
                for n, (Q, kt) in enumerate(blocks):
                    if n + 1 < N_HI_DVE:
                        split_hi(n + 1)
                    split_lo(n)
                    if b + 1 < NB and n >= NBLK - 1 - TB:
                        statistics(b + 1, n - (NBLK - 1 - TB))
                    if Q > 0 and kt < GT - 1:
                        finish(Q - 1, kt)
                        if kt == GT - 2:
                            finish(Q - 1, kt + 1)
                for j in range(GT):
                    finish(GB - 1, j)

        @block.tensor
        def _(pe):
            pe.sem_inc(s_eb, NE)
            pe.wait_ge(s_wm, 32)
            for ci in range(KC):
                for cd in range(KC):
                    pe.matmul(M_ps[ci][:, 0:D], wv_raw[:, cd, ci * P:(ci + 1) * P], woT_raw[:, cd, :],
                              start=(cd == 0), stop=(cd == KC - 1))
            pe.wait_ge(s_w, 64)
            for cd in range(KC):
                mm = pe.matmul(c_ps[0:1, 0:D], bv_col[:, cd:cd + 1], woT_raw[:, cd, :],
                               start=(cd == 0), stop=(cd == KC - 1))
            mm.then_inc(s_cps, 1)
            pe.wait_ge(s_const, 9)
            pe.wait_ge(s_M, 4)
            for b in range(NB):
                def group_transpose(g):
                    G = b * GB + g
                    pe.wait_ge(s_xn, GT * G + GT)
                    for c in range(KC):
                        pe.wait_ge(s_xtl, KC * G + c + 1)
                        for j in range(GT):
                            mm = pe.transpose(T_ps[g % 2][c][:, j * P:(j + 1) * P],
                                              XN[:, g % 2, j, c * P:(c + 1) * P], ident[:, :])
                        mm.then_inc(s_T, 1)

                group_transpose(0)
                for g in range(GB):
                    G = b * GB + g
                    if g + 1 < GB:
                        group_transpose(g + 1)
                    pe.wait_ge(s_xtl, KC * G + 3 * KC)
                    for j in range(GT):
                        pe.wait_ge(s_vol, GT * G + j + 1)
                        tok = slice(j * P, (j + 1) * P)
                        out = V_ps[j][:, 0:MW]
                        for c in range(KC):
                            hi, lo = XT_hi[:, g % 2, c, tok], XT_lo[:, g % 2, c, tok]
                            pe.matmul(out, hi, M_hi[:, c, :], start=(c == 0), stop=False)
                            pe.matmul(out, hi, M_lo[:, c, :], start=False, stop=False)
                            pe.matmul(out, lo, M_hi[:, c, :], start=False, stop=False)
                        pe.matmul(out, one_row[:, :], c_hi[:, :], start=False, stop=False)
                        pe.matmul(out, one_row[:, :], c_lo[:, :], start=False, stop=True).then_inc(s_vps[j % 2], 1)
                pe.wait_ge(s_f, N_POS * b + 1)
                pe.wait_ge(s_vol, GT * GB * b + GT * GB + GT)
                pe.transpose(turn_ps[0:1, 0:P], pmax[:, :], ident[:, :]).then_inc(s_pt, 1)
                pe.wait_ge(s_f, N_POS * b + 2)
                pe.matmul(spread_ps[:, 0:1], one_f[:, :], pmax_row[:, :], start=True, stop=True).then_inc(s_pt, 1)
                pe.wait_ge(s_f, N_POS * b + N_POS)
                for g in range(GB):
                    for k, F in enumerate((FQ, FKh, FKl)):
                        n = 3 * g + k
                        if n >= 4:
                            pe.wait_ge(s_fr, 3 * GB * b + n - 3)
                        pe.transpose(Q_ps[n % 4][:, 0:P], ident[:, :], ident[:, :])
                        for j in range(GT):
                            mm = pe.transpose(Q_ps[n % 4][0:2 * KR, j * P:(j + 1) * P], F[:, g * GT + j, :],
                                              ident[:, :])
                        mm.then_inc(s_ft, 1)
                pe.wait_ge(s_fr, 3 * GB * b + 3 * GB)
                for n, (Q, kt) in enumerate(sq_blocks):
                    _, q0, w = block_of(Q, kt)
                    pe.wait_ge(s_e2, b * NBLK + n + 1)
                    key = slice(kt * P, (kt + 1) * P)
                    pe.matmul(Q_ps[n % NQ][:, 0:w], KTh[:, key], QT[:, q0:q0 + w], start=True, stop=False)
                    pe.matmul(Q_ps[n % NQ][:, 0:w], KTl[:, key], QT[:, q0:q0 + w], start=False, stop=True)\
                      .then_inc(s_q, 1)
                for n, (Q, kt) in enumerate(blocks):
                    pe.wait_ge(s_el, b * NBLK + n + 1)
                    q0 = max(kt, GT * Q)
                    for qt in range(q0, GT * Q + GT):
                        j = qt - GT * Q
                        if kt == 0:
                            pe.wait_ge(s_x1, b * TB + GT * Q + j + 1)
                        cols = slice((qt - q0) * P, (qt - q0 + 1) * P)
                        pe.matmul(O_ps[Q % 2][j][:, 0:D + 2], E_hi[:, n % NE, cols], VO[:, kt, 0:D + 2],
                                  start=(kt == 0), stop=False)
                        pe.matmul(O_ps[Q % 2][j][:, 0:D], E_hi[:, n % NE, cols], VO[:, kt, D + 2:VW],
                                  start=False, stop=False)
                        mm = pe.matmul(O_ps[Q % 2][j][:, 0:D + 2], E_lo[:, n % NE, cols], VO[:, kt, 0:D + 2],
                                       start=False, stop=(kt == qt))
                        if kt == qt and j < GT - 1:
                            mm.then_inc(s_acc, 1)
                    mm.then_inc(s_eb, 1)

    with ExitStack() as ctx:
        def sb(name, shape, dt=f32):
            return ctx.enter_context(nc.sbuf_tensor(name, shape, dt))

        def sem(name):
            return ctx.enter_context(nc.semaphore(name))

        ident = sb("ident2", [P, P])
        eps_col = sb("eps_col2", [P, 1])
        mv = sb("mv2", [P, NT, 2])
        std = sb("std2", [P, NT])
        rstd = sb("rstd2", [P, NT])
        gate_raw = sb("gate_raw", [P, KC, NX])
        gate_hi = sb("gate_hi", [P, KC, NX], f32r)
        gate_lo = sb("gate_lo", [P, KC, NX], f32r)
        gbias = sb("gbias", [P, NX])
        logit = sb("logit", [P, NT, NX])
        score = sb("score", [P, NT, NX])
        pick = [sb(f"pick{k}", [P, NT, NX]) for k in range(TOPK)]
        tmp = sb("tmp", [P, NT, NX])
        chosen = sb("chosen", [P, NT, NX], bf16)
        red = sb("red", [P, NT])
        red2 = sb("red2", [P, NT])
        weight = [sb(f"weight{k}", [P, NT]) for k in range(TOPK)]
        slot = [sb(f"slot{k}", [P, NT], u32) for k in range(TOPK)]
        rank = sb("rank", [P, NX])
        before = sb("before", [P, P], bf16)
        ones_b = sb("ones_b", [P, P], bf16)
        one8 = sb("one8", [P, NX])
        n_i = sb("n_i", [P, NX], i32)
        n_j = sb("n_j", [P, NX], i32)
        n_f = sb("n_f", [P, NX])
        ends = sb("ends", [P, NX])
        base = sb("base", [P, NX])
        tile_id = sb("tile_id", [P, NSLOT])
        which = sb("which", [P, NSLOT])
        expert = sb("expert", [P, NSLOT], i32)

        def whole_and_low(name, shape):
            with nc.sbuf_tensor(name + "_raw", shape, f32) as raw:
                pass
            return raw, sb(name + "_lo", shape, f32r)

        sw13_hi = sb("sw13_hi", [P, KC, 2 * NS], f32r)
        sw13_raw, sw13_lo = whole_and_low("sw13", [P, KC, 2 * NS])
        sw2_hi = sb("sw2_hi", [P, MC, D], f32r)
        sw2_raw, sw2_lo = whole_and_low("sw2", [P, MC, D])
        W_hi = sb("W_hi", [P, KC, NX, 3 * D], f32r)
        W_raw, W_lo = whole_and_low("W", [P, KC, NX, 3 * D])
        with ExitStack() as first:
            def early(name, shape, dt=f32):
                return first.enter_context(nc.sbuf_tensor(name, shape, dt))
            biased = early("biased", [P, NT, NX])
            slot_e = early("slot_e", [P, NT, NX])
            total = early("total", [P, NX, NT])
            upto = early("upto", [P, NX, NT])
            keep = early("keep", [P, NX, NT])
            passed = early("passed", [P, NSLOT, NX])
        YG = sb("YG", [P, 4, TOPK, D])
        XR = YG[:, :, 0, :]
        with ExitStack() as first:
            XN = early("XN2", [P, 2, GT, D])
            sg = early("sg", [P, 2, GT * P])
            lgT = sg
            h_hi = early("h_hi", [P, 2, GT * P], f32r)
            with nc.sbuf_tensor("hf", [P, 2, GT * P], f32) as hf:
                pass
            h_lo = early("h_lo", [P, 2, GT * P], f32r)
            XT_hi = early("XT2_hi", [P, 2, KC, GT * P], f32r)
            XT_lo = early("XT2_lo", [P, 2, KC, GT * P], f32r)
        XS = sb("XS", [P, 4, D])
        YS = sb("YS", [P, 2, D])
        sr = sb("sr", [P, 2, D])
        hr = sb("hr", [P, 2, D])
        hT_hi = sb("hT_hi", [P, 2, KC, P], f32r)
        hT_lo = sb("hT_lo", [P, 2, KC, P], f32r)
        XST_hi = sb("XST_hi", [P, 2, KC, P], f32r)
        XST_lo = sb("XST_lo", [P, 2, KC, P], f32r)
        sb("rest", [P, 9, 512])

        bank = [ctx.enter_context(nc.psum_tensor(f"bank{i}", [P, 512], f32)) for i in range(8)]
        TL_ps, L_ps, LT_ps, C_ps = (bank[0:2], bank[2:4]), bank[4:6], bank[6:8], bank[6:8]
        T_ps, G_ps, U_ps, Z_ps = bank[0:2], bank[2:4], bank[4:6], bank[6:8]
        XT_ps, S_ps, HT_ps, Y_ps = bank[0:2], bank[2:4], bank[4:6], bank[6:8]

        s_const = sem("f_const")
        s_gate = sem("f_gate")
        s_w = sem("f_w")
        s_whi = sem("f_whi")
        s_wlo = sem("f_wlo")
        s_mv = sem("f_mv")
        s_std = sem("f_std")
        s_rstd = sem("f_rstd")
        s_xn = sem("f_xn")
        s_T = sem("f_T")
        s_xth = sem("f_xth")
        s_xtl = sem("f_xtl")
        s_lps = sem("f_lps")
        s_lc = sem("f_lc")
        s_lt = sem("f_lt")
        s_lg = sem("f_lg")
        s_g = sem("f_g")
        s_u = sem("f_u")
        s_sg = sem("f_sg")
        s_hf = sem("f_hf")
        s_hh = sem("f_hh")
        s_hl = sem("f_hl")
        s_hu = sem("f_hu")
        s_z = sem("f_z")
        s_zf = sem("f_zf")
        s_r = sem("f_r")
        s_ex = sem("f_ex")
        s_cnt = sem("f_cnt")
        s_slot = sem("f_slot")
        s_xr = sem("f_xr")
        s_sc = [sem(f"f_sc{i}") for i in range(4)]
        s_wr = sem("f_wr")
        s_wrh = sem("f_wrh")
        s_wrl = sem("f_wrl")
        s_xs = [sem(f"f_xs{i}") for i in range(4)]
        s_xsT = sem("f_xsT")
        s_xsh = sem("f_xsh")
        s_xsl = sem("f_xsl")
        s_s1 = sem("f_s1")
        s_sr = sem("f_sr")
        s_hr = sem("f_hr")
        s_hT = sem("f_hT")
        s_hTh = sem("f_hTh")
        s_hTl = sem("f_hTl")
        s_s2 = sem("f_s2")
        s_ys = sem("f_ys")
        s_yst = [sem(f"f_yst{i}") for i in range(2)]
        s_yg = [sem(f"f_yg{i}") for i in range(4)]
        s_y = sem("f_y")
        s_out = sem("f_out")

        N_XN, N_T, N_XTL = NT, KC * NG, KC * NG + 2 * KC
        HALF = NG // 2

        def tiles_to_scatter(n):
            return range(2 * n + 2, min(2 * n + 4, NT))

        def tiles_to_add(n):
            c = n - MC * HALF
            return range(max(2 * c - 4, 0), max(2 * c - 2, 0))

        block = ctx.enter_context(nc.Block())

        @block.sync
        def _(sp):
            sp.dma_start(gate_raw[:, :, :], gateT.rearrange("(c p) n -> p c n", p=P)).then_inc(s_gate, 16)
            sp.dma_start(gbias[:, :], gate_bias.rearrange("(a n) -> a n", a=1).to_broadcast([P, NX]))\
              .then_inc(s_gate, 16)
            sp.dma_start(sw13_raw[:, :, :], sw13T.rearrange("(c p) n -> p c n", p=P)).then_inc(s_w, 16)
            sp.dma_start(sw2_raw[:, :, :], sw2T.rearrange("(c p) n -> p c n", p=P)).then_inc(s_w, 16)
            for e in range(NX):
                sp.dma_start(W_raw[:, :, e, :], wT[e, :, :].rearrange("(c p) n -> p c n", p=P))\
                  .then_inc(s_wr, 16)
            sp.wait_ge(s_T, N_T + KC * HALF)
            for k in range(4):
                sp.wait_ge(s_sc[k], 16 * TOPK * NT // 4)
            for k in range(4):
                sp.dma_start(XS[:, k, :], xs_t[k, :, :]).then_inc(s_xs[k], 16)
            for i in range(-3, NSLOT):
                if i + 7 < NSLOT:
                    sp.wait_ge(s_xsT, i + 4)
                    sp.dma_start(XS[:, (i + 3) % 4, :], xs_t[i + 7, :, :]).then_inc(s_xs[(i + 3) % 4], 16)
                if i < 0:
                    continue
                sp.wait_ge(s_ys, i + 3)
                sp.dma_start(ys_t[i, :, :], YS[:, i % 2, :]).then_inc(s_yst[i % 2], 16)
            for t in range(NT):
                sp.wait_ge(s_y, TOPK * t + TOPK)
                sp.dma_start(out_v[:, t, :], X[:, t, :]).then_inc(s_out, 16)
            sp.wait_ge(s_out, 16 * NT)

        @block.gpsimd
        def _(pool):
            def const(ins):
                ins.then_inc(s_const, 1)
            const(pool.memset(ident[:, :], 0.0))
            const(pool.memset(before[:, :], 1.0))
            const(pool.memset(ones_b[:, :], 1.0))
            const(pool.memset(eps_col[:, :], EPS))
            const(pool.memset(one8[:, :], 1.0))
            const(pool.memset(keep[:, :, 1:NT], 1.0))
            const(pool.memset(keep[:, :, 0:1], 0.0))
            const(pool.iota(rank[:, :], pattern=[[-1, NX]], base=NX, channel_multiplier=0,
                            allow_small_or_imprecise_dtypes=True))
            const(pool.iota(tile_id[:, :], pattern=[[1, NSLOT]], base=0, channel_multiplier=0,
                            allow_small_or_imprecise_dtypes=True))
            pool.wait_ge(s_const, 9)
            const(pool.affine_select(out=ident[:, :], in_=ident[:, :], compare_op=ALU.not_equal, fill=1.0, base=0,
                                     pattern=[[-1, P]], channel_multiplier=1))
            const(pool.affine_select(out=before[:, :], in_=before[:, :], compare_op=ALU.is_gt, fill=0.0, base=0,
                                     pattern=[[1, P]], channel_multiplier=-1))
            pool.wait_ge(s_slot, 1)
            for t in range(NT):
                pool.wait_ge(s_xr, t + 1)
                for k in range(TOPK):
                    pool.indirect_dma_start(out=xs,
                                            out_offset=bass.IndirectOffsetOnAxis(ap=slot[k][:, t:t + 1], axis=0),
                                            in_=XR[:, t % 4, :], in_offset=None).then_inc(s_sc[t % 4], 16)
            for v in range(2):
                pool.wait_ge(s_yst[v], 16 * (NSLOT // 2) + 16)
            for t in range(NT):
                if t >= 4:
                    pool.wait_ge(s_y, TOPK * (t - 3))
                for k in range(TOPK):
                    pool.indirect_dma_start(out=YG[:, t % 4, k, :], out_offset=None, in_=ys,
                                            in_offset=bass.IndirectOffsetOnAxis(ap=slot[k][:, t:t + 1], axis=0))\
                        .then_inc(s_yg[t % 4], 16)

        @block.scalar
        def _(act):
            act.sem_inc(s_yst[0], 16)
            act.sem_inc(s_yst[1], 16)
            act.sem_inc(s_ys, 2)
            act.wait_ge(s_const, 11)
            act.wait_ge(s_mv, NT)
            act.activation(std[:, :], mv[:, :, 1], ACT.Sqrt, bias=eps_col[:, 0:1]).then_inc(s_std, 1)
            act.wait_ge(s_gate, 32)
            act.activation(gate_hi[:, :, :], gate_raw[:, :, :], ACT.Copy).then_inc(s_whi, 1)
            def logits_hi(G, v):
                for c in range(KC):
                    act.wait_ge(s_T, G * KC + c + 1)
                    act.activation(XT_hi[:, v, c, :], TL_ps[v][c][:, :], ACT.Copy).then_inc(s_xth, 1)

            def logits_copy(G, v):
                act.wait_ge(s_lps, G + 1)
                act.activation(lgT[0:NX, v, :], L_ps[v][0:NX, :], ACT.Copy).then_inc(s_lc, 1)

            logits_hi(0, 0)
            logits_hi(1, 1)
            logits_copy(0, 0)
            with act.Fori(0, NG // 2 - 1) as k:
                for v in range(2):
                    logits_hi(k * 2 + v + 2, v)
                    logits_copy(k * 2 + v + 1, 1 - v)
            logits_copy(NG - 1, 1)
            act.wait_ge(s_w, 32)
            act.activation(sw13_hi[:, :, :], sw13_raw[:, :, :], ACT.Copy).then_inc(s_whi, 1)
            act.activation(sw2_hi[:, :, :], sw2_raw[:, :, :], ACT.Copy).then_inc(s_whi, 1)

            def group_hi(G):
                for c in range(KC):
                    act.wait_ge(s_T, N_T + KC * G + c + 1)
                    act.activation(XT_hi[:, G % 2, c, :], T_ps[c][:, :], ACT.Copy).then_inc(s_xth, 1)

            def gate_silu(n):
                act.wait_ge(s_g, n + 1)
                if n >= 2:
                    act.wait_ge(s_hf, n - 1)
                act.activation(sg[:, n % 2, :], G_ps[n % 2][:, :], ACT.Silu).then_inc(s_sg, 1)

            def chunk_hi(n):
                act.wait_ge(s_hf, n + 1)
                if n >= 2:
                    act.wait_ge(s_hu, n - 1)
                act.activation(h_hi[:, n % 2, :], hf[:, n % 2, :], ACT.Copy).then_inc(s_hh, 1)

            def shared(groups):
                for G in groups:
                    for n in range(MC * G, MC * G + MC):
                        gate_silu(n)
                        chunk_hi(n)
                        if n % MC == 2 and G + 1 in groups:
                            group_hi(G + 1)
                        if n < KC * NX:
                            act.activation(W_hi[:, n % KC, n // KC, :], W_raw[:, n % KC, n // KC, :],
                                           ACT.Copy).then_inc(s_wrh, 1)

            group_hi(0)
            act.wait_ge(s_r, 2)
            act.activation(tmp[:, :, :], logit[:, :, :], ACT.Exp).then_inc(s_ex, 1)
            act.wait_ge(s_wr, 16 * NX)
            shared(range(HALF))

            def hidden_hi(i, v):
                act.wait_ge(s_hT, i + 1)
                act.activation(hT_hi[:, v, :, :], HT_ps[v][:, 0:D].rearrange("p (c n) -> p c n", c=KC), ACT.Copy)\
                   .then_inc(s_hTh, 1)

            def silu(i, v):
                act.wait_ge(s_s1, i + 1)
                act.activation(sr[:, v, :], S_ps[v][:, 0:D], ACT.Silu).then_inc(s_sr, 1)

            def tokens_hi(i, v):
                act.wait_ge(s_xsT, i + 1)
                act.activation(XST_hi[:, v, :, :], XT_ps[v][:, 0:D].rearrange("p (c n) -> p c n", c=KC), ACT.Copy)\
                   .then_inc(s_xsh, 1)

            def output(i, v, k):
                act.wait_ge(s_s2, i + 1)
                act.wait_ge(s_yst[v], 16 * k + 16)
                act.activation(YS[:, v, :], Y_ps[v][:, 0:D], ACT.Copy).then_inc(s_ys, 1)

            for i in range(-3, 0):
                tokens_hi(i + 3, (i + 3) % 2)
                if i + 2 >= 0:
                    silu(i + 2, i % 2)
                if i + 1 >= 0:
                    hidden_hi(i + 1, (i + 1) % 2)
            with act.Fori(0, N_FULL // 2) as k:
                for v in range(2):
                    tokens_hi(k * 2 + v + 3, 1 - v)
                    silu(k * 2 + v + 2, v)
                    hidden_hi(k * 2 + v + 1, 1 - v)
                    output(k * 2 + v, v, k)
            for i in range(N_FULL, NSLOT):
                if i + 3 < NSLOT:
                    tokens_hi(i + 3, (i + 3) % 2)
                if i + 2 < NSLOT:
                    silu(i + 2, i % 2)
                if i + 1 < NSLOT:
                    hidden_hi(i + 1, (i + 1) % 2)
                output(i, i % 2, i // 2)
            group_hi(HALF)
            for v in range(2):
                act.wait_ge(s_yst[v], 16 * (NSLOT // 2) + 16)
            shared(range(HALF, NG))

        @block.vector
        def _(dve):
            dve.sem_inc(s_xtl, 2 * KC)
            dve.sem_inc(s_lg, 2)
            dve.sem_inc(s_xsl, 2)
            dve.sem_inc(s_hTl, 2)
            dve.sem_inc(s_hr, 2)
            dve.wait_ge(s_const, 11)
            for t in range(NT):
                dve.bn_aggr(mv[:, t, :], st1[:, t, :]).then_inc(s_mv, 1)
            dve.wait_ge(s_std, 1)
            dve.reciprocal(rstd[:, :], std[:, :]).then_inc(s_rstd, 1)
            dve.wait_ge(s_rstd, 1)
            dve.wait_ge(s_mv, NT)

            def normalised(out, t):
                return dve.tensor_scalar(out, tile_of(X, t), flat(mv[:, bass.ds(t, 1), 0:1]), rstd[:, bass.ds(t, 1)],
                                         ALU.subtract, ALU.mult)

            def logits_xn(G, v):
                for j in range(GT):
                    normalised(XN[:, v, j, :], G * GT + j).then_inc(s_xn, 1)

            def logits_lo(G, v):
                for c in range(KC):
                    dve.wait_ge(s_xth, G * KC + c + 1)
                    dve.tensor_tensor(XT_lo[:, v, c, :], TL_ps[v][c][:, :], XT_hi[:, v, c, :].bitcast(f32),
                                      ALU.subtract).then_inc(s_xtl, 1)

            def logits_out(G, v):
                dve.wait_ge(s_lt, G + 1)
                dve.tensor_copy(logit[:, bass.ds(G * GT, GT), :],
                                LT_ps[v][:, 0:GT * NX].rearrange("p (t e) -> p t e", t=GT)).then_inc(s_lg, 1)

            logits_xn(0, 0)
            dve.wait_ge(s_whi, 1)
            dve.tensor_tensor(gate_lo[:, :, :], gate_raw[:, :, :], gate_hi[:, :, :].bitcast(f32), ALU.subtract)\
               .then_inc(s_wlo, 1)
            logits_xn(1, 1)
            logits_lo(0, 0)
            logits_xn(2, 0)
            logits_lo(1, 1)
            with dve.Fori(0, NG // 2 - 2) as k:
                for v in range(2):
                    logits_xn(k * 2 + v + 3, 1 - v)
                    logits_lo(k * 2 + v + 2, v)
                    logits_out(k * 2 + v, v)
            logits_xn(NG - 1, 1)
            logits_lo(NG - 2, 0)
            logits_out(NG - 4, 0)
            logits_lo(NG - 1, 1)
            logits_out(NG - 3, 1)

            def group_xn(G):
                for j in range(GT):
                    normalised(XN[:, G % 2, j, :], G * GT + j).then_inc(s_xn, 1)

            def group_lo(G):
                for c in range(KC):
                    dve.wait_ge(s_xth, KC * (NG + G) + c + 1)
                    dve.tensor_tensor(XT_lo[:, G % 2, c, :], T_ps[c][:, :], XT_hi[:, G % 2, c, :].bitcast(f32),
                                      ALU.subtract).then_inc(s_xtl, 1)

            group_xn(0)
            for G in (NG - 2, NG - 1):
                logits_out(G, G % 2)
            dve.wait_ge(s_whi, 3)
            for raw, hi, lo in ((sw13_raw, sw13_hi, sw13_lo), (sw2_raw, sw2_hi, sw2_lo)):
                dve.tensor_tensor(lo[:, :, :], raw[:, :, :], hi[:, :, :].bitcast(f32), ALU.subtract)\
                   .then_inc(s_wlo, 1)
            group_lo(0)

            step = [0]

            def done(ins):
                step[0] += 1
                ins.then_inc(s_r, 1)
                dve.wait_ge(s_r, step[0])

            def over_e(ap):
                return ap[:, :].unsqueeze(2).to_broadcast([P, NT, NX])

            def over_t(ap):
                return ap[:, :].unsqueeze(1).to_broadcast([P, NT, NX])

            dve.wait_ge(s_lg, NG + 2)
            done(dve.tensor_reduce(red[:, :], logit[:, :, :], AX.X, ALU.max))
            done(dve.tensor_tensor(logit[:, :, :], logit[:, :, :], over_e(red), ALU.subtract))
            dve.wait_ge(s_ex, 1)
            done(dve.tensor_reduce(red[:, :], tmp[:, :, :], AX.X, ALU.add))
            done(dve.reciprocal(red2[:, :], red[:, :]))
            done(dve.tensor_tensor(score[:, :, :], tmp[:, :, :], over_e(red2), ALU.mult))
            done(dve.tensor_tensor(biased[:, :, :], score[:, :, :], over_t(gbias), ALU.add))
            for k in range(TOPK):
                done(dve.tensor_reduce(red[:, :], biased[:, :, :], AX.X, ALU.max))
                done(dve.tensor_tensor(tmp[:, :, :], biased[:, :, :], over_e(red), ALU.is_equal))
                done(dve.tensor_tensor(tmp[:, :, :], tmp[:, :, :], over_t(rank), ALU.mult))
                done(dve.tensor_reduce(red2[:, :], tmp[:, :, :], AX.X, ALU.max))
                done(dve.tensor_tensor(pick[k][:, :, :], over_t(rank), over_e(red2), ALU.is_equal))
                if k + 1 < TOPK:
                    done(dve.scalar_tensor_tensor(out=biased[:, :, :], in0=pick[k][:, :, :], scalar=-3.0e38,
                                                  in1=biased[:, :, :], op0=ALU.mult, op1=ALU.add))
            done(dve.tensor_tensor(chosen[:, :, :], pick[0][:, :, :], pick[1][:, :, :], ALU.add))
            assert step[0] == N_CHOSEN
            dve.wait_ge(s_cnt, 1)
            done(dve.tensor_copy(total[:, :, :], C_ps[1][:, 0:NT * NX].rearrange("p (t e) -> p e t", t=NT)))
            flat3 = [ap[:, :, :].rearrange("p e t -> p (e t)") for ap in (keep, total, upto)]
            done(dve.tensor_tensor_scan(out=flat3[2], data0=flat3[0], data1=flat3[1], initial=0.0,
                                        op0=ALU.mult, op1=ALU.add))
            done(dve.tensor_scalar(n_i[:, :], upto[:, :, NT - 1], float(P - 1), None, ALU.add))
            done(dve.tensor_scalar(n_j[:, :], n_i[:, :], P.bit_length() - 1, None, ALU.logical_shift_right))
            done(dve.tensor_copy(n_f[:, :], n_j[:, :]))
            done(dve.tensor_tensor_scan(out=ends[:, :], data0=one8[:, :], data1=n_f[:, :], initial=0.0,
                                        op0=ALU.mult, op1=ALU.add))
            done(dve.tensor_tensor(base[:, :], ends[:, :], n_f[:, :], ALU.subtract))
            done(dve.tensor_scalar(base[:, :], base[:, :], float(P), None, ALU.mult))
            done(dve.tensor_tensor(upto[:, :, :], upto[:, :, :], total[:, :, :], ALU.subtract))
            done(dve.tensor_tensor(upto[:, :, :], upto[:, :, :],
                                   base[:, :].unsqueeze(2).to_broadcast([P, NX, NT]), ALU.add))
            done(dve.tensor_tensor(slot_e[:, :, :], C_ps[0][:, 0:NT * NX].rearrange("p (t e) -> p t e", t=NT),
                                   upto[:, :, :].rearrange("p e t -> p t e"), ALU.add))
            for k in range(TOPK):
                done(dve.tensor_tensor(tmp[:, :, :], pick[k][:, :, :], slot_e[:, :, :], ALU.mult))
                done(dve.tensor_reduce(red[:, :], tmp[:, :, :], AX.X, ALU.add))
                done(dve.tensor_copy(slot[k][:, :], red[:, :]))
            dve.sem_inc(s_slot, 1)

            def slot_experts():
                done(dve.tensor_tensor(passed[:, :, :], tile_id[:, :].unsqueeze(2).to_broadcast([P, NSLOT, NX]),
                                       ends[:, :].unsqueeze(1).to_broadcast([P, NSLOT, NX]), ALU.is_ge))
                done(dve.tensor_reduce(which[:, :], passed[:, :, :], AX.X, ALU.add))
                done(dve.tensor_scalar(expert[:, :], which[:, :], float(NX - 1), None, ALU.min))
                dve.sem_inc(s_slot, 1)

            def choice_weights():
                for k in range(TOPK):
                    done(dve.tensor_tensor(tmp[:, :, :], pick[k][:, :, :], score[:, :, :], ALU.mult))
                    done(dve.tensor_reduce(weight[k][:, :], tmp[:, :, :], AX.X, ALU.add))

            def scatter_tile(t):
                if t >= 4:
                    dve.wait_ge(s_sc[t % 4], 16 * TOPK * (t // 4))
                normalised(XR[:, t % 4, :], t).then_inc(s_xr, 1)

            def add_routed(t):
                dve.wait_ge(s_yg[t % 4], 16 * TOPK * (t // 4 + 1))
                dve.wait_ge(s_zf, 2 * (t // GT) + 2)
                for k in range(TOPK):
                    if k:
                        dve.wait_ge(s_y, TOPK * t + k)
                    dve.scalar_tensor_tensor(out=X[:, t, :], in0=YG[:, t % 4, k, :], scalar=weight[k][:, t:t + 1],
                                             in1=X[:, t, :], op0=ALU.mult, op1=ALU.add).then_inc(s_y, 1)

            def add_shared(G, z):
                if z == 0:
                    dve.wait_ge(s_z, G + 1)
                else:
                    dve.wait_ge(s_hu, MC * G + MC)
                xz = X[:, G * GT + 2 * z:G * GT + 2 * z + 2, :].rearrange("p t n -> p (t n)")
                dve.tensor_tensor(xz, xz, Z_ps[z][:, :], ALU.add).then_inc(s_zf, 1)

            def shared(groups):
                for G in groups:
                    for n in range(MC * G, MC * G + MC):
                        dve.wait_ge(s_sg, n + 1)
                        dve.wait_ge(s_u, n + 1)
                        if n >= 2:
                            dve.wait_ge(s_hu, n - 1)
                        dve.tensor_tensor(hf[:, n % 2, :], U_ps[n % 2][:, :], sg[:, n % 2, :],
                                          ALU.mult).then_inc(s_hf, 1)
                        if n == 0:
                            slot_experts()
                        if n == 2:
                            choice_weights()
                        if G < HALF:
                            for t in tiles_to_scatter(n):
                                scatter_tile(t)
                        else:
                            for t in tiles_to_add(n):
                                add_routed(t)
                        dve.wait_ge(s_hh, n + 1)
                        dve.tensor_tensor(h_lo[:, n % 2, :], hf[:, n % 2, :],
                                          h_hi[:, n % 2, :].bitcast(f32), ALU.subtract).then_inc(s_hl, 1)
                        if n < KC * NX:
                            dve.wait_ge(s_wrh, n + 1)
                            dve.tensor_tensor(W_lo[:, n % KC, n // KC, :], W_raw[:, n % KC, n // KC, :],
                                              W_hi[:, n % KC, n // KC, :].bitcast(f32), ALU.subtract)\
                               .then_inc(s_wrl, 1)
                        if n % MC == 0 and G - 1 in groups:
                            add_shared(G - 1, 0)
                            add_shared(G - 1, 1)
                        if n % MC == 1 and G + 1 in groups:
                            group_xn(G + 1)
                        if n % MC == 2 and G + 1 in groups:
                            group_lo(G + 1)
                add_shared(groups[-1], 0)
                add_shared(groups[-1], 1)

            scatter_tile(0)
            scatter_tile(1)
            shared(range(HALF))

            def hidden_lo(i, v):
                dve.wait_ge(s_hTh, i + 1)
                dve.tensor_tensor(hT_lo[:, v, :, :], HT_ps[v][:, 0:D].rearrange("p (c n) -> p c n", c=KC),
                                  hT_hi[:, v, :, :].bitcast(f32), ALU.subtract).then_inc(s_hTl, 1)

            def hidden(i, v):
                dve.wait_ge(s_sr, i + 1)
                dve.tensor_tensor(hr[:, v, :], S_ps[v][:, D:2 * D], sr[:, v, :], ALU.mult).then_inc(s_hr, 1)

            def tokens_lo(i, v):
                dve.wait_ge(s_xsh, i + 1)
                dve.tensor_tensor(XST_lo[:, v, :, :], XT_ps[v][:, 0:D].rearrange("p (c n) -> p c n", c=KC),
                                  XST_hi[:, v, :, :].bitcast(f32), ALU.subtract).then_inc(s_xsl, 1)

            for i in range(-3, 0):
                tokens_lo(i + 3, (i + 3) % 2)
                if i + 2 >= 0:
                    hidden(i + 2, i % 2)
                if i + 1 >= 0:
                    hidden_lo(i + 1, (i + 1) % 2)
            with dve.Fori(0, N_FULL // 2) as k:
                for v in range(2):
                    tokens_lo(k * 2 + v + 3, 1 - v)
                    hidden(k * 2 + v + 2, v)
                    hidden_lo(k * 2 + v + 1, 1 - v)
            for i in range(N_FULL, NSLOT):
                if i + 3 < NSLOT:
                    tokens_lo(i + 3, (i + 3) % 2)
                if i + 2 < NSLOT:
                    hidden(i + 2, i % 2)
                if i + 1 < NSLOT:
                    hidden_lo(i + 1, (i + 1) % 2)
            dve.wait_ge(s_xsT, NSLOT)
            group_xn(HALF)
            group_lo(HALF)
            for v in range(2):
                dve.wait_ge(s_yst[v], 16 * (NSLOT // 2) + 16)
            shared(range(HALF, NG))
            for t in range(NT - 4, NT):
                add_routed(t)

        @block.tensor
        def _(pe):
            pe.wait_ge(s_const, 11)

            def three(out, a_hi, a_lo, b_hi, b_lo, start, stop, **kw):
                pe.matmul(out, a_hi, b_hi, start=start, stop=False, **kw)
                pe.matmul(out, a_hi, b_lo, start=False, stop=False, **kw)
                return pe.matmul(out, a_lo, b_hi, start=False, stop=stop, **kw)

            def logits_transpose(G, v):
                pe.wait_ge(s_xn, G * GT + GT)
                for c in range(KC):
                    pe.wait_ge(s_xtl, G * KC + c + 1)
                    for j in range(GT):
                        mm = pe.transpose(TL_ps[v][c][:, j * P:(j + 1) * P], XN[:, v, j, c * P:(c + 1) * P],
                                          ident[:, :])
                    mm.then_inc(s_T, 1)

            def logits(G, v):
                pe.wait_ge(s_xtl, G * KC + 3 * KC)
                if not (isinstance(G, int) and G == 0):
                    pe.wait_ge(s_lc, G)
                    pe.wait_ge(s_lg, G)
                for c in range(KC):
                    mm = three(L_ps[v][0:NX, :], gate_hi[:, c, :], gate_lo[:, c, :], XT_hi[:, v, c, :],
                               XT_lo[:, v, c, :], c == 0, c == KC - 1)
                mm.then_inc(s_lps, 1)

            def turn_logits(v):
                for j in range(GT):
                    mm = pe.transpose(LT_ps[v][:, j * NX:(j + 1) * NX], lgT[0:NX, v, j * P:(j + 1) * P],
                                      ident[0:NX, 0:NX])
                mm.then_inc(s_lt, 1)

            logits_transpose(0, 0)
            pe.wait_ge(s_wlo, 1)
            logits_transpose(1, 1)
            logits(0, 0)
            with pe.Fori(0, NG // 2 - 1) as k:
                for v in range(2):
                    logits_transpose(k * 2 + v + 2, v)
                    logits(k * 2 + v + 1, 1 - v)
                    turn_logits(v)
            logits(NG - 1, 1)
            turn_logits(0)
            pe.wait_ge(s_lc, NG)
            pe.wait_ge(s_lg, NG)
            turn_logits(1)

            def group_transpose(G):
                pe.wait_ge(s_xn, N_XN + GT * G + GT)
                for c in range(KC):
                    pe.wait_ge(s_xtl, N_XTL + KC * (G - 1) + c + 1)
                    for j in range(GT):
                        mm = pe.transpose(T_ps[c][:, j * P:(j + 1) * P], XN[:, G % 2, j, c * P:(c + 1) * P],
                                          ident[:, :])
                    mm.then_inc(s_T, 1)

            def products(n):
                G, m = n // MC, n % MC
                pe.wait_ge(s_xtl, N_XTL + KC * G + KC)
                if n >= 2:
                    pe.wait_ge(s_hf, n - 1)
                for w, bk, s_ready in ((0, G_ps, s_g), (NS, U_ps, s_u)):
                    rows = slice(w + m * P, w + (m + 1) * P)
                    for c in range(KC):
                        mm = three(bk[n % 2][:, :], sw13_hi[:, c, rows], sw13_lo[:, c, rows],
                                   XT_hi[:, G % 2, c, :], XT_lo[:, G % 2, c, :], c == 0, c == KC - 1)
                    mm.then_inc(s_ready, 1)

            def outputs(n):
                G, m = n // MC, n % MC
                pe.wait_ge(s_hl, n + 1)
                for j in range(GT):
                    if m == 0 and j % 2 == 0 and G > 0:
                        pe.wait_ge(s_zf, 2 * (G - 1) + j // 2 + 1)
                    tok = slice(j * P, (j + 1) * P)
                    mm = three(Z_ps[j // 2][:, (j % 2) * D:(j % 2 + 1) * D], h_hi[:, n % 2, tok],
                               h_lo[:, n % 2, tok], sw2_hi[:, m, :], sw2_lo[:, m, :],
                               m == 0 and j % 2 == 0, m == MC - 1, skip_group_check=True)
                    if m == MC - 1 and j == 1:
                        mm.then_inc(s_z, 1)
                mm.then_inc(s_hu, 1)

            def shared(groups, ahead):
                for G in groups:
                    for n in range(MC * G, MC * G + MC):
                        if n not in ahead:
                            products(n)
                        if n > MC * groups[0]:
                            outputs(n - 1)
                        if n % MC == 2 and G + 1 in groups:
                            group_transpose(G + 1)
                outputs(MC * groups[-1] + MC - 1)

            group_transpose(0)
            pe.wait_ge(s_wlo, 3)
            products(0)
            products(1)
            pe.wait_ge(s_r, N_CHOSEN)
            rhs = chosen[:, :, :].rearrange("p t e -> p (t e)")
            pe.matmul(C_ps[0][:, 0:NT * NX], before[:, :], rhs, start=True, stop=True)
            pe.matmul(C_ps[1][:, 0:NT * NX], ones_b[:, :], rhs, start=True, stop=True).then_inc(s_cnt, 1)
            shared(range(HALF), (0, 1))
            pe.wait_ge(s_slot, 2)
            pe.wait_ge(s_wrl, KC * NX)
            pe.wait_ge(s_zf, 2 * HALF)

            expert_reg = [pe.alloc_register(f"expert{q}") for q in range(4)]

            def load_expert(i, q):
                pe.reg_load(expert_reg[q], expert[0:1, bass.ds(i, 1)])

            def weights(e, lo, hi):
                return [[w[:, c, bass.ds(e, 1), lo:hi].rearrange("p a n -> p (a n)") for w in (W_hi, W_lo)]
                        for c in range(KC)]

            def transpose_tokens(i, v, slot4, k4):
                pe.wait_ge(s_xs[slot4], 16 * k4 + 16)
                pe.wait_ge(s_xsl, i + 1)
                for c in range(KC):
                    mm = pe.transpose(XT_ps[v][:, c * P:(c + 1) * P], XS[:, slot4, c * P:(c + 1) * P], ident[:, :])
                mm.then_inc(s_xsT, 1)

            def gate_up(i, v, q):
                w = weights(pe.snap(expert_reg[q], min_val=0, max_val=NX - 1), 0, 2 * D)
                pe.wait_ge(s_xsl, i + 3)
                pe.wait_ge(s_hr, i + 1)
                for c in range(KC):
                    mm = three(S_ps[v][:, :], XST_hi[:, v, c, :], XST_lo[:, v, c, :], w[c][0], w[c][1],
                               c == 0, c == KC - 1)
                mm.then_inc(s_s1, 1)

            def transpose_hidden(i, v):
                pe.wait_ge(s_hr, i + 3)
                pe.wait_ge(s_hTl, i + 1)
                for c in range(KC):
                    mm = pe.transpose(HT_ps[v][:, c * P:(c + 1) * P], hr[:, v, c * P:(c + 1) * P], ident[:, :])
                mm.then_inc(s_hT, 1)

            def down(i, v, q):
                w = weights(pe.snap(expert_reg[q], min_val=0, max_val=NX - 1), 2 * D, 3 * D)
                pe.wait_ge(s_hTl, i + 3)
                pe.wait_ge(s_ys, i + 1)
                for c in range(KC):
                    mm = three(Y_ps[v][:, 0:D], hT_hi[:, v, c, :], hT_lo[:, v, c, :], w[c][0], w[c][1],
                               c == 0, c == KC - 1)
                mm.then_inc(s_s2, 1)

            for i in range(-3, 0):
                load_expert(i + 3, i + 3)
                transpose_tokens(i + 3, (i + 3) % 2, i + 3, 0)
                if i + 2 >= 0:
                    gate_up(i + 2, i % 2, i + 2)
                if i + 1 >= 0:
                    transpose_hidden(i + 1, (i + 1) % 2)
            with pe.Fori(0, N_FULL // 4) as k:
                for q in range(4):
                    i, v = k * 4 + q, q % 2
                    load_expert(i + 3, (q + 3) % 4)
                    transpose_tokens(i + 3, 1 - v, (q + 3) % 4, k + (q + 3) // 4)
                    gate_up(i + 2, v, (q + 2) % 4)
                    transpose_hidden(i + 1, 1 - v)
                    down(i, v, q)
            for i in range(N_FULL, NSLOT):
                v = i % 2
                if i + 3 < NSLOT:
                    load_expert(i + 3, (i + 3) % 4)
                    transpose_tokens(i + 3, 1 - v, (i + 3) % 4, (i + 3) // 4)
                if i + 2 < NSLOT:
                    gate_up(i + 2, v, (i + 2) % 4)
                if i + 1 < NSLOT:
                    transpose_hidden(i + 1, 1 - v)
                down(i, v, i % 4)
            group_transpose(HALF)
            pe.wait_ge(s_ys, NSLOT + 2)
            shared(range(HALF, NG), ())

    outer.close()


def kernel(**inputs):
    import numpy as _np
    import concourse.bacc as _bacc
    from concourse import mybir as _mybir
    from concourse.bass_utils import run_bass_kernel_spmd as _run

    a = {name: _np.asarray(v) for name, v in inputs.items()}
    laid = {
        "x": a["L0_attn_x"], "wv": a["L0_attn_wv"], "bv": a["L0_attn_bv"], "woT": a["L0_attn_wo"].T,
        "bo": a["L0_attn_bo"], "w3dT": a["L0_attn_w3d"].T, "b3d": a["L0_attn_b3d"],
        "gateT": a["L0_ffn_gate_w"].T, "gate_bias": a["L0_ffn_gate_bias"],
        "wT": _np.concatenate([a[f"L0_ffn_{w}"].transpose(0, 2, 1) for w in ("w1", "w3", "w2")], axis=2),
        "sw13T": _np.concatenate([a["L0_ffn_sw1"].T, a["L0_ffn_sw3"].T], axis=1),
        "sw2T": a["L0_ffn_sw2"].T,
    }
    nc = _bacc.Bacc("TRN2", target_bir_lowering=False, num_devices=1)
    arrays, args = {}, []
    for name, v in laid.items():
        arrays[f"in_{name}_dram"] = v = _np.ascontiguousarray(v)
        args.append(nc.dram_tensor(f"in_{name}_dram", v.shape, _mybir.dt.from_np(v.dtype), kind="ExternalInput").ap())
    args.append(nc.dram_tensor("out_0_dram", (NB, S, D), f32, kind="ExternalOutput").ap())
    attention_and_experts(nc, *args)
    r = _run(nc, [arrays], core_ids=[0])
    return r.results[0]["out_0_dram"]
```
